# Optimizing a Trainium2 kernel written in Bass

```python
import numpy as np
import jax
import jax.numpy as jnp

def _softmax(x, axis=-1):
    return jax.nn.softmax(x, axis=axis)

def _gelu(x):
    return jax.nn.gelu(x, approximate=True)

def _silu(x):
    return jax.nn.silu(x)

def _sigmoid(x):
    return jax.nn.sigmoid(x)

def _layernorm(x, axis=-1, eps=1e-05):
    m = jnp.mean(x, axis=axis, keepdims=True)
    v = jnp.var(x, axis=axis, keepdims=True)
    return (x - m) / jnp.sqrt(v + eps)

def _scatter_add(tgt, idx, src, axis=0):
    return tgt.at[idx].add(src)

def _segment_sum(src, seg, n):
    return jax.ops.segment_sum(src, seg, n)
kernel_name = 'mk_perceiver_d1_seqx_r2_93db66'

def setup_inputs(seed: int=0):
    np.random.seed(seed)
    _w = jnp.asarray

    def _rec_inputs():
        import jax
        import jax.numpy as jnp
        _rk = jax.random.key(seed)
        x = -0.0003929 + 0.9999 * jax.random.normal(jax.random.fold_in(_rk, 1), (2, 512, 512), jnp.float32)
        _lenS = 512 - jax.random.randint(jax.random.fold_in(_rk, 7), (2,), 0, max(1, 512 // 4) + 1, jnp.int32)
        _lenS2 = 8192 - jax.random.randint(jax.random.fold_in(_rk, 8), (2,), 0, max(1, 8192 // 4) + 1, jnp.int32)
        _ctx_1024P = jax.random.normal(jax.random.fold_in(_rk, 11), (2, 16, 512), jnp.float32)
        _ctx_1024c = jax.random.dirichlet(jax.random.fold_in(_rk, 511), 0.3 * jnp.ones((16,), jnp.float32), (2, 8192))
        _ctx_1024t = jnp.einsum('bsk,bkd->bsd', _ctx_1024c, _ctx_1024P)
        _ctx_1024t = _ctx_1024t * jax.lax.rsqrt(jnp.mean(jnp.square(_ctx_1024t)) + 1e-12) * 0.953939
        ctx_1024 = 2.81802e-05 + 1.00001 * (_ctx_1024t + 0.3 * jax.random.normal(jax.random.fold_in(_rk, 611), (2, 8192, 512), jnp.float32))
        return (x, ctx_1024)
    x, ctx_1024 = _rec_inputs()

    def _L0_xattn_setup():
        import jax, jax.numpy as jnp
        import numpy as np
        key = jax.random.key(seed)
        k1, k2, k3, k4 = jax.random.split(key, 4)
        B, L1, L2, D = (32, 256, 256, 512)
        ix = jax.random.normal(k1, (B, L1, D), dtype=jnp.float32)
        iother = jax.random.normal(k2, (B, L2, D), dtype=jnp.float32)
        scale = 1.0 / np.sqrt(D)
        W = jax.random.uniform(k3, (D, D), dtype=jnp.float32, minval=-scale, maxval=scale)
        b = jax.random.uniform(k4, (D,), dtype=jnp.float32, minval=-scale, maxval=scale)
        return {'ix': ix, 'iother': iother, 'W': W, 'b': b}
    _L0_xattn_all = _L0_xattn_setup()
    _L0_xattn_in = {k: v for k, v in _L0_xattn_all.items() if k in ('W', 'b')}
    del _L0_xattn_all

    def _L0_attn_setup():
        import jax, jax.numpy as jnp
        import numpy as np
        D_MODEL = 512
        NUM_HEADS = 16
        HEAD_DIM = D_MODEL // NUM_HEADS
        ROT_DIM = 32
        THETA = 10000.0
        XPOS_SCALE_BASE = 512.0
        GN_EPS = 1e-05

        def _rotate_half(x):
            x1 = x[..., 0::2]
            x2 = x[..., 1::2]
            return jnp.stack([-x2, x1], axis=-1).reshape(x.shape)

        def _rotary_xpos(q, k):
            S = q.shape[-2]
            inv_freq = 1.0 / THETA ** (jnp.arange(0, ROT_DIM, 2, dtype=jnp.float32) / ROT_DIM)
            t = jnp.arange(S, dtype=jnp.float32)
            freqs = jnp.repeat(t[:, None] * inv_freq[None, :], 2, axis=-1)
            base = (jnp.arange(0, ROT_DIM, 2, dtype=jnp.float32) + 0.4 * ROT_DIM) / (1.4 * ROT_DIM)
            power = (t - S // 2) / XPOS_SCALE_BASE
            scale = jnp.repeat(base[None, :] ** power[:, None], 2, axis=-1)
            cos, sin = (jnp.cos(freqs), jnp.sin(freqs))

            def apply(x, s):
                xm, xr = (x[..., :ROT_DIM], x[..., ROT_DIM:])
                xm = xm * (cos * s) + _rotate_half(xm) * (sin * s)
                return jnp.concatenate([xm, xr], axis=-1)
            return (apply(q, scale), apply(k, 1.0 / scale))

        def _decay_mask(S):
            h = jnp.arange(NUM_HEADS, dtype=jnp.float32)
            gamma = 1.0 - 2.0 ** (-5.0 - h)
            idx = jnp.arange(S)
            pw = (idx[:, None] - idx[None, :]).astype(jnp.float32)
            mask = jnp.where(pw >= 0, gamma[:, None, None] ** pw, 0.0)
            return mask / jnp.sqrt(jnp.sum(mask, axis=-1, keepdims=True))

        def _heads(x):
            B, S, _ = x.shape
            return x.reshape(B, S, NUM_HEADS, HEAD_DIM).transpose(0, 2, 1, 3)
        key = jax.random.key(seed)
        ks = jax.random.split(key, 12)
        d = D_MODEL
        s = 0.02
        return {'x': jax.random.normal(ks[0], (2, 1024, d), dtype=jnp.float32), 'Wq': jax.random.normal(ks[1], (d, d), dtype=jnp.float32) * s, 'bq': jnp.zeros((d,), jnp.float32), 'Wk': jax.random.normal(ks[2], (d, d), dtype=jnp.float32) * s, 'bk': jnp.zeros((d,), jnp.float32), 'Wv': jax.random.normal(ks[3], (d, d), dtype=jnp.float32) * s, 'bv': jnp.zeros((d,), jnp.float32), 'Wg': jax.random.normal(ks[4], (d, d), dtype=jnp.float32) * s, 'bg': jnp.zeros((d,), jnp.float32), 'Wo': jax.random.normal(ks[5], (d, d), dtype=jnp.float32) * s, 'bo': jnp.zeros((d,), jnp.float32), 'gn_w': jnp.ones((NUM_HEADS,), jnp.float32), 'gn_b': jnp.zeros((NUM_HEADS,), jnp.float32)}
    _L0_attn_all = _L0_attn_setup()
    _L0_attn_in = {k: v for k, v in _L0_attn_all.items() if k in ('Wq', 'bq', 'Wk', 'bk', 'Wv', 'bv', 'Wg', 'bg', 'Wo', 'bo', 'gn_w', 'gn_b')}
    del _L0_attn_all

    def _L0_ffn_setup():
        import jax, jax.numpy as jnp
        import numpy as np
        E = 8
        K = 2
        D = 512
        H = 2048
        CAP_FACTOR = 1.0
        key = jax.random.key(seed)
        ks = jax.random.split(key, 5)
        x = jax.random.normal(ks[0], (4, 1024, D), jnp.float32)
        gate_w = jax.random.normal(ks[1], (E, D), jnp.float32) * 0.02
        fc1_w = jax.random.normal(ks[2], (E, H, D), jnp.float32) * 0.02
        fc1_b = jnp.zeros((E, 1, H), jnp.float32)
        fc2_w = jax.random.normal(ks[3], (E, H, D), jnp.float32) * 0.02
        fc2_b = jnp.zeros((E, 1, D), jnp.float32)
        return {'x': x, 'gate_w': gate_w, 'fc1_w': fc1_w, 'fc1_b': fc1_b, 'fc2_w': fc2_w, 'fc2_b': fc2_b}
    _L0_ffn_all = _L0_ffn_setup()
    _L0_ffn_in = {k: v for k, v in _L0_ffn_all.items() if k in ('gate_w', 'fc1_w', 'fc1_b', 'fc2_w', 'fc2_b')}
    del _L0_ffn_all
    return {'x': x, 'ctx_1024': ctx_1024, 'L0_xattn_W': _L0_xattn_in['W'], 'L0_xattn_b': _L0_xattn_in['b'], 'L0_attn_Wq': _L0_attn_in['Wq'], 'L0_attn_bq': _L0_attn_in['bq'], 'L0_attn_Wk': _L0_attn_in['Wk'], 'L0_attn_bk': _L0_attn_in['bk'], 'L0_attn_Wv': _L0_attn_in['Wv'], 'L0_attn_bv': _L0_attn_in['bv'], 'L0_attn_Wg': _L0_attn_in['Wg'], 'L0_attn_bg': _L0_attn_in['bg'], 'L0_attn_Wo': _L0_attn_in['Wo'], 'L0_attn_bo': _L0_attn_in['bo'], 'L0_attn_gn_w': _L0_attn_in['gn_w'], 'L0_attn_gn_b': _L0_attn_in['gn_b'], 'L0_ffn_gate_w': _L0_ffn_in['gate_w'], 'L0_ffn_fc1_w': _L0_ffn_in['fc1_w'], 'L0_ffn_fc1_b': _L0_ffn_in['fc1_b'], 'L0_ffn_fc2_w': _L0_ffn_in['fc2_w'], 'L0_ffn_fc2_b': _L0_ffn_in['fc2_b']}

def reference(x, ctx_1024, L0_xattn_W, L0_xattn_b, L0_attn_Wq, L0_attn_bq, L0_attn_Wk, L0_attn_bk, L0_attn_Wv, L0_attn_bv, L0_attn_Wg, L0_attn_bg, L0_attn_Wo, L0_attn_bo, L0_attn_gn_w, L0_attn_gn_b, L0_ffn_gate_w, L0_ffn_fc1_w, L0_ffn_fc1_b, L0_ffn_fc2_w, L0_ffn_fc2_b):
    import jax
    import jax.numpy as jnp

    def _L0_xattn_ref(ix, iother, W, b):
        import jax, jax.numpy as jnp
        import numpy as np
        ex = jnp.einsum('bld,ed->ble', ix, W) + b
        eother = jnp.einsum('bld,ed->ble', iother, W) + b
        scores = jnp.einsum('bld,bmd->blm', ex, eother)
        attn = jax.nn.softmax(scores, axis=-1)
        aligned = jnp.einsum('blm,bmd->bld', attn, iother)
        return aligned

    def _L0_attn_ref(x, Wq, bq, Wk, bk, Wv, bv, Wg, bg, Wo, bo, gn_w, gn_b):
        import jax, jax.numpy as jnp
        import numpy as np
        D_MODEL = 512
        NUM_HEADS = 16
        HEAD_DIM = D_MODEL // NUM_HEADS
        ROT_DIM = 32
        THETA = 10000.0
        XPOS_SCALE_BASE = 512.0
        GN_EPS = 1e-05

        def _rotate_half(x):
            x1 = x[..., 0::2]
            x2 = x[..., 1::2]
            return jnp.stack([-x2, x1], axis=-1).reshape(x.shape)

        def _rotary_xpos(q, k):
            S = q.shape[-2]
            inv_freq = 1.0 / THETA ** (jnp.arange(0, ROT_DIM, 2, dtype=jnp.float32) / ROT_DIM)
            t = jnp.arange(S, dtype=jnp.float32)
            freqs = jnp.repeat(t[:, None] * inv_freq[None, :], 2, axis=-1)
            base = (jnp.arange(0, ROT_DIM, 2, dtype=jnp.float32) + 0.4 * ROT_DIM) / (1.4 * ROT_DIM)
            power = (t - S // 2) / XPOS_SCALE_BASE
            scale = jnp.repeat(base[None, :] ** power[:, None], 2, axis=-1)
            cos, sin = (jnp.cos(freqs), jnp.sin(freqs))

            def apply(x, s):
                xm, xr = (x[..., :ROT_DIM], x[..., ROT_DIM:])
                xm = xm * (cos * s) + _rotate_half(xm) * (sin * s)
                return jnp.concatenate([xm, xr], axis=-1)
            return (apply(q, scale), apply(k, 1.0 / scale))

        def _decay_mask(S):
            h = jnp.arange(NUM_HEADS, dtype=jnp.float32)
            gamma = 1.0 - 2.0 ** (-5.0 - h)
            idx = jnp.arange(S)
            pw = (idx[:, None] - idx[None, :]).astype(jnp.float32)
            mask = jnp.where(pw >= 0, gamma[:, None, None] ** pw, 0.0)
            return mask / jnp.sqrt(jnp.sum(mask, axis=-1, keepdims=True))

        def _heads(x):
            B, S, _ = x.shape
            return x.reshape(B, S, NUM_HEADS, HEAD_DIM).transpose(0, 2, 1, 3)
        B, S, d = x.shape
        q = _heads(x @ Wq + bq)
        k = _heads(x @ Wk + bk)
        v = _heads(x @ Wv + bv)
        q, k = _rotary_xpos(q, k)
        mask = _decay_mask(S)
        scores = jnp.einsum('bhqd,bhkd->bhqk', q, k) * mask[None]
        ret = jnp.einsum('bhqk,bhkd->bhqd', scores, v)
        mean = jnp.mean(ret, axis=(2, 3), keepdims=True)
        var = jnp.var(ret, axis=(2, 3), keepdims=True)
        ret = (ret - mean) / jnp.sqrt(var + GN_EPS)
        ret = ret * gn_w[None, :, None, None] + gn_b[None, :, None, None]
        concat = ret.transpose(0, 2, 1, 3).reshape(B, S, d)
        gate = jax.nn.silu(x @ Wg + bg)
        return gate * concat @ Wo + bo

    def _L0_ffn_ref(x, gate_w, fc1_w, fc1_b, fc2_w, fc2_b):
        import jax, jax.numpy as jnp
        import numpy as np
        E = 8
        K = 2
        D = 512
        H = 2048
        CAP_FACTOR = 1.0
        B, S, Dm = x.shape
        xf = x.reshape(-1, Dm)
        N = xf.shape[0]
        cap = int(K * CAP_FACTOR * ((N + E - 1) // E))
        logits = xf @ gate_w.T
        scores = jax.nn.softmax(logits, axis=-1)
        topv, topi = jax.lax.top_k(scores, K)
        gates = topv / jnp.sum(topv, axis=-1, keepdims=True)
        offset = jnp.zeros((E,), jnp.int32)
        locs = []
        for j in range(K):
            mask = jax.nn.one_hot(topi[:, j], E, dtype=jnp.int32)
            loc_in = jnp.cumsum(mask, axis=0) - 1 + offset[None, :]
            locs.append(jnp.take_along_axis(loc_in, topi[:, j:j + 1], axis=1)[:, 0])
            offset = offset + mask.sum(axis=0)
        loc = jnp.stack(locs, axis=1)
        valid = loc < cap
        flat_idx = jnp.where(valid, topi * cap + loc, 0)
        w = valid.astype(xf.dtype)
        disp = jnp.zeros((E * cap, Dm), xf.dtype)
        disp = disp.at[flat_idx.reshape(-1)].add((xf[:, None, :] * w[:, :, None]).reshape(-1, Dm))
        de = disp.reshape(E, cap, Dm)
        h = jax.nn.relu(jnp.einsum('ecd,ehd->ech', de, fc1_w) + fc1_b)
        eo = jnp.einsum('ech,ehd->ecd', h, fc2_w) + fc2_b
        gathered = eo.reshape(E * cap, Dm)[flat_idx]
        out = jnp.sum(gathered * (gates * w)[:, :, None], axis=1)
        return out.reshape(B, S, Dm)
    x = x + _L0_xattn_ref(_layernorm(x, axis=-1), ctx_1024, L0_xattn_W, L0_xattn_b)
    x = x + _L0_attn_ref(_layernorm(x, axis=-1), L0_attn_Wq, L0_attn_bq, L0_attn_Wk, L0_attn_bk, L0_attn_Wv, L0_attn_bv, L0_attn_Wg, L0_attn_bg, L0_attn_Wo, L0_attn_bo, L0_attn_gn_w, L0_attn_gn_b)
    x = x + _L0_ffn_ref(_layernorm(x, axis=-1), L0_ffn_gate_w, L0_ffn_fc1_w, L0_ffn_fc1_b, L0_ffn_fc2_w, L0_ffn_fc2_b)
    return x

_drawn_inputs = setup_inputs


def setup_inputs(seed=0):
    import zlib

    import numpy as np

    out = dict(_drawn_inputs(seed))
    spreads = {'L0_attn_bq': (0.0, 0.38),
     'L0_attn_bk': (0.0, 0.1),
     'L0_attn_bv': (0.0, 0.1),
     'L0_attn_bg': (0.0, 0.368),
     'L0_attn_bo': (0.0, 0.1),
     'L0_attn_gn_w': (1.0, 0.6),
     'L0_attn_gn_b': (0.0, 0.661),
     'L0_ffn_fc1_b': (0.0, 0.323),
     'L0_ffn_fc2_b': (0.0, 0.1)}
    factors = {}
    for name, (base, spread) in spreads.items():
        noise = np.random.default_rng([zlib.crc32(name.encode()), seed]).standard_normal(out[name].shape)
        drawn = base * np.exp(spread * noise) if base else spread * noise
        out[name] = jnp.asarray(drawn.astype(out[name].dtype))
    for name, factor in factors.items():
        out[name] = (out[name] * factor).astype(out[name].dtype)
    return out
```

```python
from contextlib import ExitStack

import numpy as np

import concourse.bass as bass
from concourse import mybir

F32 = mybir.dt.float32
F16 = mybir.dt.float16
U32 = mybir.dt.uint32
I32 = mybir.dt.int32
ALU = mybir.AluOpType
ACT = mybir.ActivationFunctionType
AX = mybir.AxisListType.X

P = 128
BATCH, SEQ, D = 2, 512, 512
CTX = 8192
TOK = BATCH * SEQ
TILES = TOK // P
SEQ_TILES = SEQ // P
KD = D // P
CHUNK = 512
CHUNKS = CTX // CHUNK
HEADS, HEAD = 16, 32
GROUPS = HEADS * HEAD // P
GH = P // HEAD
EXPERTS, TOPK, HID = 8, 2, 2048
CAP = TOPK * (TOK // EXPERTS)
CAP_TILES = CAP // P
HCHUNK = 512
HCHUNKS = HID // HCHUNK
HT = HCHUNK // P
EPS = 1e-5
W_SCALE = 64.0
P_SCALE = 4096.0
FAR = -1e30
N_W = 5


class Arena:

    def __init__(self, tensor, words):
        self.tensor, self.words, self.at = tensor, words, 0

    def take(self, shape, dtype=F32):
        n = int(np.prod(shape))
        words = n if dtype != F16 else n // 2
        view = self.tensor[:, self.at:self.at + words]
        self.at += words
        assert self.at <= self.words, (self.at, self.words)
        if dtype != F32:
            view = view.bitcast(dtype)
        if len(shape) == 2:
            return view.rearrange("p (a b) -> p a b", a=shape[0])
        if len(shape) == 3:
            return view.rearrange("p (a b c) -> p a b c", a=shape[0], b=shape[1])
        return view


def three(pe, out, left_hi, left_lo, right_hi, right_lo, first, last):
    pe.matmul(out, left_hi, right_hi, start=first, stop=False)
    pe.matmul(out, left_hi, right_lo, start=False, stop=False)
    return pe.matmul(out, left_lo, right_hi, start=False, stop=last)


def perceiver_layer(nc, t):
    ARENA = 29 * 1024
    with ExitStack() as top:
        def sb(name, shape, dtype=F32):
            return top.enter_context(nc.sbuf_tensor(name + "_sb", shape, dtype))

        X = sb("X", [P, TILES, D])
        XN = sb("XN", [P, TILES, D])
        xt_hi = sb("xt_hi", [P, KD, TOK], F16)
        xt_lo = sb("xt_lo", [P, KD, TOK], F16)
        w_hi = sb("w_hi", [P, N_W, KD, D], F16)
        w_lo = sb("w_lo", [P, N_W, KD, D], F16)
        ident = sb("ident", [P, P])
        stats = sb("stats", [P, TILES, 6])
        mv = sb("mv", [P, TILES, 2])
        var = sb("var", [P, TILES])
        std = sb("std", [P, TILES])
        rstd = sb("rstd", [P, TILES])
        arena_t = sb("arena", [P, ARENA])
        banks = [top.enter_context(nc.psum_tensor(f"bank{i}", [P, 512], F32)) for i in range(8)]
        disp = nc.dram_tensor("disp", (EXPERTS * CAP, D), F32, kind="Internal").ap()
        eo_d = nc.dram_tensor("expert_out", (EXPERTS * CAP, D), F32, kind="Internal").ap()

        shared = dict(X=X, XN=XN, xt_hi=xt_hi, xt_lo=xt_lo, w_hi=w_hi, w_lo=w_lo, ident=ident,
                      stats=stats, mv=mv, var=var, std=std, rstd=rstd, banks=banks,
                      disp=disp, eo_d=eo_d)
        used = cross_attention(nc, t, shared, Arena(arena_t, ARENA))
        nc.clear_and_free_semaphores(list(used.values()))
        nc.all_engine_barrier()
        used = retention(nc, t, shared, Arena(arena_t, ARENA))
        nc.clear_and_free_semaphores(list(used.values()))
        nc.all_engine_barrier()
        experts(nc, t, shared, Arena(arena_t, ARENA))


def wait(engine, sem, value):
    if not isinstance(value, int) or value > 0:
        engine.wait_ge(sem, value)


def norm_vector(dve, s, m, sem):
    X, XN, stats, mv, var, rstd = s["X"], s["XN"], s["stats"], s["mv"], s["var"], s["rstd"]
    for i in range(TILES):
        dve.bn_stats(stats[:, i, :], X[:, i, :]).then_inc(sem["ln_stats"], 1)
    for i in range(TILES):
        dve.wait_ge(sem["ln_stats"], i + 1)
        dve.bn_aggr(mv[:, i, :], stats[:, i, :]).then_inc(sem["ln_aggr"], 1)
    dve.wait_ge(sem["ln_aggr"], TILES)
    dve.tensor_scalar(var[:, :], mv[:, :, 1], EPS, None, ALU.add).then_inc(sem["ln_var"], 1)
    dve.wait_ge(sem["ln_std"], 1)
    dve.reciprocal(rstd[:, :], s["std"][:, :]).then_inc(sem["ln_rstd"], 1)
    dve.wait_ge(sem["ln_rstd"], 1)

    def low(i):
        dve.wait_ge(sem["xt_hi"], i + 1)
        dve.tensor_tensor(s["xt_lo"][:, :, i * P:(i + 1) * P], m[i % 2][:, :, :],
                          s["xt_hi"][:, :, i * P:(i + 1) * P], ALU.subtract).then_inc(sem["xt_lo"], 1)
    for i in range(TILES):
        dve.tensor_scalar(XN[:, i, :], X[:, i, :], mv[:, i, 0:1], rstd[:, i:i + 1],
                          ALU.subtract, ALU.mult).then_inc(sem["xn"], 1)
        if i >= 2:
            low(i - 2)
    low(TILES - 2)
    low(TILES - 1)


def norm_scalar(act, s, m, sem):
    act.wait_ge(sem["ln_var"], 1)
    act.activation(s["std"][:, :], s["var"][:, :], ACT.Sqrt).then_inc(sem["ln_std"], 1)
    for i in range(TILES):
        act.wait_ge(sem["xt_psum"], i + 1)
        act.activation(s["xt_hi"][:, :, i * P:(i + 1) * P], m[i % 2][:, :, :], ACT.Copy)\
           .then_inc(sem["xt_hi"], 1)


def norm_tensor(pe, s, m, sem):
    for i in range(TILES):
        pe.wait_ge(sem["xn"], i + 1)
        if i >= 2:
            pe.wait_ge(sem["xt_lo"], i - 1)
        for k in range(KD):
            last = pe.transpose(m[i % 2][:, k, :], s["XN"][:, i, k * P:(k + 1) * P], s["ident"][:, :])
        last.then_inc(sem["xt_psum"], 1)


def semaphores(nc, prefix, names):
    return {n: nc.alloc_semaphore(prefix + n) for n in names}


NORM_SEMS = ["ln_stats", "ln_aggr", "ln_var", "ln_std", "ln_rstd", "xn", "xt_psum", "xt_hi", "xt_lo"]


def cross_attention(nc, t, s, arena):
    X, XN, xt_hi, xt_lo = s["X"], s["XN"], s["xt_hi"], s["xt_lo"]
    LT = SEQ_TILES
    raw_w = arena.take([2, KD, D])
    qt_hi = arena.take([KD, TOK], F16)
    qt_lo = arena.take([KD, TOK], F16)
    ctx_t = arena.take([2, KD, CHUNK])
    ctx_n = arena.take([2, KD, D])
    t_hi, t_lo, n_hi, n_lo = (arena.take([2 * KD, CHUNK], F16) for _ in range(4))
    at_pt = arena.at
    prob = arena.take([2, CHUNK])
    pt_hi = arena.take([2 * 4, P], F16)
    pt_lo = arena.take([2 * 4, P], F16)
    again = Arena(arena.tensor, arena.words)
    again.at = at_pt
    ext_hi = again.take([KD, SEQ], F16)
    ext_lo = again.take([KD, SEQ], F16)
    arena.at = max(arena.at, again.at)
    ext = arena.take([2, SEQ])
    xb = arena.take([KD])
    xb_cols = arena.take([KD])
    xb_hi = arena.take([KD], F16)
    xb_lo = arena.take([KD], F16)
    ex_b = arena.take([TILES])
    ms = [arena.take([TILES]) for _ in range(2)]
    cmax, nbias, drop, alpha, rows = (arena.take([4]) for _ in range(5))
    total = arena.take([TILES])
    recip, recip_s = arena.take([TILES]), arena.take([TILES])
    acc = XN
    bank = s["banks"]
    tp = [bank[i][:, :].rearrange("p (k n) -> p k n", k=KD) for i in range(8)]

    PAIR = 2 * LT
    PAIRS = BATCH * CHUNKS // 2
    UNITS = PAIR * PAIRS

    def within(i, place, count=UNITS, step=PAIR):
        return not isinstance(i, int) or 0 <= step * i + place < count

    def cell(i, place):
        c = (i + place // PAIR) // (CHUNKS // 2) * LT + place % LT
        return slice(c, c + 1) if isinstance(c, int) else bass.ds(c, 1)

    def tile(i, place):
        c = (i + place // PAIR) // (CHUNKS // 2) * LT + place % LT
        return c if isinstance(c, int) else bass.ds(c, 1)

    def queries(i, place):
        c = (i + place // PAIR) // (CHUNKS // 2) * LT + place % LT
        return slice(c * P, c * P + P) if isinstance(c, int) else bass.ds(c * P, P)

    def steps(engine, slot):
        for j in range(-2, PAIR):
            slot(0, j)
        with engine.Fori(1, PAIRS - 1) as i:
            for j in range(PAIR):
                slot(i, j)
        for j in range(PAIR + 1):
            slot(PAIRS - 1, j)

    def split_piece(i, place):
        ahead = place // LT + 1
        return ahead % 2, place % LT, (2 * i + ahead) * KD + place % LT, i + ahead // 2

    with ExitStack() as ctx:
        names = NORM_SEMS + [
            "x_in", "wxt_in", "wxn_in", "xb_in", "ident_in", "raw_in0", "raw_in1",
            "wx_hi", "wx_lo", "xb_s", "xb_h", "xb_l", "ex_psum", "ex", "ex_hi", "ex_lo",
            "q_psum", "q_hi", "q_lo", "exb_psum", "exb", "init", "w_s", "w_h", "w_l",
            "ct_in0", "ct_in1", "cn_in0", "cn_in1", "ct_hi", "ct_lo", "cn_hi", "cn_lo",
            "score", "cmax", "mnew", "nbias", "drop", "alpha", "prob", "pt_psum", "pt_hi", "pt_lo",
            "av", "acc", "total", "recip", "recip_s", "x1"]
        sem = semaphores(nc, "a_", names)
        block = ctx.enter_context(nc.Block())

        @block.sync
        def _(sp):
            sp.dma_start(X[:, :, :], t["x"]).then_inc(sem["x_in"], 16)
            sp.dma_start(s["ident"][:, :], t["ident"]).then_inc(sem["ident_in"], 16)
            sp.dma_start(raw_w[:, 0, :, :], t["wxt"]).then_inc(sem["wxt_in"], 16)
            sp.dma_start(raw_w[:, 1, :, :], t["wxn"]).then_inc(sem["wxn_in"], 16)
            sp.dma_start(xb[:, :], t["xb"]).then_inc(sem["xb_in"], 16)

            def rows(name, i):
                if isinstance(i, int):
                    return t[name][i]
                return t[name][bass.ds(i, 1), :, :, :].rearrange("a p k m -> (a p) k m")

            def chunk(i, parity):
                sp.dma_start(ctx_t[:, parity, :, :], rows("ctx_t", i)).then_inc(sem[f"ct_in{parity}"], 16)
                sp.dma_start(ctx_n[:, parity, :, :], rows("ctx_n", i)).then_inc(sem[f"cn_in{parity}"], 16)
            chunk(0, 0)
            chunk(1, 1)
            for n in range(N_W):
                if n < 2:
                    sp.wait_ge(sem["wx_lo"], KD * (n + 1))
                else:
                    sp.wait_ge(sem["w_l"], n - 1)
                sp.dma_start(raw_w[:, n % 2, :, :], t["w5"][n]).then_inc(sem[f"raw_in{n % 2}"], 16)
            with sp.Fori(1, PAIRS) as i:
                for parity in range(2):
                    for part in ("ct_hi", "ct_lo", "cn_hi", "cn_lo"):
                        sp.wait_ge(sem[part], (2 * i + parity - 1) * KD)
                    chunk(2 * i + parity, parity)

        @block.gpsimd
        def _(pool):
            for n in range(N_W):
                if n == 3:
                    pool.wait_ge(sem["exb_psum"], BATCH)
                raw = raw_w[:, n % 2, :, :]
                pool.wait_ge(sem[f"raw_in{n % 2}"], 16 * (n // 2 + 1))
                pool.tensor_scalar(raw, raw, W_SCALE, None, ALU.mult).then_inc(sem["w_s"], 1)
                pool.wait_ge(sem["w_s"], n + 1)
                pool.tensor_copy(s["w_hi"][:, n, :, :], raw).then_inc(sem["w_h"], 1)
                pool.wait_ge(sem["w_h"], n + 1)
                pool.tensor_tensor(s["w_lo"][:, n, :, :], raw, s["w_hi"][:, n, :, :], ALU.subtract)\
                    .then_inc(sem["w_l"], 1)

        @block.scalar
        def _(act):
            for n, name in enumerate(("wxt_in", "wxn_in")):
                act.wait_ge(sem[name], 16)
                for k in range(KD):
                    act.activation(s["w_hi"][:, 3 + n, k, :], raw_w[:, n, k, :], ACT.Copy, scale=W_SCALE)\
                       .then_inc(sem["wx_hi"], 1)
            act.wait_ge(sem["xb_in"], 16)
            act.activation(xb_cols[:, :], xb[:, :], ACT.Copy, scale=W_SCALE).then_inc(sem["xb_s"], 1)
            act.wait_ge(sem["xb_s"], 1)
            act.activation(xb_hi[:, :], xb_cols[:, :], ACT.Copy).then_inc(sem["xb_h"], 1)
            norm_scalar(act, s, tp, sem)
            for b in range(BATCH):
                for e in range(KD):
                    n = b * KD + e
                    act.wait_ge(sem["ex_psum"], n + 1)
                    wait(act, sem["ex_lo"], n - 1)
                    act.activation(ext[:, n % 2, :], bank[2 + n % 2][:, :], ACT.Identity,
                                   bias=xb[:, e:e + 1], scale=1 / W_SCALE).then_inc(sem["ex"], 1)
                    act.wait_ge(sem["ex"], n + 1)
                    if b and e == 0:
                        act.wait_ge(sem["exb_psum"], b)
                    act.activation(ext_hi[:, e, :], ext[:, n % 2, :], ACT.Copy).then_inc(sem["ex_hi"], 1)
                for d in range(KD):
                    n = b * KD + d
                    act.wait_ge(sem["q_psum"], n + 1)
                    act.activation(qt_hi[:, d, b * SEQ:(b + 1) * SEQ], bank[4 + n % 2][:, :], ACT.Copy,
                                   scale=1 / W_SCALE).then_inc(sem["q_hi"], 1)
            act.wait_ge(sem["init"], 3)

            def t_high(parity, k, count, pair):
                if k == 0:
                    act.wait_ge(sem[f"ct_in{parity}"], 16 * (pair + 1))
                if k == 0:
                    wait(act, sem["score"], count - KD)
                act.activation(t_hi[:, parity * KD + k, :], ctx_t[:, parity, k, :], ACT.Copy)\
                   .then_inc(sem["ct_hi"], 1)

            def n_high(parity, k, count, pair):
                if k == 0:
                    act.wait_ge(sem[f"cn_in{parity}"], 16 * (pair + 1))
                    wait(act, sem["av"], count - KD)
                act.activation(n_hi[:, parity * KD + k, :], ctx_n[:, parity, k, :], ACT.Copy)\
                   .then_inc(sem["cn_hi"], 1)

            def slot(i, j):
                if within(i, j + 2 + LT):
                    t_high(*split_piece(i, j + 2))
                if within(i, j) and within(i, j + LT):
                    n_high(*split_piece(i, j))
                v = PAIR * i + j + 1
                if within(i, j + 1):
                    m = (j + 1) % 2
                    act.wait_ge(sem["pt_psum"], v + 1)
                    wait(act, sem["av"], v - 1)
                    act.activation(pt_hi[:, 4 * m:4 * m + 4, :], tp[2 + m][:, :, :], ACT.Copy,
                                   scale=P_SCALE).then_inc(sem["pt_hi"], 1)
                v = PAIR * i + j + 2
                if within(i, j + 2):
                    m, q, new = (j + 2) % 2, (j + 2) % 4, (j + 2) // LT % 2
                    act.wait_ge(sem["drop"], v + 1)
                    wait(act, sem["acc"], v - 3)
                    wait(act, sem["total"], v - 3)
                    act.activation(alpha[:, q:q + 1], drop[:, q:q + 1], ACT.Exp).then_inc(sem["alpha"], 1)
                    act.wait_ge(sem["nbias"], v + 1)
                    wait(act, sem["pt_psum"], v - 1)
                    act.activation(prob[:, m, :], bank[m][:, :], ACT.Exp, bias=nbias[:, q:q + 1],
                                   accum_out=rows[:, q:q + 1]).then_inc(sem["prob"], 1)
            for k in range(KD):
                t_high(0, k, k, 0)
            for k in range(KD):
                n_high(0, k, k, 0)
            steps(act, slot)

        @block.vector
        def _(dve):
            dve.wait_ge(sem["x_in"], 16)
            norm_vector(dve, s, tp, sem)
            for n in range(2):
                for k in range(KD):
                    dve.wait_ge(sem["wx_hi"], n * KD + k + 1)
                    dve.scalar_tensor_tensor(out=s["w_lo"][:, 3 + n, k, :], in0=raw_w[:, n, k, :],
                                             scalar=W_SCALE, in1=s["w_hi"][:, 3 + n, k, :],
                                             op0=ALU.mult, op1=ALU.subtract).then_inc(sem["wx_lo"], 1)
            dve.wait_ge(sem["xb_h"], 1)
            dve.tensor_tensor(xb_lo[:, :], xb_cols[:, :], xb_hi[:, :], ALU.subtract).then_inc(sem["xb_l"], 1)
            dve.memset(total[:, :], 0.0).then_inc(sem["init"], 1)
            dve.memset(ms[1][:, :], FAR).then_inc(sem["init"], 1)
            dve.wait_ge(sem["xt_psum"], TILES)
            dve.memset(acc[:, :, :], 0.0).then_inc(sem["init"], 1)
            for b in range(BATCH):
                for e in range(KD):
                    n = b * KD + e
                    dve.wait_ge(sem["ex_hi"], n + 1)
                    dve.tensor_tensor(ext_lo[:, e, :], ext[:, n % 2, :], ext_hi[:, e, :], ALU.subtract)\
                       .then_inc(sem["ex_lo"], 1)
                for d in range(KD):
                    n = b * KD + d
                    dve.wait_ge(sem["q_hi"], n + 1)
                    dve.scalar_tensor_tensor(out=qt_lo[:, d, b * SEQ:(b + 1) * SEQ], in0=bank[4 + n % 2][:, :],
                                             scalar=1 / W_SCALE, in1=qt_hi[:, d, b * SEQ:(b + 1) * SEQ],
                                             op0=ALU.mult, op1=ALU.subtract).then_inc(sem["q_lo"], 1)
                dve.wait_ge(sem["exb_psum"], b + 1)
                dve.tensor_scalar(ex_b[:, b * LT:(b + 1) * LT], bank[6][:, b * LT:(b + 1) * LT],
                                  1 / W_SCALE, None, ALU.mult).then_inc(sem["exb"], 1)
            dve.wait_ge(sem["init"], 3)
            dve.wait_ge(sem["exb"], BATCH)

            def t_low(parity, k, count, pair):
                dve.wait_ge(sem["ct_hi"], count + 1)
                dve.tensor_tensor(t_lo[:, parity * KD + k, :], ctx_t[:, parity, k, :],
                                  t_hi[:, parity * KD + k, :], ALU.subtract).then_inc(sem["ct_lo"], 1)

            def n_low(parity, k, count, pair):
                dve.wait_ge(sem["cn_hi"], count + 1)
                dve.tensor_tensor(n_lo[:, parity * KD + k, :], ctx_n[:, parity, k, :],
                                  n_hi[:, parity * KD + k, :], ALU.subtract).then_inc(sem["cn_lo"], 1)

            def slot(i, j):
                v = PAIR * i + j - 1
                if within(i, j - 1):
                    m, q = (j - 1) % 2, (j - 1) % 4
                    dve.wait_ge(sem["av"], v + 1)
                    wait(dve, sem["acc"], v - 3)
                    here = tile(i, j - 1)
                    sums = acc[:, here, :] if isinstance(here, int) else \
                        acc[:, here, :].rearrange("p a d -> p (a d)")
                    dve.scalar_tensor_tensor(out=sums, in0=sums, scalar=alpha[:, q:q + 1],
                                             in1=bank[4 + m][:, :], op0=ALU.mult, op1=ALU.add)\
                       .then_inc(sem["acc"], 1)
                    wait(dve, sem["total"], v - 3)
                    c = cell(i, j - 1)
                    dve.scalar_tensor_tensor(out=total[:, c], in0=total[:, c], scalar=alpha[:, q:q + 1],
                                             in1=rows[:, q:q + 1], op0=ALU.mult, op1=ALU.add)\
                       .then_inc(sem["total"], 1)
                if within(i, j + 2 + LT):
                    t_low(*split_piece(i, j + 2))
                if within(i, j) and within(i, j + LT):
                    n_low(*split_piece(i, j))
                v = PAIR * i + j + 2
                if within(i, j + 2):
                    m, q, new = (j + 2) % 2, (j + 2) % 4, (j + 2) // LT % 2
                    c = cell(i, j + 2)
                    dve.wait_ge(sem["score"], v + 1)
                    dve.reduce_max(cmax[:, q:q + 1], bank[m][:, :], AX).then_inc(sem["cmax"], 1)
                    dve.wait_ge(sem["cmax"], v + 1)
                    dve.tensor_scalar(ms[new][:, c], cmax[:, q:q + 1], ex_b[:, c], ms[1 - new][:, c],
                                      ALU.add, ALU.max).then_inc(sem["mnew"], 1)
                    dve.wait_ge(sem["mnew"], v + 1)
                    dve.tensor_tensor(nbias[:, q:q + 1], ex_b[:, c], ms[new][:, c], ALU.subtract)\
                       .then_inc(sem["nbias"], 1)
                    wait(dve, sem["alpha"], v - 3)
                    dve.tensor_tensor(drop[:, q:q + 1], ms[1 - new][:, c], ms[new][:, c], ALU.subtract)\
                       .then_inc(sem["drop"], 1)
                v = PAIR * i + j + 1
                if within(i, j + 1):
                    m = (j + 1) % 2
                    dve.wait_ge(sem["pt_hi"], v + 1)
                    dve.scalar_tensor_tensor(out=pt_lo[:, 4 * m:4 * m + 4, :], in0=tp[2 + m][:, :, :],
                                             scalar=P_SCALE, in1=pt_hi[:, 4 * m:4 * m + 4, :],
                                             op0=ALU.mult, op1=ALU.subtract).then_inc(sem["pt_lo"], 1)
            for k in range(KD):
                t_low(0, k, k, 0)
            for k in range(KD):
                n_low(0, k, k, 0)
            steps(dve, slot)
            dve.wait_ge(sem["total"], UNITS)
            dve.reciprocal(recip[:, :], total[:, :]).then_inc(sem["recip"], 1)
            dve.wait_ge(sem["recip"], 1)
            dve.tensor_scalar(recip_s[:, :], recip[:, :], 1 / P_SCALE, None, ALU.mult)\
               .then_inc(sem["recip_s"], 1)
            dve.wait_ge(sem["recip_s"], 1)
            dve.wait_ge(sem["acc"], UNITS)
            for n in range(TILES):
                dve.scalar_tensor_tensor(out=X[:, n, :], in0=acc[:, n, :], scalar=recip_s[:, n:n + 1],
                                         in1=X[:, n, :], op0=ALU.mult, op1=ALU.add)\
                   .then_inc(sem["x1"], 1)

        @block.tensor
        def _(pe):
            pe.wait_ge(sem["ident_in"], 16)
            norm_tensor(pe, s, tp, sem)
            for b in range(BATCH):
                pe.wait_ge(sem["xt_lo"], SEQ_TILES * (b + 1))
                seq = slice(b * SEQ, (b + 1) * SEQ)
                for e in range(KD):
                    n = b * KD + e
                    pe.wait_ge(sem["wx_lo"], KD)
                    wait(pe, sem["ex"], n - 1)
                    for k in range(KD):
                        last = three(pe, bank[2 + n % 2][:, :], s["w_hi"][:, 3, k, e * P:(e + 1) * P],
                                     s["w_lo"][:, 3, k, e * P:(e + 1) * P], xt_hi[:, k, seq],
                                     xt_lo[:, k, seq], k == 0, k == KD - 1)
                    last.then_inc(sem["ex_psum"], 1)
                pe.wait_ge(sem["wx_lo"], 2 * KD)
                pe.wait_ge(sem["ex_lo"], KD * (b + 1))
                for d in range(KD):
                    n = b * KD + d
                    wait(pe, sem["q_lo"], n - 1)
                    for e in range(KD):
                        last = three(pe, bank[4 + n % 2][:, :], s["w_hi"][:, 4, e, d * P:(d + 1) * P],
                                     s["w_lo"][:, 4, e, d * P:(d + 1) * P], ext_hi[:, e, :],
                                     ext_lo[:, e, :], e == 0, e == KD - 1)
                    last.then_inc(sem["q_psum"], 1)
                pe.wait_ge(sem["xb_l"], 1)
                wait(pe, sem["exb"], b)
                for n in range(LT):
                    for e in range(KD):
                        last = three(pe, bank[6][:, b * LT + n:b * LT + n + 1],
                                     ext_hi[:, e, n * P:(n + 1) * P], ext_lo[:, e, n * P:(n + 1) * P],
                                     xb_hi[:, e:e + 1], xb_lo[:, e:e + 1], e == 0, e == KD - 1)
                last.then_inc(sem["exb_psum"], 1)
            pe.wait_ge(sem["q_lo"], BATCH * KD)

            def slot(i, j):
                v = PAIR * i + j + 2
                if within(i, j + 2):
                    m, par = (j + 2) % 2, (j + 2) // LT % 2
                    if j % LT == LT - 2:
                        pe.wait_ge(sem["ct_lo"], v + KD)
                    wait(pe, sem["prob"], v - 1)
                    q = queries(i, j + 2)
                    for k in range(KD):
                        last = three(pe, bank[m][:, :], qt_hi[:, k, q], qt_lo[:, k, q],
                                     t_hi[:, par * KD + k, :], t_lo[:, par * KD + k, :],
                                     k == 0, k == KD - 1)
                    last.then_inc(sem["score"], 1)
                v = PAIR * i + j + 1
                if within(i, j + 1):
                    m = (j + 1) % 2
                    pe.wait_ge(sem["prob"], v + 1)
                    wait(pe, sem["pt_lo"], v - 1)
                    for k in range(CHUNK // P):
                        last = pe.transpose(tp[2 + m][:, k, :], prob[:, m, k * P:(k + 1) * P],
                                            s["ident"][:, :])
                    last.then_inc(sem["pt_psum"], 1)
                v = PAIR * i + j
                if within(i, j):
                    m, par = j % 2, j // LT % 2
                    if j % LT == 0:
                        pe.wait_ge(sem["cn_lo"], v + KD)
                    pe.wait_ge(sem["pt_lo"], v + 1)
                    wait(pe, sem["acc"], v - 1)
                    for k in range(CHUNK // P):
                        last = three(pe, bank[4 + m][:, :], pt_hi[:, 4 * m + k, :], pt_lo[:, 4 * m + k, :],
                                     n_hi[:, par * KD + k, :], n_lo[:, par * KD + k, :],
                                     k == 0, k == CHUNK // P - 1)
                    last.then_inc(sem["av"], 1)
            steps(pe, slot)
    return sem


def retention(nc, t, s, arena):
    X, XN, xt_hi, xt_lo, w_hi, w_lo = (s[n] for n in ("X", "XN", "xt_hi", "xt_lo", "w_hi", "w_lo"))
    QT = SEQ_TILES
    HALVES = ("q", "k")
    cos = {h: arena.take([QT, D]) for h in HALVES}
    sin = {h: arena.take([QT, D]) for h in HALVES}
    bias = arena.take([4, D])
    decay = arena.take([2 * GH, SEQ])
    qk_hi = {h: arena.take([GROUPS, SEQ], F16) for h in HALVES}
    qk_lo = {h: arena.take([GROUPS, SEQ], F16) for h in HALVES}
    v_hi = arena.take([QT, D], F16)
    v_lo = arena.take([QT, D], F16)
    gated_hi = arena.take([GROUPS, SEQ], F16)
    gated_lo = arena.take([GROUPS, SEQ], F16)
    bg, gn_w, gn_b = (arena.take([GROUPS]) for _ in range(3))
    same_head = arena.take([P])
    hstats = arena.take([GROUPS, 6])
    hmv = arena.take([GROUPS, 2])
    sums = arena.take([2, GROUPS])
    means = arena.take([2, GROUPS])
    sq, hvar, hstd, hrstd, gscale, gshift, tmp = (arena.take([GROUPS]) for _ in range(7))
    place = arena.at
    biased = {h: arena.take([D]) for h in ("q", "k", "v")}
    swapped = {h: arena.take([D]) for h in HALVES}
    turned = {h: arena.take([D]) for h in HALVES}
    arena.at = place
    masked = arena.take([4, SEQ])
    s_hi = arena.take([8, SEQ], F16)
    s_lo = arena.take([8, SEQ], F16)
    ret = XN[:, 0:GROUPS, :]
    gate = XN[:, GROUPS:2 * GROUPS, :]
    bank = s["banks"]
    tp = [bank[i][:, :].rearrange("p (k n) -> p k n", k=KD) for i in range(8)]
    qkv_banks = [(0, 1, 2), (3, 6, 7)]
    ring = (0, 1, 2, 3, 6, 7)
    STEPS = GROUPS * QT

    def pairs(row):
        return row.rearrange("p (a two) -> p a two", two=2)

    with ExitStack() as ctx:
        names = NORM_SEMS + [f"{a}_{b}_in" for a in ("q", "k") for b in ("cos", "sin")] + [
            "bias_in", "bg_in", "gnw_in", "gnb_in", "same_in", "decay_in0", "decay_in1",
            "qkv", "q_b", "k_b", "v_b", "q_cos", "k_cos", "q_swap", "k_swap", "q_turn", "k_turn", "v_hi", "v_lo",
            "q_tp", "k_tp", "q_hi", "k_hi", "q_lo", "k_lo", "gate_psum", "gate",
            "score", "masked", "s_hi", "s_lo_dve", "s_lo_pool", "pv", "ret", "hstats", "hmv",
            "sums", "head_psum", "small", "hvar", "hstd", "gshift", "gn", "gated", "g_hi", "g_lo",
            "wo", "x2a", "x2"]
        sem = semaphores(nc, "r_", names)
        block = ctx.enter_context(nc.Block())

        @block.sync
        def _(sp):
            for h in HALVES:
                sp.dma_start(cos[h], t[h + "_cos"]).then_inc(sem[f"{h}_cos_in"], 16)
                sp.dma_start(sin[h], t[h + "_sin"]).then_inc(sem[f"{h}_sin_in"], 16)
            sp.dma_start(bias, t["bias_rows"]).then_inc(sem["bias_in"], 16)
            sp.dma_start(bg, t["bg"]).then_inc(sem["bg_in"], 16)
            sp.dma_start(gn_w, t["gn_w"]).then_inc(sem["gnw_in"], 16)
            sp.dma_start(gn_b, t["gn_b"]).then_inc(sem["gnb_in"], 16)
            sp.dma_start(same_head, t["same_head"]).then_inc(sem["same_in"], 16)
            for n in range(BATCH * GROUPS):
                wait(sp, sem["masked"], (n - 1) * QT * GH)
                sp.dma_start(decay[:, n % 2 * GH:(n % 2 + 1) * GH, :], t["decay"][n % GROUPS])\
                    .then_inc(sem[f"decay_in{n % 2}"], 16)

        @block.gpsimd
        def _(pool):
            def swap(i):
                for h in HALVES:
                    if i == 0:
                        pool.wait_ge(sem[f"{h}_sin_in"], 16)
                    pool.wait_ge(sem[f"{h}_b"], i + 1)
                    wait(pool, sem[f"{h}_turn"], i)
                    a, b, c = pairs(swapped[h]), pairs(biased[h]), pairs(sin[h][:, i % QT, :])
                    for o in range(2):
                        pool.tensor_tensor(a[:, :, o], b[:, :, 1 - o], c[:, :, o], ALU.mult)\
                            .then_inc(sem[f"{h}_swap"], 1)

            def low(r):
                for j in range(2, GH):
                    m = GH * r + j
                    n = SEQ - r % QT * P
                    pool.wait_ge(sem["s_hi"], m + 1)
                    pool.tensor_tensor(s_lo[:, m % 8, 0:n], masked[:, m % 4, 0:n], s_hi[:, m % 8, 0:n],
                                       ALU.subtract).then_inc(sem["s_lo_pool"], 1)
            def out_bias(i):
                pool.wait_ge(sem["x2a"], i + 1)
                pool.tensor_tensor(X[:, i, :], X[:, i, :], bias[:, 3, :], ALU.add).then_inc(sem["x2"], 1)

            for b in range(BATCH):
                for i in range(QT):
                    swap(b * QT + i)
                for i in range(QT * (b - 1), QT * b):
                    if b:
                        out_bias(i)
                for r in range(STEPS):
                    low(b * STEPS + r)
            for i in range(QT * (BATCH - 1), QT * BATCH):
                out_bias(i)

        @block.scalar
        def _(act):
            norm_scalar(act, s, tp[4:6], sem)

            def v_high(i):
                act.wait_ge(sem["v_b"], i + 1)
                wait(act, sem["pv"], i // QT * STEPS)
                act.activation(v_hi[:, i % QT, :], biased["v"], ACT.Copy).then_inc(sem["v_hi"], 1)

            def qk_high(i):
                for n, h in enumerate(HALVES):
                    act.wait_ge(sem[f"{h}_tp"], i + 1)
                    act.activation(qk_hi[h][:, :, i % QT * P:(i % QT + 1) * P], tp[4 + n][:, :, :], ACT.Copy)\
                       .then_inc(sem[f"{h}_hi"], 1)

            def gates(b):
                if b == 0:
                    act.wait_ge(sem["bg_in"], 16)
                for g in range(GROUPS):
                    act.wait_ge(sem["gate_psum"], b * GROUPS + g + 1)
                    wait(act, sem["gated"], b * GROUPS)
                    act.activation(gate[:, g, :], bank[g % 2][:, :], ACT.Silu, bias=bg[:, g:g + 1],
                                   scale=1 / W_SCALE).then_inc(sem["gate"], 1)

            def gated_high(b):
                act.wait_ge(sem["hvar"], b + 1)
                act.activation(hstd, hvar, ACT.Sqrt).then_inc(sem["hstd"], 1)
                for g in range(GROUPS):
                    act.wait_ge(sem["gated"], b * GROUPS + g + 1)
                    act.activation(gated_hi[:, g, :], ret[:, g, :], ACT.Copy).then_inc(sem["g_hi"], 1)

            def evacuate(n):
                act.wait_ge(sem["pv"], (n + 1) * QT)
                wait(act, sem["g_lo"], n // GROUPS * GROUPS)
                act.activation(ret[:, n % GROUPS, :], bank[4 + n % 2][:, :], ACT.Copy).then_inc(sem["ret"], 1)

            for b in range(BATCH):
                v_high(b * QT)
                if b:
                    gated_high(b - 1)
                for i in range(1, QT):
                    v_high(b * QT + i)
                    qk_high(b * QT + i - 1)
                gates(b)
                qk_high(b * QT + QT - 1)
                for r in range(STEPS):
                    for j in range(GH):
                        m = GH * (b * STEPS + r) + j
                        n = SEQ - r % QT * P
                        act.wait_ge(sem["masked"], m + 1)
                        wait(act, sem["pv"], m // GH - 1)
                        act.activation(s_hi[:, m % 8, 0:n], masked[:, m % 4, 0:n], ACT.Copy)\
                           .then_inc(sem["s_hi"], 1)
                    if r and r % QT == 0:
                        evacuate(b * GROUPS + r // QT - 1)
                evacuate(b * GROUPS + GROUPS - 1)
            gated_high(BATCH - 1)

        @block.vector
        def _(dve):
            norm_vector(dve, s, tp[4:6], sem)
            small = [0]

            def link(ins):
                small[0] += 1
                ins.then_inc(sem["small"], 1)
                dve.wait_ge(sem["small"], small[0])

            def project(i):
                if i == 0:
                    dve.wait_ge(sem["bias_in"], 16)
                for n, h in enumerate(("q", "k", "v")):
                    dve.wait_ge(sem["qkv"], 3 * i + n + 1)
                    if h == "v":
                        wait(dve, sem["v_lo"], i)
                    else:
                        wait(dve, sem[f"{h}_swap"], 2 * i)
                        wait(dve, sem[f"{h}_cos"], i)
                    if i and i % QT == 0:
                        dve.wait_ge(sem["pv"], i // QT * STEPS)
                        dve.wait_ge(sem["s_lo_pool"], i // QT * STEPS * 2)
                    dve.scalar_tensor_tensor(out=biased[h], in0=bank[qkv_banks[i % 2][n]][:, :],
                                             scalar=1 / W_SCALE, in1=bias[:, n, :], op0=ALU.mult, op1=ALU.add)\
                       .then_inc(sem[f"{h}_b"], 1)
                for h in HALVES:
                    if i == 0:
                        dve.wait_ge(sem[f"{h}_cos_in"], 16)
                    dve.wait_ge(sem[f"{h}_b"], i + 1)
                    wait(dve, sem[f"{h}_tp"], i)
                    dve.tensor_tensor(turned[h], biased[h], cos[h][:, i % QT, :], ALU.mult)\
                       .then_inc(sem[f"{h}_cos"], 1)
                dve.wait_ge(sem["v_hi"], i + 1)
                dve.tensor_tensor(v_lo[:, i % QT, :], biased["v"], v_hi[:, i % QT, :], ALU.subtract)\
                   .then_inc(sem["v_lo"], 1)
                for h in HALVES:
                    dve.wait_ge(sem[f"{h}_swap"], 2 * i + 2)
                    dve.wait_ge(sem[f"{h}_cos"], i + 1)
                    dve.tensor_tensor(turned[h], turned[h], swapped[h], ALU.add).then_inc(sem[f"{h}_turn"], 1)

            def qk_low(i):
                for n, h in enumerate(HALVES):
                    dve.wait_ge(sem[f"{h}_hi"], i + 1)
                    rows = slice(i % QT * P, (i % QT + 1) * P)
                    dve.tensor_tensor(qk_lo[h][:, :, rows], tp[4 + n][:, :, :], qk_hi[h][:, :, rows],
                                      ALU.subtract).then_inc(sem[f"{h}_lo"], 1)

            def head_stats(n):
                g = n % GROUPS
                dve.wait_ge(sem["ret"], n + 1)
                dve.bn_stats(hstats[:, g, :], ret[:, g, :]).then_inc(sem["hstats"], 1)
                dve.wait_ge(sem["hstats"], n + 1)
                dve.bn_aggr(hmv[:, g, :], hstats[:, g, :]).then_inc(sem["hmv"], 1)

            def head_sums(b):
                dve.wait_ge(sem["hmv"], (b + 1) * GROUPS)
                link(dve.tensor_tensor(sq, hmv[:, :, 0], hmv[:, :, 0], ALU.mult))
                link(dve.tensor_copy(sums[:, 0, :], hmv[:, :, 0]))
                dve.tensor_tensor(sums[:, 1, :], sq, hmv[:, :, 1], ALU.add).then_inc(sem["sums"], 1)

            def group_norm(b):
                dve.wait_ge(sem["head_psum"], b + 1)
                link(dve.tensor_copy(means, bank[5][:, 0:2 * GROUPS].rearrange("p (a g) -> p a g", a=2)))
                link(dve.tensor_tensor(sq, means[:, 0, :], means[:, 0, :], ALU.mult))
                link(dve.tensor_tensor(tmp, means[:, 1, :], sq, ALU.subtract))
                dve.tensor_scalar(hvar, tmp, EPS, None, ALU.add).then_inc(sem["hvar"], 1)
                dve.wait_ge(sem["hstd"], b + 1)
                link(dve.reciprocal(hrstd, hstd))
                if b == 0:
                    dve.wait_ge(sem["gnw_in"], 16)
                    dve.wait_ge(sem["gnb_in"], 16)
                link(dve.tensor_tensor(gscale, gn_w, hrstd, ALU.mult))
                link(dve.tensor_tensor(tmp, means[:, 0, :], gscale, ALU.mult))
                link(dve.tensor_tensor(gshift, gn_b, tmp, ALU.subtract))
                for g in range(GROUPS):
                    n = b * GROUPS + g
                    dve.tensor_scalar(ret[:, g, :], ret[:, g, :], gscale[:, g:g + 1], gshift[:, g:g + 1],
                                      ALU.mult, ALU.add).then_inc(sem["gn"], 1)
                    dve.wait_ge(sem["gate"], n + 1)
                    dve.wait_ge(sem["gn"], n + 1)
                    dve.tensor_tensor(ret[:, g, :], ret[:, g, :], gate[:, g, :], ALU.mult)\
                       .then_inc(sem["gated"], 1)
                for g in range(GROUPS):
                    n = b * GROUPS + g
                    dve.wait_ge(sem["g_hi"], n + 1)
                    dve.tensor_tensor(gated_lo[:, g, :], ret[:, g, :], gated_hi[:, g, :], ALU.subtract)\
                       .then_inc(sem["g_lo"], 1)

            def residual(b):
                for i in range(b * QT, (b + 1) * QT):
                    dve.wait_ge(sem["wo"], i + 1)
                    dve.scalar_tensor_tensor(out=X[:, i, :], in0=bank[i % 2][:, :], scalar=1 / W_SCALE,
                                             in1=X[:, i, :], op0=ALU.mult, op1=ALU.add).then_inc(sem["x2a"], 1)

            for b in range(BATCH):
                if b:
                    head_sums(b - 1)
                project(b * QT)
                if b:
                    group_norm(b - 1)
                for i in range(1, QT):
                    project(b * QT + i)
                    qk_low(b * QT + i - 1)
                if b:
                    residual(b - 1)
                qk_low(b * QT + QT - 1)
                for r in range(STEPS):
                    g, kt = r // QT, r % QT
                    n = SEQ - kt * P
                    gi = b * GROUPS + g
                    if kt == 0:
                        dve.wait_ge(sem[f"decay_in{g % 2}"], 16 * (gi // 2 + 1))
                    for j in range(GH):
                        m = GH * (b * STEPS + r) + j
                        dve.wait_ge(sem["score"], m + 1)
                        wait(dve, sem["s_lo_dve" if j < 2 else "s_lo_pool"], 2 * (m // GH - 1) + j % 2 + 1
                             if m >= GH else 0)
                        dve.tensor_tensor(masked[:, m % 4, 0:n], bank[ring[m % 6]][:, 0:n],
                                          decay[:, g % 2 * GH + j, 0:n], ALU.mult).then_inc(sem["masked"], 1)
                    for j in range(2):
                        m = GH * (b * STEPS + r) + j
                        dve.wait_ge(sem["s_hi"], m + 1)
                        dve.tensor_tensor(s_lo[:, m % 8, 0:n], masked[:, m % 4, 0:n], s_hi[:, m % 8, 0:n],
                                          ALU.subtract).then_inc(sem["s_lo_dve"], 1)
                    if g and kt == 1:
                        head_stats(gi - 1)
                head_stats(b * GROUPS + GROUPS - 1)
            head_sums(BATCH - 1)
            group_norm(BATCH - 1)
            residual(BATCH - 1)

        @block.tensor
        def _(pe):
            norm_tensor(pe, s, tp[4:6], sem)

            def project(i):
                pe.wait_ge(sem["xt_lo"], i + 1)
                if i and i % QT == 0:
                    pe.wait_ge(sem["masked"], i // QT * STEPS * GH)
                for n, h in enumerate(("q", "k", "v")):
                    wait(pe, sem[f"{h}_b"], i - 1)
                    for k in range(KD):
                        last = three(pe, bank[qkv_banks[i % 2][n]][:, :], xt_hi[:, k, i * P:(i + 1) * P],
                                     xt_lo[:, k, i * P:(i + 1) * P], w_hi[:, n, k, :], w_lo[:, n, k, :],
                                     k == 0, k == KD - 1)
                    last.then_inc(sem["qkv"], 1)

            def turn(i):
                if i == 0:
                    pe.wait_ge(sem["xt_lo"], TILES)
                elif i % QT == 0:
                    pe.wait_ge(sem["ret"], i // QT * GROUPS)
                    pe.wait_ge(sem["hvar"], i // QT)
                for n, h in enumerate(HALVES):
                    pe.wait_ge(sem[f"{h}_turn"], i + 1)
                    wait(pe, sem[f"{h}_lo"], i)
                    for g in range(GROUPS):
                        last = pe.transpose(tp[4 + n][:, g, :], turned[h][:, g * P:(g + 1) * P],
                                            s["ident"][:, :])
                    last.then_inc(sem[f"{h}_tp"], 1)

            def gates(b):
                for g in range(GROUPS):
                    n = b * GROUPS + g
                    if g < 2:
                        pe.wait_ge(sem["qkqk"[g] + "_b"], b * QT + QT - 1)
                        wait(pe, sem["x2a"], b * QT)
                    else:
                        pe.wait_ge(sem["gate"], n - 1)
                    for k in range(KD):
                        last = three(pe, bank[g % 2][:, :], w_hi[:, 3, k, g * P:(g + 1) * P],
                                     w_lo[:, 3, k, g * P:(g + 1) * P], xt_hi[:, k, b * SEQ:(b + 1) * SEQ],
                                     xt_lo[:, k, b * SEQ:(b + 1) * SEQ], k == 0, k == KD - 1)
                    last.then_inc(sem["gate_psum"], 1)

            def head_means(b):
                if b == 0:
                    pe.wait_ge(sem["same_in"], 16)
                pe.wait_ge(sem["ret"], (b + 1) * GROUPS)
                pe.wait_ge(sem["sums"], b + 1)
                pe.matmul(bank[5][:, 0:2 * GROUPS], same_head, sums.rearrange("p a g -> p (a g)"),
                          start=True, stop=True).then_inc(sem["head_psum"], 1)

            def out(b):
                for i in range(b * QT, (b + 1) * QT):
                    if i % QT == 0:
                        pe.wait_ge(sem["g_lo"], (b + 1) * GROUPS)
                    if i % QT < 2:
                        if b < BATCH - 1:
                            pe.wait_ge(sem["qkqk"[i % QT] + "_b"], (b + 1) * QT + QT - 1)
                    else:
                        pe.wait_ge(sem["x2a"], i - 1)
                    c = i % QT
                    for g in range(GROUPS):
                        last = three(pe, bank[i % 2][:, :], gated_hi[:, g, c * P:(c + 1) * P],
                                     gated_lo[:, g, c * P:(c + 1) * P], w_hi[:, 4, g, :], w_lo[:, 4, g, :],
                                     g == 0, g == GROUPS - 1)
                    last.then_inc(sem["wo"], 1)

            def scores(b, r):
                g, kt = r // QT, r % QT
                n = SEQ - kt * P
                m = GH * (b * STEPS + r)
                if r:
                    pe.wait_ge(sem["masked"], m - 2)
                else:
                    for name in ("q_lo", "k_lo", "v_lo"):
                        pe.wait_ge(sem[name], (b + 1) * QT)
                    pe.wait_ge(sem["gate"], (b + 1) * GROUPS)
                for p in range(3):
                    for j in range(GH):
                        keys = (qk_lo if p == 2 else qk_hi)["k"]
                        queries = (qk_lo if p == 1 else qk_hi)["q"]
                        rows = slice(j * HEAD, (j + 1) * HEAD)
                        last = pe.matmul(bank[ring[(m + j) % 6]][:, 0:n], keys[rows, g, kt * P:(kt + 1) * P],
                                         queries[rows, g, kt * P:SEQ], start=(p == 0), stop=(p == 2))
                        if p == 2:
                            last.then_inc(sem["score"], 1)

            def values(b, r):
                g, kt = r // QT, r % QT
                n = SEQ - kt * P
                r += b * STEPS
                pe.wait_ge(sem["s_lo_dve"], 2 * r + 2)
                pe.wait_ge(sem["s_lo_pool"], 2 * r + 2)
                if kt == 0:
                    wait(pe, sem["ret"], b * GROUPS + g - 1)
                for p in range(3):
                    for j in range(GH):
                        m = (GH * r + j) % 8
                        v = (v_lo if p == 2 else v_hi)[:, kt, (GH * g + j) * HEAD:(GH * g + j + 1) * HEAD]
                        sc = (s_lo if p == 1 else s_hi)[:, m, 0:n]
                        last = pe.matmul(bank[4 + g % 2][j * HEAD:(j + 1) * HEAD, kt * P:SEQ], v, sc,
                                         start=(kt == 0 and p == 0), stop=(kt == QT - 1 and p == 2))
                last.then_inc(sem["pv"], 1)

            for b in range(BATCH):
                project(b * QT)
                if b:
                    head_means(b - 1)
                for i in range(1, QT):
                    project(b * QT + i)
                    turn(b * QT + i - 1)
                if b:
                    out(b - 1)
                gates(b)
                turn(b * QT + QT - 1)
                for r in range(STEPS):
                    scores(b, r)
                    if r:
                        values(b, r - 1)
                values(b, STEPS - 1)
            head_means(BATCH - 1)
            out(BATCH - 1)
    return sem


def experts(nc, t, s, arena):
    X, XN, xt_hi, xt_lo = s["X"], s["XN"], s["xt_hi"], s["xt_lo"]
    PICKS = TOPK * TILES
    raw_t = arena.take([2, KD, HCHUNK])
    raw_n = arena.take([2, HT, D])
    t_hi, t_lo, n_hi, n_lo = (arena.take([2 * KD, HCHUNK], F16) for _ in range(4))
    hidden = arena.take([2, HT * CAP])
    h_hi = arena.take([2 * HT, CAP], F16)
    h_lo = arena.take([2 * HT, CAP], F16)
    de = arena.take([CAP_TILES, D])
    de_hi = arena.take([KD, CAP], F16)
    de_lo = arena.take([KD, CAP], F16)
    eo = arena.take([CAP_TILES, D])
    b1 = arena.take([HID // P])
    b2 = arena.take([D])
    zeros = arena.take([D])
    gw = arena.take([KD, EXPERTS])
    gw_s = arena.take([KD, EXPERTS])
    gw_hi = arena.take([KD, EXPERTS], F16)
    gw_lo = arena.take([KD, EXPERTS], F16)
    number = arena.take([EXPERTS])
    before = arena.take([P], F16)
    ones = arena.take([P], F16)
    logits, shifted, raised, score = (arena.take([TILES, EXPERTS]) for _ in range(4))
    top8 = arena.take([TILES, 8])
    top8_at = arena.take([TILES, 8]).bitcast(U32)
    peak, mass, mass_r, pair, pair_r = (arena.take([TILES]) for _ in range(5))
    expert = arena.take([TOPK, TILES])
    chosen = arena.take([PICKS, EXPERTS])
    chosen_h = arena.take([PICKS, EXPERTS], F16)
    spread = arena.take([PICKS, EXPERTS])
    loc, valid, flat, kept, far = (arena.take([PICKS]) for _ in range(5))
    weight = arena.take([TOPK, TILES])
    to_slot = arena.take([PICKS]).bitcast(U32)
    from_slot = arena.take([PICKS]).bitcast(U32)
    over = Arena(arena.tensor, arena.words)
    got = over.take([PICKS, D])
    bank = s["banks"]
    tp = [bank[i][:, :].rearrange("p (k n) -> p k n", k=KD) for i in range(8)]
    CHUNKS_ALL = EXPERTS * HCHUNKS
    SLOTS = EXPERTS * CAP
    FAR_SLOT = 2 * SLOTS

    def within(e, place):
        return not isinstance(e, int) or 0 <= HCHUNKS * e + place < CHUNKS_ALL

    def steps(engine, slot):
        for c in range(-1, HCHUNKS):
            slot(0, c)
        with engine.Fori(1, EXPERTS - 1) as e:
            for c in range(HCHUNKS):
                slot(e, c)
        for c in range(HCHUNKS + 1):
            slot(EXPERTS - 1, c)

    with ExitStack() as ctx:
        names = NORM_SEMS + [
            "gw_in", "number_in", "before_in", "zero", "zeroed", "gw_s", "gw_hi", "gw_lo", "ones",
            "logit_psum", "small", "raised", "expd", "chosen", "loc_psum", "routed", "scattered",
            "t_in0", "t_in1", "n_in0", "n_in1", "b1_in", "b2_in", "de_in", "de_tp", "de_hi", "de_lo",
            "t_hi", "t_lo", "n_hi", "n_lo", "fc1", "relu", "h_hi", "h_lo", "fc2", "eo", "eo_out",
            "half", "sum", "out"]
        sem = semaphores(nc, "e_", names)
        got_in = [nc.alloc_semaphore(f"e_got_in{n}") for n in range(PICKS)]
        block = ctx.enter_context(nc.Block())

        @block.sync
        def _(sp):
            def at(a, i):
                if isinstance(i, int):
                    return a[i]
                a = a[bass.ds(i, 1)]
                return a.rearrange("a p n -> (a p) n") if len(a.shape) == 3 else \
                    a.rearrange("a p k n -> (a p) k n")

            def weights(e, c, part):
                u = HCHUNKS * e + c
                name, raw = (("t", raw_t), ("n", raw_n))[part]
                wait(sp, sem[name + "_hi"], (u - 1) * KD)
                wait(sp, sem[name + "_lo"], (u - 1) * KD)
                sp.dma_start(raw[:, c % 2], at(t[("fc1", "fc2")[part]], u)).then_inc(sem[f"{name}_in{c % 2}"], 16)

            def tokens(e):
                wait(sp, sem["de_tp"], CAP_TILES * e)
                src = s["disp"].rearrange("(e a p) d -> e p a d", p=P, a=CAP_TILES)
                sp.dma_start(de, at(src, e)).then_inc(sem["de_in"], 16)

            def bias1(e):
                wait(sp, sem["relu"], HT * HCHUNKS * e)
                sp.dma_start(b1, at(t["fc1_b"], e)).then_inc(sem["b1_in"], 16)

            def store(e):
                sp.wait_ge(sem["eo"], CAP_TILES * (e + 1))
                dst = s["eo_d"].rearrange("(e a p) d -> e p a d", p=P, a=CAP_TILES)
                sp.dma_start(at(dst, e), eo).then_inc(sem["eo_out"], 16)

            def bias2(e):
                wait(sp, sem["eo"], CAP_TILES * e)
                sp.dma_start(b2, at(t["fc2_b"], e)).then_inc(sem["b2_in"], 16)

            sp.dma_start(gw, t["gate_w"]).then_inc(sem["gw_in"], 16)
            sp.dma_start(number, t["expert_no"]).then_inc(sem["number_in"], 16)
            sp.dma_start(before, t["before"]).then_inc(sem["before_in"], 16)
            sp.wait_ge(sem["zero"], 1)
            for n in range(SLOTS // P):
                sp.dma_start(s["disp"][n * P:(n + 1) * P, :], zeros).then_inc(sem["zeroed"], 16)
            for c in range(2):
                weights(0, c, 0)
                weights(0, c, 1)
            bias1(0)
            bias2(0)
            sp.wait_ge(sem["scattered"], 16 * PICKS)
            tokens(0)
            for c in range(2, HCHUNKS):
                weights(0, c, 0)
                weights(0, c, 1)
            tokens(1)

            def step(e, last):
                for c in range(HCHUNKS):
                    weights(e, c, 0)
                    weights(e, c, 1)
                    if c == 1:
                        bias1(e)
                store(e - 1)
                bias2(e)
                if not last:
                    tokens(e + 1)
            with sp.Fori(1, EXPERTS - 1) as e:
                step(e, False)
            step(EXPERTS - 1, True)
            store(EXPERTS - 1)
            for i in range(TILES):
                sp.wait_ge(sem["sum"], i + 1)
                sp.dma_start(t["out"][:, i, :], X[:, i, :]).then_inc(sem["out"], 16)
            sp.wait_ge(sem["out"], 16 * TILES)

        @block.gpsimd
        def _(pool):
            pool.memset(zeros, 0.0).then_inc(sem["zero"], 1)
            pool.memset(ones, 1.0).then_inc(sem["ones"], 1)
            pool.wait_ge(sem["zeroed"], 16 * (SLOTS // P))
            pool.wait_ge(sem["xn"], TILES)
            pool.wait_ge(sem["routed"], 1)
            for n in range(PICKS):
                pool.indirect_dma_start(
                    out=s["disp"], out_offset=bass.IndirectOffsetOnAxis(ap=to_slot[:, n:n + 1], axis=0),
                    in_=XN[:, n % TILES, :], in_offset=None, bounds_check=SLOTS - 1, oob_is_err=False)\
                    .then_inc(sem["scattered"], 16)
            pool.wait_ge(sem["eo_out"], 16 * EXPERTS)
            for i in range(TILES):
                for k in range(TOPK):
                    n = k * TILES + i
                    pool.indirect_dma_start(
                        out=got[:, n, :], out_offset=None, in_=s["eo_d"],
                        in_offset=bass.IndirectOffsetOnAxis(ap=from_slot[:, n:n + 1], axis=0),
                        bounds_check=SLOTS - 1, oob_is_err=False).then_inc(got_in[n], 16)

        @block.scalar
        def _(act):
            act.wait_ge(sem["gw_in"], 16)
            act.activation(gw_s, gw, ACT.Copy, scale=W_SCALE).then_inc(sem["gw_s"], 1)
            act.wait_ge(sem["gw_s"], 1)
            act.activation(gw_hi, gw_s, ACT.Copy).then_inc(sem["gw_hi"], 1)
            norm_scalar(act, s, tp, sem)
            act.wait_ge(sem["raised"], 1)
            act.activation(raised, shifted, ACT.Exp).then_inc(sem["expd"], 1)

            def t_high(e, place):
                par = place % 2
                act.wait_ge(sem[f"t_in{par}"], 16 * (HCHUNKS // 2 * e + place // 2 + 1))
                wait(act, sem["fc1"], 2 * (HCHUNKS * e + place - 1))
                for k in range(KD):
                    act.activation(t_hi[:, par * KD + k, :], raw_t[:, par, k, :], ACT.Copy, scale=W_SCALE)\
                       .then_inc(sem["t_hi"], 1)

            def n_high(e, place):
                par = place % 2
                act.wait_ge(sem[f"n_in{par}"], 16 * (HCHUNKS // 2 * e + place // 2 + 1))
                wait(act, sem["fc2"], HCHUNKS * e + place - 1)
                for k in range(HT):
                    act.activation(n_hi[:, par * HT + k, :], raw_n[:, par, k, :], ACT.Copy, scale=W_SCALE)\
                       .then_inc(sem["n_hi"], 1)

            def de_high(e):
                for a in range(CAP_TILES):
                    act.wait_ge(sem["de_tp"], CAP_TILES * e + a + 1)
                    act.activation(de_hi[:, :, a * P:(a + 1) * P], tp[2 + a][:, :, :], ACT.Copy)\
                       .then_inc(sem["de_hi"], 1)

            def relus(e, place):
                u = HCHUNKS * e + place
                if place % HCHUNKS == 0:
                    act.wait_ge(sem["b1_in"], 16 * (e + place // HCHUNKS + 1))
                for h in range(HT):
                    if h % 2 == 0:
                        act.wait_ge(sem["fc1"], 2 * u + h // 2 + 1)
                        wait(act, sem["h_lo"], u - 1)
                    act.activation(hidden[:, place % 2, h * CAP:(h + 1) * CAP],
                                   bank[h // 2][:, h % 2 * CAP:(h % 2 + 1) * CAP], ACT.Relu,
                                   bias=b1[:, place % HCHUNKS * HT + h:place % HCHUNKS * HT + h + 1],
                                   scale=1 / W_SCALE).then_inc(sem["relu"], 1)

            def h_high(e, place):
                u = HCHUNKS * e + place
                par = place % 2
                act.wait_ge(sem["relu"], HT * (u + 1))
                wait(act, sem["fc2"], u - 1)
                act.activation(h_hi[:, par * HT:(par + 1) * HT, :].rearrange("p a c -> p (a c)"),
                               hidden[:, par, :], ACT.Copy).then_inc(sem["h_hi"], 1)

            def slot(e, c):
                if within(e, c + 2):
                    t_high(e, c + 2)
                if within(e, c + 1):
                    n_high(e, c + 1)
                    relus(e, c + 1)
                if c == 2 and (not isinstance(e, int) or e < EXPERTS - 1):
                    de_high(e + 1)
                if within(e, c + 1):
                    h_high(e, c + 1)
            t_high(0, 0)
            de_high(0)
            steps(act, slot)

        @block.vector
        def _(dve):
            norm_vector(dve, s, tp, sem)
            dve.wait_ge(sem["gw_hi"], 1)
            dve.tensor_tensor(gw_lo, gw_s, gw_hi, ALU.subtract).then_inc(sem["gw_lo"], 1)
            small = [0]

            def link(ins):
                small[0] += 1
                ins.then_inc(sem["small"], 1)
                dve.wait_ge(sem["small"], small[0])

            def along(a):
                return a.unsqueeze(2).to_broadcast([P, a.shape[1], EXPERTS])

            dve.wait_ge(sem["logit_psum"], 1)
            link(dve.tensor_scalar(logits, bank[2][:, 0:TILES * EXPERTS].rearrange("p (i e) -> p i e", e=EXPERTS),
                                   1 / W_SCALE, None, ALU.mult))
            link(dve.reduce_max(peak, logits, AX))
            dve.tensor_tensor(shifted, logits, along(peak), ALU.subtract).then_inc(sem["raised"], 1)
            dve.wait_ge(sem["expd"], 1)
            link(dve.reduce_sum(mass, raised, AX))
            link(dve.reciprocal(mass_r, mass))
            link(dve.tensor_tensor(score, raised, along(mass_r), ALU.mult))
            for i in range(TILES):
                link(dve.max(top8[:, i, :], score[:, i, :]))
                link(dve.max_index(top8_at[:, i, :], top8[:, i, :], score[:, i, :]))
            link(dve.tensor_tensor(pair, top8[:, :, 0], top8[:, :, 1], ALU.add))
            link(dve.reciprocal(pair_r, pair))
            for k in range(TOPK):
                link(dve.tensor_copy(expert[:, k, :], top8_at[:, :, k]))
            dve.wait_ge(sem["number_in"], 16)
            link(dve.tensor_tensor(chosen, along(expert.rearrange("p k i -> p (k i)")),
                                   number.unsqueeze(1).to_broadcast([P, PICKS, EXPERTS]), ALU.is_equal))
            dve.tensor_copy(chosen_h, chosen).then_inc(sem["chosen"], 1)
            dve.wait_ge(sem["loc_psum"], 1)
            link(dve.tensor_tensor(spread, bank[3][:, 0:PICKS * EXPERTS].rearrange("p (n e) -> p n e", e=EXPERTS),
                                   chosen, ALU.mult))
            link(dve.reduce_sum(loc, spread, AX))
            link(dve.tensor_scalar(valid, loc, float(CAP), None, ALU.is_lt))
            link(dve.scalar_tensor_tensor(out=flat, in0=expert.rearrange("p k i -> p (k i)"), scalar=float(CAP),
                                          in1=loc, op0=ALU.mult, op1=ALU.add))
            link(dve.tensor_tensor(kept, flat, valid, ALU.mult))
            link(dve.tensor_copy(from_slot, kept))
            link(dve.tensor_scalar(far, flat, -float(FAR_SLOT), None, ALU.add))
            link(dve.tensor_tensor(far, far, valid, ALU.mult))
            link(dve.tensor_scalar(far, far, float(FAR_SLOT), None, ALU.add))
            dve.tensor_copy(to_slot, far).then_inc(sem["routed"], 1)
            for k in range(TOPK):
                link(dve.tensor_tensor(weight[:, k, :], top8[:, :, k], pair_r, ALU.mult))
            link(dve.tensor_tensor(weight.rearrange("p k i -> p (k i)"), weight.rearrange("p k i -> p (k i)"),
                                   valid, ALU.mult))

            def lows(e, place, raw, hi, lo, name):
                par = place % 2
                for k in range(KD):
                    dve.wait_ge(sem[name + "_hi"], KD * (HCHUNKS * e + place) + k + 1)
                    dve.scalar_tensor_tensor(out=lo[:, par * KD + k, :], in0=raw[:, par, k, :], scalar=W_SCALE,
                                             in1=hi[:, par * KD + k, :], op0=ALU.mult, op1=ALU.subtract)\
                       .then_inc(sem[name + "_lo"], 1)

            def de_low(e):
                for a in range(CAP_TILES):
                    dve.wait_ge(sem["de_hi"], CAP_TILES * e + a + 1)
                    dve.tensor_tensor(de_lo[:, :, a * P:(a + 1) * P], tp[2 + a][:, :, :],
                                      de_hi[:, :, a * P:(a + 1) * P], ALU.subtract).then_inc(sem["de_lo"], 1)

            def result(e):
                dve.wait_ge(sem["fc2"], HCHUNKS * (e + 1))
                dve.wait_ge(sem["b2_in"], 16 * (e + 1))
                wait(dve, sem["eo_out"], 16 * e)
                for a in range(CAP_TILES):
                    dve.scalar_tensor_tensor(out=eo[:, a, :], in0=bank[4 + a][:, :], scalar=1 / W_SCALE,
                                             in1=b2, op0=ALU.mult, op1=ALU.add).then_inc(sem["eo"], 1)

            def slot(e, c):
                if c % HCHUNKS == 0 and (not isinstance(e, int) or e + c // HCHUNKS > 0):
                    result(e + c // HCHUNKS - 1)
                if within(e, c + 2):
                    lows(e, c + 2, raw_t, t_hi, t_lo, "t")
                if within(e, c + 1):
                    lows(e, c + 1, raw_n, n_hi, n_lo, "n")
                if c == 2 and (not isinstance(e, int) or e < EXPERTS - 1):
                    de_low(e + 1)
                if within(e, c + 1):
                    u = HCHUNKS * e + c + 1
                    par = (c + 1) % 2
                    dve.wait_ge(sem["h_hi"], u + 1)
                    dve.tensor_tensor(h_lo[:, par * HT:(par + 1) * HT, :].rearrange("p a c -> p (a c)"),
                                      hidden[:, par, :],
                                      h_hi[:, par * HT:(par + 1) * HT, :].rearrange("p a c -> p (a c)"),
                                      ALU.subtract).then_inc(sem["h_lo"], 1)
            lows(0, 0, raw_t, t_hi, t_lo, "t")
            de_low(0)
            steps(dve, slot)
            for i in range(TILES):
                for k in range(TOPK):
                    n = k * TILES + i
                    dve.wait_ge(got_in[n], 16)
                    if k:
                        dve.wait_ge(sem["half"], i + 1)
                    dve.scalar_tensor_tensor(out=X[:, i, :], in0=got[:, n, :], scalar=weight[:, k, i:i + 1],
                                             in1=X[:, i, :], op0=ALU.mult, op1=ALU.add)\
                       .then_inc(sem[("half", "sum")[k]], 1)

        @block.tensor
        def _(pe):
            norm_tensor(pe, s, tp, sem)
            pe.wait_ge(sem["gw_lo"], 1)
            for i in range(TILES):
                pe.wait_ge(sem["xt_lo"], i + 1)
                for k in range(KD):
                    last = three(pe, bank[2][:, i * EXPERTS:(i + 1) * EXPERTS], xt_hi[:, k, i * P:(i + 1) * P],
                                 xt_lo[:, k, i * P:(i + 1) * P], gw_hi[:, k, :], gw_lo[:, k, :],
                                 k == 0, k == KD - 1)
            last.then_inc(sem["logit_psum"], 1)
            pe.wait_ge(sem["chosen"], 1)
            pe.wait_ge(sem["before_in"], 16)
            pe.wait_ge(sem["ones"], 1)
            pe.matmul(bank[3][:, 0:PICKS * EXPERTS], before, chosen_h.rearrange("p n e -> p (n e)"),
                      start=True, stop=False)
            for n in range(PICKS - 1):
                last = pe.matmul(bank[3][:, (n + 1) * EXPERTS:PICKS * EXPERTS], ones,
                                 chosen_h[:, n:n + 1, :].to_broadcast([P, PICKS - 1 - n, EXPERTS]),
                                 start=False, stop=(n == PICKS - 2))
            last.then_inc(sem["loc_psum"], 1)

            def turn(e):
                pe.wait_ge(sem["de_in"], 16 * (e + 1))
                wait(pe, sem["de_lo"], CAP_TILES * e)
                for a in range(CAP_TILES):
                    for k in range(KD):
                        last = pe.transpose(tp[2 + a][:, k, :], de[:, a, k * P:(k + 1) * P], s["ident"][:, :])
                    last.then_inc(sem["de_tp"], 1)

            def fc1(e, place):
                u = HCHUNKS * e + place
                par = place % 2
                pe.wait_ge(sem["t_lo"], KD * (u + 1))
                if place % HCHUNKS == 0:
                    pe.wait_ge(sem["de_lo"], CAP_TILES * (e + place // HCHUNKS + 1))
                wait(pe, sem["relu"], HT * u)
                for h in range(HT):
                    for k in range(KD):
                        last = three(pe, bank[h // 2][:, h % 2 * CAP:(h % 2 + 1) * CAP],
                                     t_hi[:, par * KD + k, h * P:(h + 1) * P],
                                     t_lo[:, par * KD + k, h * P:(h + 1) * P], de_hi[:, k, :], de_lo[:, k, :],
                                     k == 0, k == KD - 1)
                    if h % 2:
                        last.then_inc(sem["fc1"], 1)

            def fc2(e, place):
                u = HCHUNKS * e + place
                par = place % 2
                pe.wait_ge(sem["n_lo"], HT * (u + 1))
                pe.wait_ge(sem["h_lo"], u + 1)
                if place % HCHUNKS == 0:
                    wait(pe, sem["eo"], CAP_TILES * (e + place // HCHUNKS))
                for a in range(CAP_TILES):
                    for h in range(HT):
                        last = three(pe, bank[4 + a][:, :], h_hi[:, par * HT + h, a * P:(a + 1) * P],
                                     h_lo[:, par * HT + h, a * P:(a + 1) * P], n_hi[:, par * HT + h, :],
                                     n_lo[:, par * HT + h, :], place % HCHUNKS == 0 and h == 0,
                                     place % HCHUNKS == HCHUNKS - 1 and h == HT - 1)
                last.then_inc(sem["fc2"], 1)

            def slot(e, c):
                if within(e, c + 1):
                    fc1(e, c + 1)
                if c == 2 and (not isinstance(e, int) or e < EXPERTS - 1):
                    turn(e + 1)
                if within(e, c):
                    fc2(e, c)
            turn(0)
            steps(pe, slot)


def _tables():
    f = np.float32
    inv = (1.0 / f(10000.0) ** (np.arange(0, HEAD, 2, dtype=f) / f(HEAD))).astype(f)
    pos = np.arange(SEQ, dtype=f)
    freqs = np.repeat(pos[:, None] * inv[None, :], 2, axis=-1).astype(f)
    base = ((np.arange(0, HEAD, 2, dtype=f) + f(0.4 * HEAD)) / f(1.4 * HEAD)).astype(f)
    power = (pos - SEQ // 2) / f(512.0)
    scale = np.repeat(base[None, :] ** power[:, None], 2, axis=-1).astype(f)
    cos, sin = np.cos(freqs), np.sin(freqs)
    sign = np.where(np.arange(HEAD) % 2 == 0, -1.0, 1.0).astype(f)
    gamma = (1.0 - 2.0 ** (-5.0 - np.arange(HEADS))).astype(np.float64)
    norm = 1 / np.sqrt(np.cumsum(gamma[None, :] ** np.arange(SEQ)[:, None], axis=0))
    q_cos = (cos * scale)[:, None, :] * norm[:, :, None]
    q_sin = (sin * scale * sign)[:, None, :] * norm[:, :, None]
    k_cos, k_sin = (np.tile(a, (1, HEADS)) for a in (cos / scale, sin / scale * sign))

    def tiles(a):
        return np.ascontiguousarray(a.reshape(SEQ_TILES, P, -1).transpose(1, 0, 2), dtype=f)
    back = np.arange(SEQ)[None, :] - np.arange(P)[:, None]
    decay = np.where(back >= 0, gamma[:, None, None] ** np.maximum(back, 0), 0.0)
    decay = decay.reshape(GROUPS, GH, P, SEQ).transpose(0, 2, 1, 3)
    return tiles(q_cos), tiles(q_sin), tiles(k_cos), tiles(k_sin), np.ascontiguousarray(decay, dtype=f)


def kernel(x, ctx_1024, L0_xattn_W, L0_xattn_b, L0_attn_Wq, L0_attn_bq, L0_attn_Wk, L0_attn_bk, L0_attn_Wv,
           L0_attn_bv, L0_attn_Wg, L0_attn_bg, L0_attn_Wo, L0_attn_bo, L0_attn_gn_w, L0_attn_gn_b,
           L0_ffn_gate_w, L0_ffn_fc1_w, L0_ffn_fc1_b, L0_ffn_fc2_w, L0_ffn_fc2_b):
    import concourse.bacc as bacc
    from concourse.bass_utils import run_bass_kernel_spmd

    def rows(a):
        a = np.asarray(a)
        return a.reshape(-1, P, a.shape[-1]).transpose(1, 0, 2)

    def cols(a):
        return np.asarray(a).reshape(-1, P).T

    ctx = np.asarray(ctx_1024).reshape(BATCH * CHUNKS, CHUNK, KD, P)
    fc1 = np.asarray(L0_ffn_fc1_w).reshape(EXPERTS * HCHUNKS, HCHUNK, KD, P)
    fc2 = np.asarray(L0_ffn_fc2_w).reshape(EXPERTS * HCHUNKS, HT, P, D)
    q_cos, q_sin, k_cos, k_sin, decay = _tables()
    lane = np.arange(P)
    heads = lambda a: np.repeat(np.asarray(a).reshape(GROUPS, GH), HEAD, axis=1).T
    arrays = {
        "x": rows(np.asarray(x).reshape(TOK, D)),
        "ident": np.eye(P, dtype=np.float32),
        "wxt": rows(np.asarray(L0_xattn_W).T),
        "wxn": rows(L0_xattn_W),
        "xb": cols(L0_xattn_b),
        "ctx_t": ctx.transpose(0, 3, 2, 1),
        "ctx_n": ctx.reshape(BATCH * CHUNKS, CHUNK // P, P, D).transpose(0, 2, 1, 3),
        "w5": np.stack([rows(w) for w in (L0_attn_Wq, L0_attn_Wk, L0_attn_Wv, L0_attn_Wg, L0_attn_Wo)]),
        "bias_rows": np.broadcast_to(np.stack([np.asarray(b) for b in (L0_attn_bq, L0_attn_bk, L0_attn_bv,
                                                                       L0_attn_bo)]), (P, 4, D)),
        "bg": cols(L0_attn_bg),
        "gn_w": heads(L0_attn_gn_w),
        "gn_b": heads(L0_attn_gn_b),
        "same_head": (lane[:, None] // HEAD == lane[None, :] // HEAD).astype(np.float32) / HEAD,
        "q_cos": q_cos, "q_sin": q_sin, "k_cos": k_cos, "k_sin": k_sin,
        "decay": decay,
        "gate_w": rows(np.asarray(L0_ffn_gate_w).T),
        "fc1": fc1.transpose(0, 3, 2, 1),
        "fc2": fc2.transpose(0, 2, 1, 3),
        "fc1_b": np.asarray(L0_ffn_fc1_b).reshape(EXPERTS, HID // P, P).transpose(0, 2, 1),
        "fc2_b": np.broadcast_to(np.asarray(L0_ffn_fc2_b), (EXPERTS, P, D)),
        "expert_no": np.broadcast_to(np.arange(EXPERTS, dtype=np.float32), (P, EXPERTS)),
        "before": (lane[:, None] < lane[None, :]).astype(np.float16),
    }
    nc = bacc.Bacc("TRN2", target_bir_lowering=False, num_devices=1)
    arrays = {n: np.ascontiguousarray(a) for n, a in arrays.items()}
    t = {n: nc.dram_tensor(n, a.shape, mybir.dt.from_np(a.dtype), kind="ExternalInput").ap()
         for n, a in arrays.items()}
    t["out"] = nc.dram_tensor("out", (P, TILES, D), F32, kind="ExternalOutput").ap()
    perceiver_layer(nc, t)
    got = run_bass_kernel_spmd(nc, [arrays], core_ids=[0]).results[0]["out"]
    return np.ascontiguousarray(got.transpose(1, 0, 2)).reshape(BATCH, SEQ, D)
```

```python
from contextlib import ExitStack

import numpy as np

import concourse.bass as bass
from concourse import mybir

F32 = mybir.dt.float32
F16 = mybir.dt.float16
U32 = mybir.dt.uint32
I32 = mybir.dt.int32
ALU = mybir.AluOpType
ACT = mybir.ActivationFunctionType
AX = mybir.AxisListType.X

P = 128
BATCH, SEQ, D = 2, 512, 512
CTX = 8192
TOK = BATCH * SEQ
TILES = TOK // P
SEQ_TILES = SEQ // P
KD = D // P
CHUNK = 512
CHUNKS = CTX // CHUNK
HEADS, HEAD = 16, 32
GROUPS = HEADS * HEAD // P
GH = P // HEAD
EXPERTS, TOPK, HID = 8, 2, 2048
CAP = TOPK * (TOK // EXPERTS)
CAP_TILES = CAP // P
HCHUNK = 512
HCHUNKS = HID // HCHUNK
HT = HCHUNK // P
EPS = 1e-5
W_SCALE = 64.0
P_SCALE = 4096.0
Q_SCALE = 64.0
FAR = -1e30
N_W = 5
GATED_AT = {SEQ_TILES + 1: ((0, 0), (0, 1)), SEQ_TILES + 2: ((0, 2), (0, 3))}


class Arena:

    def __init__(self, tensor, words):
        self.tensor, self.words, self.at = tensor, words, 0

    def take(self, shape, dtype=F32):
        n = int(np.prod(shape))
        words = n if dtype != F16 else n // 2
        view = self.tensor[:, self.at:self.at + words]
        self.at += words
        assert self.at <= self.words, (self.at, self.words)
        if dtype != F32:
            view = view.bitcast(dtype)
        if len(shape) == 2:
            return view.rearrange("p (a b) -> p a b", a=shape[0])
        if len(shape) == 3:
            return view.rearrange("p (a b c) -> p a b c", a=shape[0], b=shape[1])
        return view


def three(pe, out, left_hi, left_lo, right_hi, right_lo, first, last):
    pe.matmul(out, left_hi, right_hi, start=first, stop=False)
    pe.matmul(out, left_hi, right_lo, start=False, stop=False)
    return pe.matmul(out, left_lo, right_hi, start=False, stop=last)


def perceiver_layer(nc, t):
    ARENA = 29 * 1024
    with ExitStack() as top:
        def sb(name, shape, dtype=F32):
            return top.enter_context(nc.sbuf_tensor(name + "_sb", shape, dtype))

        X = sb("X", [P, TILES, D])
        XN = sb("XN", [P, TILES, D])
        xt_hi = sb("xt_hi", [P, KD, TOK], F16)
        xt_lo = sb("xt_lo", [P, KD, TOK], F16)
        w_hi = sb("w_hi", [P, N_W, KD, D], F16)
        w_lo = sb("w_lo", [P, N_W, KD, D], F16)
        ident = sb("ident", [P, P])
        stats = sb("stats", [P, TILES, 6])
        mv = sb("mv", [P, TILES, 2])
        var = sb("var", [P, TILES])
        std = sb("std", [P, TILES])
        rstd = sb("rstd", [P, TILES])
        arena_t = sb("arena", [P, ARENA])
        banks = [top.enter_context(nc.psum_tensor(f"bank{i}", [P, 512], F32)) for i in range(8)]
        disp = nc.dram_tensor("disp", (EXPERTS * CAP, D), F32, kind="Internal").ap()
        eo_d = nc.dram_tensor("expert_out", (EXPERTS * CAP, D), F32, kind="Internal").ap()

        shared = dict(X=X, XN=XN, xt_hi=xt_hi, xt_lo=xt_lo, w_hi=w_hi, w_lo=w_lo, ident=ident,
                      stats=stats, mv=mv, var=var, std=std, rstd=rstd, banks=banks,
                      disp=disp, eo_d=eo_d)
        used = cross_attention(nc, t, shared, Arena(arena_t, ARENA))
        nc.clear_and_free_semaphores(list(used.values()))
        nc.all_engine_barrier()
        used = retention(nc, t, shared, Arena(arena_t, ARENA))
        nc.clear_and_free_semaphores(list(used.values()))
        nc.all_engine_barrier()
        experts(nc, t, shared, Arena(arena_t, ARENA))


def wait(engine, sem, value):
    if not isinstance(value, int) or value > 0:
        engine.wait_ge(sem, value)


def norm_vector(dve, s, m, sem):
    X, XN, stats, mv, var, rstd = s["X"], s["XN"], s["stats"], s["mv"], s["var"], s["rstd"]
    for i in range(TILES):
        dve.bn_stats(stats[:, i, :], X[:, i, :]).then_inc(sem["ln_stats"], 1)
    for i in range(TILES):
        dve.wait_ge(sem["ln_stats"], i + 1)
        dve.bn_aggr(mv[:, i, :], stats[:, i, :]).then_inc(sem["ln_aggr"], 1)
    dve.wait_ge(sem["ln_aggr"], TILES)
    dve.tensor_scalar(var[:, :], mv[:, :, 1], EPS, None, ALU.add).then_inc(sem["ln_var"], 1)
    dve.wait_ge(sem["ln_std"], 1)
    dve.reciprocal(rstd[:, :], s["std"][:, :]).then_inc(sem["ln_rstd"], 1)
    dve.wait_ge(sem["ln_rstd"], 1)

    def low(i):
        dve.wait_ge(sem["xt_hi"], i + 1)
        dve.tensor_tensor(s["xt_lo"][:, :, i * P:(i + 1) * P], m[i % 2][:, :, :],
                          s["xt_hi"][:, :, i * P:(i + 1) * P], ALU.subtract).then_inc(sem["xt_lo"], 1)
    for i in range(TILES):
        dve.tensor_scalar(XN[:, i, :], X[:, i, :], mv[:, i, 0:1], rstd[:, i:i + 1],
                          ALU.subtract, ALU.mult).then_inc(sem["xn"], 1)
        if i >= 2:
            low(i - 2)
    low(TILES - 2)
    low(TILES - 1)


def norm_scalar(act, s, m, sem):
    act.wait_ge(sem["ln_var"], 1)
    act.activation(s["std"][:, :], s["var"][:, :], ACT.Sqrt).then_inc(sem["ln_std"], 1)
    for i in range(TILES):
        act.wait_ge(sem["xt_psum"], i + 1)
        act.activation(s["xt_hi"][:, :, i * P:(i + 1) * P], m[i % 2][:, :, :], ACT.Copy)\
           .then_inc(sem["xt_hi"], 1)


def norm_tensor(pe, s, m, sem, tiles=range(TILES)):
    for i in tiles:
        pe.wait_ge(sem["xn"], i + 1)
        if i >= 2:
            pe.wait_ge(sem["xt_lo"], i - 1)
        for k in range(KD):
            last = pe.transpose(m[i % 2][:, k, :], s["XN"][:, i, k * P:(k + 1) * P], s["ident"][:, :])
        last.then_inc(sem["xt_psum"], 1)


def semaphores(nc, prefix, names):
    return {n: nc.alloc_semaphore(prefix + n) for n in names}


NORM_SEMS = ["ln_stats", "ln_aggr", "ln_var", "ln_std", "ln_rstd", "xn", "xt_psum", "xt_hi", "xt_lo"]


def cross_attention(nc, t, s, arena):
    X, XN, xt_hi, xt_lo = s["X"], s["XN"], s["xt_hi"], s["xt_lo"]
    LT = SEQ_TILES
    raw_w = arena.take([2, KD, D])
    qt_hi = arena.take([KD, TOK], F16)
    qt_lo = arena.take([KD, TOK], F16)
    ctx_t = arena.take([2, KD, CHUNK])
    ctx_n = arena.take([2, KD, D])
    t_hi, t_lo, n_hi, n_lo = (arena.take([2 * KD, CHUNK], F16) for _ in range(4))
    at_pt = arena.at
    prob = arena.take([2, CHUNK])
    pt_hi = arena.take([2 * 4, P], F16)
    pt_lo = arena.take([2 * 4, P], F16)
    again = Arena(arena.tensor, arena.words)
    again.at = at_pt
    ext_hi = again.take([KD, SEQ], F16)
    ext_lo = again.take([KD, SEQ], F16)
    arena.at = max(arena.at, again.at)
    ext = arena.take([2, SEQ])
    xb = arena.take([KD])
    xb_cols = arena.take([KD])
    xb_hi = arena.take([KD], F16)
    xb_lo = arena.take([KD], F16)
    ex_b = arena.take([TILES])
    ms = [arena.take([TILES]) for _ in range(2)]
    cmax, nbias, drop, alpha, rows = (arena.take([4]) for _ in range(5))
    total = arena.take([TILES])
    recip, recip_s = arena.take([TILES]), arena.take([TILES])
    acc = XN
    bank = s["banks"]
    tp = [bank[i][:, :].rearrange("p (k n) -> p k n", k=KD) for i in range(8)]

    PAIR = 2 * LT
    PAIRS = BATCH * CHUNKS // 2
    UNITS = PAIR * PAIRS

    def within(i, place, count=UNITS, step=PAIR):
        return not isinstance(i, int) or 0 <= step * i + place < count

    def cell(i, place):
        c = (i + place // PAIR) // (CHUNKS // 2) * LT + place % LT
        return slice(c, c + 1) if isinstance(c, int) else bass.ds(c, 1)

    def tile(i, place):
        c = (i + place // PAIR) // (CHUNKS // 2) * LT + place % LT
        return c if isinstance(c, int) else bass.ds(c, 1)

    def queries(i, place):
        c = (i + place // PAIR) // (CHUNKS // 2) * LT + place % LT
        return slice(c * P, c * P + P) if isinstance(c, int) else bass.ds(c * P, P)

    def steps(engine, slot):
        for j in range(-2, PAIR):
            slot(0, j)
        with engine.Fori(1, PAIRS - 1) as i:
            for j in range(PAIR):
                slot(i, j)
        for j in range(PAIR + 1):
            slot(PAIRS - 1, j)

    def split_piece(i, place):
        ahead = place // LT + 1
        return ahead % 2, place % LT, (2 * i + ahead) * KD + place % LT, i + ahead // 2

    with ExitStack() as ctx:
        names = NORM_SEMS + [
            "x_in", "wxt_in", "wxn_in", "xb_in", "ident_in", "raw_in0", "raw_in1",
            "wx_hi", "wx_lo", "xb_s", "xb_h", "xb_l", "ex_psum", "ex", "ex_hi", "ex_lo",
            "q_psum", "q_hi", "q_lo", "exb_psum", "exb", "init", "w_s", "w_h", "w_l",
            "ct_in0", "ct_in1", "cn_in0", "cn_in1", "ct_hi", "ct_lo", "cn_hi", "cn_lo",
            "score", "cmax", "mnew", "nbias", "drop", "alpha", "prob", "pt_psum", "pt_hi", "pt_lo",
            "av", "acc", "total", "recip", "recip_s", "x1"]
        sem = semaphores(nc, "a_", names)
        block = ctx.enter_context(nc.Block())

        @block.sync
        def _(sp):
            sp.dma_start(X[:, :, :], t["x"]).then_inc(sem["x_in"], 16)
            sp.dma_start(s["ident"][:, :], t["ident"]).then_inc(sem["ident_in"], 16)
            sp.dma_start(raw_w[:, 0, :, :], t["wxt"]).then_inc(sem["wxt_in"], 16)
            sp.dma_start(raw_w[:, 1, :, :], t["wxn"]).then_inc(sem["wxn_in"], 16)
            sp.dma_start(xb[:, :], t["xb"]).then_inc(sem["xb_in"], 16)

            def rows(name, i):
                if isinstance(i, int):
                    return t[name][i]
                return t[name][bass.ds(i, 1), :, :, :].rearrange("a p k m -> (a p) k m")

            def chunk(i, parity):
                sp.dma_start(ctx_t[:, parity, :, :], rows("ctx_t", i)).then_inc(sem[f"ct_in{parity}"], 16)
                sp.dma_start(ctx_n[:, parity, :, :], rows("ctx_n", i)).then_inc(sem[f"cn_in{parity}"], 16)
            chunk(0, 0)
            chunk(1, 1)
            for n in range(N_W):
                if n < 2:
                    sp.wait_ge(sem["wx_lo"], KD * (n + 1))
                else:
                    sp.wait_ge(sem["w_l"], n - 1)
                sp.dma_start(raw_w[:, n % 2, :, :], t["w5"][n]).then_inc(sem[f"raw_in{n % 2}"], 16)
            with sp.Fori(1, PAIRS) as i:
                for parity in range(2):
                    for part in ("ct_hi", "ct_lo", "cn_hi", "cn_lo"):
                        sp.wait_ge(sem[part], (2 * i + parity - 1) * KD)
                    chunk(2 * i + parity, parity)

        @block.gpsimd
        def _(pool):
            for n in range(N_W):
                if n == 3:
                    pool.wait_ge(sem["exb_psum"], BATCH)
                raw = raw_w[:, n % 2, :, :]
                pool.wait_ge(sem[f"raw_in{n % 2}"], 16 * (n // 2 + 1))
                pool.tensor_scalar(raw, raw, W_SCALE, None, ALU.mult).then_inc(sem["w_s"], 1)
                pool.wait_ge(sem["w_s"], n + 1)
                pool.tensor_copy(s["w_hi"][:, n, :, :], raw).then_inc(sem["w_h"], 1)
                pool.wait_ge(sem["w_h"], n + 1)
                pool.tensor_tensor(s["w_lo"][:, n, :, :], raw, s["w_hi"][:, n, :, :], ALU.subtract)\
                    .then_inc(sem["w_l"], 1)

        @block.scalar
        def _(act):
            for n, name in enumerate(("wxt_in", "wxn_in")):
                act.wait_ge(sem[name], 16)
                for k in range(KD):
                    act.activation(s["w_hi"][:, 3 + n, k, :], raw_w[:, n, k, :], ACT.Copy, scale=W_SCALE)\
                       .then_inc(sem["wx_hi"], 1)
            act.wait_ge(sem["xb_in"], 16)
            act.activation(xb_cols[:, :], xb[:, :], ACT.Copy, scale=W_SCALE).then_inc(sem["xb_s"], 1)
            act.wait_ge(sem["xb_s"], 1)
            act.activation(xb_hi[:, :], xb_cols[:, :], ACT.Copy).then_inc(sem["xb_h"], 1)
            norm_scalar(act, s, tp, sem)
            for b in range(BATCH):
                for e in range(KD):
                    n = b * KD + e
                    act.wait_ge(sem["ex_psum"], n + 1)
                    wait(act, sem["ex_lo"], n - 1)
                    act.activation(ext[:, n % 2, :], bank[2 + n % 2][:, :], ACT.Identity,
                                   bias=xb[:, e:e + 1], scale=1 / W_SCALE).then_inc(sem["ex"], 1)
                    act.wait_ge(sem["ex"], n + 1)
                    if b and e == 0:
                        act.wait_ge(sem["exb_psum"], b)
                    act.activation(ext_hi[:, e, :], ext[:, n % 2, :], ACT.Copy).then_inc(sem["ex_hi"], 1)
                for d in range(KD):
                    n = b * KD + d
                    act.wait_ge(sem["q_psum"], n + 1)
                    act.activation(qt_hi[:, d, b * SEQ:(b + 1) * SEQ], bank[4 + n % 2][:, :], ACT.Copy,
                                   scale=1 / W_SCALE).then_inc(sem["q_hi"], 1)
            act.wait_ge(sem["init"], 3)

            def t_high(parity, k, count, pair):
                if k == 0:
                    act.wait_ge(sem[f"ct_in{parity}"], 16 * (pair + 1))
                if k == 0:
                    wait(act, sem["score"], count - KD)
                act.activation(t_hi[:, parity * KD + k, :], ctx_t[:, parity, k, :], ACT.Copy)\
                   .then_inc(sem["ct_hi"], 1)

            def n_high(parity, k, count, pair):
                if k == 0:
                    act.wait_ge(sem[f"cn_in{parity}"], 16 * (pair + 1))
                    wait(act, sem["av"], count - KD)
                act.activation(n_hi[:, parity * KD + k, :], ctx_n[:, parity, k, :], ACT.Copy)\
                   .then_inc(sem["cn_hi"], 1)

            def slot(i, j):
                if within(i, j + 2 + LT):
                    t_high(*split_piece(i, j + 2))
                if within(i, j) and within(i, j + LT):
                    n_high(*split_piece(i, j))
                v = PAIR * i + j + 1
                if within(i, j + 1):
                    m = (j + 1) % 2
                    act.wait_ge(sem["pt_psum"], v + 1)
                    wait(act, sem["av"], v - 1)
                    act.activation(pt_hi[:, 4 * m:4 * m + 4, :], tp[2 + m][:, :, :], ACT.Copy,
                                   scale=P_SCALE).then_inc(sem["pt_hi"], 1)
                v = PAIR * i + j + 2
                if within(i, j + 2):
                    m, q, new = (j + 2) % 2, (j + 2) % 4, (j + 2) // LT % 2
                    act.wait_ge(sem["drop"], v + 1)
                    wait(act, sem["acc"], v - 3)
                    wait(act, sem["total"], v - 3)
                    act.activation(alpha[:, q:q + 1], drop[:, q:q + 1], ACT.Exp).then_inc(sem["alpha"], 1)
                    act.wait_ge(sem["nbias"], v + 1)
                    wait(act, sem["pt_psum"], v - 1)
                    act.activation(prob[:, m, :], bank[m][:, :], ACT.Exp, bias=nbias[:, q:q + 1],
                                   accum_out=rows[:, q:q + 1]).then_inc(sem["prob"], 1)
            for k in range(KD):
                t_high(0, k, k, 0)
            for k in range(KD):
                n_high(0, k, k, 0)
            steps(act, slot)

        @block.vector
        def _(dve):
            dve.wait_ge(sem["x_in"], 16)
            norm_vector(dve, s, tp, sem)
            for n in range(2):
                for k in range(KD):
                    dve.wait_ge(sem["wx_hi"], n * KD + k + 1)
                    dve.scalar_tensor_tensor(out=s["w_lo"][:, 3 + n, k, :], in0=raw_w[:, n, k, :],
                                             scalar=W_SCALE, in1=s["w_hi"][:, 3 + n, k, :],
                                             op0=ALU.mult, op1=ALU.subtract).then_inc(sem["wx_lo"], 1)
            dve.wait_ge(sem["xb_h"], 1)
            dve.tensor_tensor(xb_lo[:, :], xb_cols[:, :], xb_hi[:, :], ALU.subtract).then_inc(sem["xb_l"], 1)
            dve.memset(total[:, :], 0.0).then_inc(sem["init"], 1)
            dve.memset(ms[1][:, :], FAR).then_inc(sem["init"], 1)
            dve.wait_ge(sem["xt_psum"], TILES)
            dve.memset(acc[:, :, :], 0.0).then_inc(sem["init"], 1)
            for b in range(BATCH):
                for e in range(KD):
                    n = b * KD + e
                    dve.wait_ge(sem["ex_hi"], n + 1)
                    dve.tensor_tensor(ext_lo[:, e, :], ext[:, n % 2, :], ext_hi[:, e, :], ALU.subtract)\
                       .then_inc(sem["ex_lo"], 1)
                for d in range(KD):
                    n = b * KD + d
                    dve.wait_ge(sem["q_hi"], n + 1)
                    dve.scalar_tensor_tensor(out=qt_lo[:, d, b * SEQ:(b + 1) * SEQ], in0=bank[4 + n % 2][:, :],
                                             scalar=1 / W_SCALE, in1=qt_hi[:, d, b * SEQ:(b + 1) * SEQ],
                                             op0=ALU.mult, op1=ALU.subtract).then_inc(sem["q_lo"], 1)
                dve.wait_ge(sem["exb_psum"], b + 1)
                dve.tensor_scalar(ex_b[:, b * LT:(b + 1) * LT], bank[6][:, b * LT:(b + 1) * LT],
                                  1 / W_SCALE, None, ALU.mult).then_inc(sem["exb"], 1)
            dve.wait_ge(sem["init"], 3)
            dve.wait_ge(sem["exb"], BATCH)

            def t_low(parity, k, count, pair):
                dve.wait_ge(sem["ct_hi"], count + 1)
                dve.tensor_tensor(t_lo[:, parity * KD + k, :], ctx_t[:, parity, k, :],
                                  t_hi[:, parity * KD + k, :], ALU.subtract).then_inc(sem["ct_lo"], 1)

            def n_low(parity, k, count, pair):
                dve.wait_ge(sem["cn_hi"], count + 1)
                dve.tensor_tensor(n_lo[:, parity * KD + k, :], ctx_n[:, parity, k, :],
                                  n_hi[:, parity * KD + k, :], ALU.subtract).then_inc(sem["cn_lo"], 1)

            def slot(i, j):
                v = PAIR * i + j - 1
                if within(i, j - 1):
                    m, q = (j - 1) % 2, (j - 1) % 4
                    dve.wait_ge(sem["av"], v + 1)
                    wait(dve, sem["acc"], v - 3)
                    here = tile(i, j - 1)
                    sums = acc[:, here, :] if isinstance(here, int) else \
                        acc[:, here, :].rearrange("p a d -> p (a d)")
                    dve.scalar_tensor_tensor(out=sums, in0=sums, scalar=alpha[:, q:q + 1],
                                             in1=bank[4 + m][:, :], op0=ALU.mult, op1=ALU.add)\
                       .then_inc(sem["acc"], 1)
                    wait(dve, sem["total"], v - 3)
                    c = cell(i, j - 1)
                    dve.scalar_tensor_tensor(out=total[:, c], in0=total[:, c], scalar=alpha[:, q:q + 1],
                                             in1=rows[:, q:q + 1], op0=ALU.mult, op1=ALU.add)\
                       .then_inc(sem["total"], 1)
                if within(i, j + 2 + LT):
                    t_low(*split_piece(i, j + 2))
                if within(i, j) and within(i, j + LT):
                    n_low(*split_piece(i, j))
                v = PAIR * i + j + 2
                if within(i, j + 2):
                    m, q, new = (j + 2) % 2, (j + 2) % 4, (j + 2) // LT % 2
                    c = cell(i, j + 2)
                    dve.wait_ge(sem["score"], v + 1)
                    dve.reduce_max(cmax[:, q:q + 1], bank[m][:, :], AX).then_inc(sem["cmax"], 1)
                    dve.wait_ge(sem["cmax"], v + 1)
                    dve.tensor_scalar(ms[new][:, c], cmax[:, q:q + 1], ex_b[:, c], ms[1 - new][:, c],
                                      ALU.add, ALU.max).then_inc(sem["mnew"], 1)
                    dve.wait_ge(sem["mnew"], v + 1)
                    dve.tensor_tensor(nbias[:, q:q + 1], ex_b[:, c], ms[new][:, c], ALU.subtract)\
                       .then_inc(sem["nbias"], 1)
                    wait(dve, sem["alpha"], v - 3)
                    dve.tensor_tensor(drop[:, q:q + 1], ms[1 - new][:, c], ms[new][:, c], ALU.subtract)\
                       .then_inc(sem["drop"], 1)
                v = PAIR * i + j + 1
                if within(i, j + 1):
                    m = (j + 1) % 2
                    dve.wait_ge(sem["pt_hi"], v + 1)
                    dve.scalar_tensor_tensor(out=pt_lo[:, 4 * m:4 * m + 4, :], in0=tp[2 + m][:, :, :],
                                             scalar=P_SCALE, in1=pt_hi[:, 4 * m:4 * m + 4, :],
                                             op0=ALU.mult, op1=ALU.subtract).then_inc(sem["pt_lo"], 1)
            for k in range(KD):
                t_low(0, k, k, 0)
            for k in range(KD):
                n_low(0, k, k, 0)
            steps(dve, slot)
            dve.wait_ge(sem["total"], UNITS)
            dve.reciprocal(recip[:, :], total[:, :]).then_inc(sem["recip"], 1)
            dve.wait_ge(sem["recip"], 1)
            dve.tensor_scalar(recip_s[:, :], recip[:, :], 1 / P_SCALE, None, ALU.mult)\
               .then_inc(sem["recip_s"], 1)
            dve.wait_ge(sem["recip_s"], 1)
            dve.wait_ge(sem["acc"], UNITS)
            for n in range(TILES):
                dve.scalar_tensor_tensor(out=X[:, n, :], in0=acc[:, n, :], scalar=recip_s[:, n:n + 1],
                                         in1=X[:, n, :], op0=ALU.mult, op1=ALU.add)\
                   .then_inc(sem["x1"], 1)

        @block.tensor
        def _(pe):
            pe.wait_ge(sem["ident_in"], 16)
            norm_tensor(pe, s, tp, sem)
            for b in range(BATCH):
                pe.wait_ge(sem["xt_lo"], SEQ_TILES * (b + 1))
                seq = slice(b * SEQ, (b + 1) * SEQ)
                for e in range(KD):
                    n = b * KD + e
                    pe.wait_ge(sem["wx_lo"], KD)
                    wait(pe, sem["ex"], n - 1)
                    for k in range(KD):
                        last = three(pe, bank[2 + n % 2][:, :], s["w_hi"][:, 3, k, e * P:(e + 1) * P],
                                     s["w_lo"][:, 3, k, e * P:(e + 1) * P], xt_hi[:, k, seq],
                                     xt_lo[:, k, seq], k == 0, k == KD - 1)
                    last.then_inc(sem["ex_psum"], 1)
                pe.wait_ge(sem["wx_lo"], 2 * KD)
                pe.wait_ge(sem["ex_lo"], KD * (b + 1))
                for d in range(KD):
                    n = b * KD + d
                    wait(pe, sem["q_lo"], n - 1)
                    for e in range(KD):
                        last = three(pe, bank[4 + n % 2][:, :], s["w_hi"][:, 4, e, d * P:(d + 1) * P],
                                     s["w_lo"][:, 4, e, d * P:(d + 1) * P], ext_hi[:, e, :],
                                     ext_lo[:, e, :], e == 0, e == KD - 1)
                    last.then_inc(sem["q_psum"], 1)
                pe.wait_ge(sem["xb_l"], 1)
                wait(pe, sem["exb"], b)
                for n in range(LT):
                    for e in range(KD):
                        last = three(pe, bank[6][:, b * LT + n:b * LT + n + 1],
                                     ext_hi[:, e, n * P:(n + 1) * P], ext_lo[:, e, n * P:(n + 1) * P],
                                     xb_hi[:, e:e + 1], xb_lo[:, e:e + 1], e == 0, e == KD - 1)
                last.then_inc(sem["exb_psum"], 1)
            pe.wait_ge(sem["q_lo"], BATCH * KD)

            def slot(i, j):
                v = PAIR * i + j + 2
                if within(i, j + 2):
                    m, par = (j + 2) % 2, (j + 2) // LT % 2
                    if j % LT == LT - 2:
                        pe.wait_ge(sem["ct_lo"], v + KD)
                    wait(pe, sem["prob"], v - 1)
                    q = queries(i, j + 2)
                    for k in range(KD):
                        last = three(pe, bank[m][:, :], qt_hi[:, k, q], qt_lo[:, k, q],
                                     t_hi[:, par * KD + k, :], t_lo[:, par * KD + k, :],
                                     k == 0, k == KD - 1)
                    last.then_inc(sem["score"], 1)
                v = PAIR * i + j + 1
                if within(i, j + 1):
                    m = (j + 1) % 2
                    pe.wait_ge(sem["prob"], v + 1)
                    wait(pe, sem["pt_lo"], v - 1)
                    for k in range(CHUNK // P):
                        last = pe.transpose(tp[2 + m][:, k, :], prob[:, m, k * P:(k + 1) * P],
                                            s["ident"][:, :])
                    last.then_inc(sem["pt_psum"], 1)
                v = PAIR * i + j
                if within(i, j):
                    m, par = j % 2, j // LT % 2
                    if j % LT == 0:
                        pe.wait_ge(sem["cn_lo"], v + KD)
                    pe.wait_ge(sem["pt_lo"], v + 1)
                    wait(pe, sem["acc"], v - 1)
                    for k in range(CHUNK // P):
                        last = three(pe, bank[4 + m][:, :], pt_hi[:, 4 * m + k, :], pt_lo[:, 4 * m + k, :],
                                     n_hi[:, par * KD + k, :], n_lo[:, par * KD + k, :],
                                     k == 0, k == CHUNK // P - 1)
                    last.then_inc(sem["av"], 1)
            steps(pe, slot)
    return sem


def retention(nc, t, s, arena):
    X, XN, xt_hi, xt_lo, w_hi, w_lo = (s[n] for n in ("X", "XN", "xt_hi", "xt_lo", "w_hi", "w_lo"))
    QT = SEQ_TILES
    HALVES = ("q", "k")
    cos = {h: arena.take([QT, D]) for h in HALVES}
    sin = {h: arena.take([QT, D]) for h in HALVES}
    bias = arena.take([3, D])
    gate = arena.take([BATCH * GROUPS, SEQ])
    bo = gate[:, BATCH * GROUPS - 1, :]
    qk_hi = {h: arena.take([2 * GROUPS, P], F16) for h in HALVES}
    qk_lo = {h: arena.take([2 * GROUPS, P], F16) for h in HALVES}
    v_hi, v_lo = arena.take([2, D], F16), arena.take([2, D], F16)
    kn_hi, kn_lo = arena.take([D], F16), arena.take([D], F16)
    masked = arena.take([GH, GROUPS * P])
    s_hi, s_lo = arena.take([GH, GROUPS * P], F16), arena.take([GH, GROUPS * P], F16)
    gated_hi = [arena.take([GROUPS, SEQ], F16), s_hi]
    gated_lo = [arena.take([GROUPS, SEQ], F16), s_lo]
    carry = arena.take([GROUPS, P])
    state = arena.take([GROUPS, P])
    grown = arena.take([GROUPS, P])
    st_hi, st_lo = arena.take([GROUPS, P], F16), arena.take([GROUPS, P], F16)
    causal = arena.take([P])
    bg, gn_w, gn_b = (arena.take([GROUPS]) for _ in range(3))
    same_head = arena.take([P])
    hstats = arena.take([GROUPS, 6])
    hmv = arena.take([GROUPS, 2])
    sums = arena.take([2, GROUPS])
    means = arena.take([2, GROUPS])
    sq, hvar, hstd, hrstd, gscale, gshift, tmp = (arena.take([GROUPS]) for _ in range(7))
    biased = {h: arena.take([D]) for h in ("q", "k", "v")}
    swapped = {h: arena.take([D]) for h in HALVES}
    turned = {h: arena.take([D]) for h in HALVES}
    ret = XN
    bank = s["banks"]
    tp = [bank[i][:, :].rearrange("p (k n) -> p k n", k=KD) for i in range(8)]
    QKV_BANK = {"q": 0, "k": 1, "v": 2}
    TURN_BANK = {"q": 3, "k": 4}
    SCORE_BANK = (3, 4, 5, 6)
    RET_BANK, STATE_BANK, HEAD_BANK = 7, 5, 2
    OUT_BANK = (0, 1, 3, 4, 5, 6, 0, 1)
    LAST = QT - 1

    def pairs(row):
        return row.rearrange("p (a two) -> p a two", two=2)

    def states(i):
        return i - i // QT

    with ExitStack() as ctx:
        names = NORM_SEMS + [f"{a}_{b}_in" for a in ("q", "k") for b in ("cos", "sin")] + [
            "bias_in", "bo_in", "bg_in", "gnw_in", "gnb_in", "same_in", "causal_in", "carry_in",
            "qkv", "q_b", "k_b", "v_b", "q_cos", "k_cos", "q_swap", "k_swap", "q_turn", "k_turn",
            "v_hi", "v_lo", "kn_hi", "kn_lo", "q_tp", "k_tp", "q_hi", "k_hi", "q_lo", "k_lo",
            "gate_psum", "gate", "score", "masked", "s_hi", "s_lo_dve", "s_lo_pool", "pv", "ret",
            "growth", "grown", "state", "st_hi", "st_lo", "hstats", "hmv",
            "sums", "head_psum", "small", "hvar", "hstd", "gn", "gated", "g_hi", "g_lo",
            "wo", "x_bo", "x2"]
        sem = semaphores(nc, "r_", names)
        block = ctx.enter_context(nc.Block())

        @block.sync
        def _(sp):
            sp.dma_start(bias, t["bias_rows"]).then_inc(sem["bias_in"], 16)
            for h in HALVES:
                sp.dma_start(cos[h], t[h + "_cos"]).then_inc(sem[f"{h}_cos_in"], 16)
                sp.dma_start(sin[h], t[h + "_sin"]).then_inc(sem[f"{h}_sin_in"], 16)
            sp.dma_start(causal, t["causal"]).then_inc(sem["causal_in"], 16)
            sp.dma_start(carry, t["carry"]).then_inc(sem["carry_in"], 16)
            sp.dma_start(bo, t["bo"]).then_inc(sem["bo_in"], 16)
            sp.dma_start(bg, t["bg"]).then_inc(sem["bg_in"], 16)
            sp.dma_start(gn_w, t["gn_w"]).then_inc(sem["gnw_in"], 16)
            sp.dma_start(gn_b, t["gn_b"]).then_inc(sem["gnb_in"], 16)
            sp.dma_start(same_head, t["same_head"]).then_inc(sem["same_in"], 16)

        @block.gpsimd
        def _(pool):
            def swap(i):
                for h in HALVES:
                    if i == 0:
                        pool.wait_ge(sem[f"{h}_sin_in"], 16)
                    pool.wait_ge(sem[f"{h}_b"], i + 1)
                    wait(pool, sem[f"{h}_turn"], i)
                    a, b, c = pairs(swapped[h]), pairs(biased[h]), pairs(sin[h][:, i % QT, :])
                    for o in range(2):
                        pool.tensor_tensor(a[:, :, o], b[:, :, 1 - o], c[:, :, o], ALU.mult)\
                            .then_inc(sem[f"{h}_swap"], 1)

            def low(i):
                wait(pool, sem["pv"], i)
                for j in range(2):
                    pool.wait_ge(sem["s_hi"], GH * i + j + 1)
                    pool.tensor_tensor(s_lo[:, j, :], masked[:, j, :], s_hi[:, j, :], ALU.subtract)\
                        .then_inc(sem["s_lo_pool"], 1)

            def decay(i):
                c = states(i)
                if i == 0:
                    pool.wait_ge(sem["carry_in"], 16)
                pool.wait_ge(sem["grown"], c + 1)
                wait(pool, sem["st_lo"], c)
                pool.tensor_tensor(state, grown, carry, ALU.mult).then_inc(sem["state"], 1)

            def out_bias(i):
                if i == 0:
                    pool.wait_ge(sem["bo_in"], 16)
                pool.wait_ge(sem["xn"], i + 1)
                pool.tensor_tensor(X[:, i, :], X[:, i, :], bo, ALU.add).then_inc(sem["x_bo"], 1)

            swap(0)
            for i in range(TILES):
                low(i)
                if i + 1 < TILES:
                    swap(i + 1)
                if i % QT < LAST:
                    decay(i)
                if i < TILES // 2:
                    out_bias(2 * i)
                    out_bias(2 * i + 1)

        @block.scalar
        def _(act):
            norm_scalar(act, s, tp[6:8], sem)

            def v_high(i):
                act.wait_ge(sem["v_b"], i + 1)
                wait(act, sem["pv"], i - 1)
                wait(act, sem["growth"], states(i - 1) if i else 0)
                act.activation(v_hi[:, i % 2, :], biased["v"], ACT.Copy).then_inc(sem["v_hi"], 1)

            def kn_high(i):
                if i % QT < LAST:
                    act.wait_ge(sem["k_turn"], i + 1)
                    wait(act, sem["growth"], states(i))
                    act.activation(kn_hi, turned["k"], ACT.Copy).then_inc(sem["kn_hi"], 1)

            def qk_high(i):
                par = i % 2 * GROUPS
                for h in HALVES:
                    act.wait_ge(sem[f"{h}_tp"], i + 1)
                    wait(act, sem["pv"], i - 1)
                    act.activation(qk_hi[h][:, par:par + GROUPS, :], tp[TURN_BANK[h]][:, :, :], ACT.Copy)\
                       .then_inc(sem[f"{h}_hi"], 1)

            def gates(i):
                if i == 0:
                    act.wait_ge(sem["bg_in"], 16)
                if i == TILES - 1:
                    act.wait_ge(sem["x_bo"], TILES)
                act.wait_ge(sem["gate_psum"], i + 1)
                act.activation(gate[:, i, :], bank[QKV_BANK["q"]][:, :], ACT.Silu,
                               bias=bg[:, i % GROUPS:i % GROUPS + 1], scale=1 / W_SCALE).then_inc(sem["gate"], 1)

            def result(i):
                act.wait_ge(sem["pv"], i + 1)
                if i == 0:
                    act.wait_ge(sem["xt_psum"], TILES)
                b, k = i // QT, i % QT
                act.activation(ret[:, b * GROUPS:(b + 1) * GROUPS, k * P:(k + 1) * P], tp[RET_BANK][:, :, :],
                               ACT.Copy, scale=1 / Q_SCALE).then_inc(sem["ret"], 1)

            def state_high(i):
                act.wait_ge(sem["state"], states(i) + 1)
                act.activation(st_hi, state, ACT.Copy).then_inc(sem["st_hi"], 1)

            def gated_high(b, groups):
                if 0 in groups:
                    act.wait_ge(sem["hvar"], b + 1)
                    act.activation(hstd, hvar, ACT.Sqrt).then_inc(sem["hstd"], 1)
                for g in groups:
                    act.wait_ge(sem["gated"], b * GROUPS + g + 1)
                    act.activation(gated_hi[b][:, g, :], ret[:, b * GROUPS + g, :], ACT.Copy)\
                       .then_inc(sem["g_hi"], 1)

            v_high(0)
            kn_high(0)
            qk_high(0)
            for i in range(TILES):
                for j in range(GH):
                    act.wait_ge(sem["masked"], GH * i + j + 1)
                    wait(act, sem["pv"], i)
                    act.activation(s_hi[:, j, :], masked[:, j, :], ACT.Copy).then_inc(sem["s_hi"], 1)
                result(i)
                if i + 1 < TILES:
                    v_high(i + 1)
                if i % QT < LAST:
                    state_high(i)
                gates(i)
                if i + 1 < TILES:
                    kn_high(i + 1)
                    qk_high(i + 1)
                for b, g in GATED_AT.get(i, ()):
                    gated_high(b, [g])
            gated_high(BATCH - 1, range(GROUPS))

        @block.vector
        def _(dve):
            norm_vector(dve, s, tp[6:8], sem)
            small = [0]

            def link(ins):
                small[0] += 1
                ins.then_inc(sem["small"], 1)
                dve.wait_ge(sem["small"], small[0])

            def biases(i, h):
                if i == 0 and h == "q":
                    dve.wait_ge(sem["bias_in"], 16)
                dve.wait_ge(sem["qkv"], 3 * i + "qkv".index(h) + 1)
                if h == "v":
                    wait(dve, sem["v_lo"], i)
                else:
                    wait(dve, sem[f"{h}_swap"], 2 * i)
                    wait(dve, sem[f"{h}_cos"], i)
                dve.scalar_tensor_tensor(out=biased[h], in0=bank[QKV_BANK[h]][:, :], scalar=1 / W_SCALE,
                                         in1=bias[:, "qkv".index(h), :], op0=ALU.mult, op1=ALU.add)\
                   .then_inc(sem[f"{h}_b"], 1)

            def cosine(i, h):
                if i == 0:
                    dve.wait_ge(sem[f"{h}_cos_in"], 16)
                dve.wait_ge(sem[f"{h}_b"], i + 1)
                wait(dve, sem[f"{h}_tp"], i)
                if h == "k":
                    wait(dve, sem["kn_lo"], states(i))
                dve.tensor_tensor(turned[h], biased[h], cos[h][:, i % QT, :], ALU.mult)\
                   .then_inc(sem[f"{h}_cos"], 1)

            def turn(i, h):
                dve.wait_ge(sem[f"{h}_swap"], 2 * i + 2)
                dve.wait_ge(sem[f"{h}_cos"], i + 1)
                dve.tensor_tensor(turned[h], turned[h], swapped[h], ALU.add).then_inc(sem[f"{h}_turn"], 1)

            def v_low(i):
                dve.wait_ge(sem["v_hi"], i + 1)
                dve.tensor_tensor(v_lo[:, i % 2, :], biased["v"], v_hi[:, i % 2, :], ALU.subtract)\
                   .then_inc(sem["v_lo"], 1)

            def kn_low(i):
                if i % QT < LAST:
                    dve.wait_ge(sem["kn_hi"], states(i) + 1)
                    dve.tensor_tensor(kn_lo, turned["k"], kn_hi, ALU.subtract).then_inc(sem["kn_lo"], 1)

            def qk_low(i):
                par = i % 2 * GROUPS
                for h in HALVES:
                    dve.wait_ge(sem[f"{h}_hi"], i + 1)
                    dve.tensor_tensor(qk_lo[h][:, par:par + GROUPS, :], tp[TURN_BANK[h]][:, :, :],
                                      qk_hi[h][:, par:par + GROUPS, :], ALU.subtract).then_inc(sem[f"{h}_lo"], 1)

            def mask(i):
                if i == 0:
                    dve.wait_ge(sem["causal_in"], 16)
                wait(dve, sem["s_lo_dve"], 2 * i)
                wait(dve, sem["s_lo_pool"], 2 * i)
                dve.wait_ge(sem["score"], i + 1)
                for j in range(GH):
                    dve.tensor_tensor(masked[:, j, :].rearrange("p (g n) -> p g n", g=GROUPS),
                                      tp[SCORE_BANK[j]][:, :, :],
                                      causal.unsqueeze(1).to_broadcast([P, GROUPS, P]), ALU.mult)\
                       .then_inc(sem["masked"], 1)
                wait(dve, sem["pv"], i)
                for j in range(2, GH):
                    dve.wait_ge(sem["s_hi"], GH * i + j + 1)
                    dve.tensor_tensor(s_lo[:, j, :], masked[:, j, :], s_hi[:, j, :], ALU.subtract)\
                       .then_inc(sem["s_lo_dve"], 1)

            def grow(i):
                c = states(i)
                dve.wait_ge(sem["growth"], c + 1)
                wait(dve, sem["state"], c)
                if i % QT == 0:
                    dve.tensor_copy(grown, tp[STATE_BANK][:, :, :]).then_inc(sem["grown"], 1)
                else:
                    dve.tensor_tensor(grown, tp[STATE_BANK][:, :, :], state, ALU.add).then_inc(sem["grown"], 1)

            def state_low(i):
                dve.wait_ge(sem["st_hi"], states(i) + 1)
                dve.tensor_tensor(st_lo, state, st_hi, ALU.subtract).then_inc(sem["st_lo"], 1)

            def head_sums(b):
                dve.wait_ge(sem["ret"], (b + 1) * QT)
                for g in range(GROUPS):
                    dve.bn_stats(hstats[:, g, :], ret[:, b * GROUPS + g, :]).then_inc(sem["hstats"], 1)
                for g in range(GROUPS):
                    dve.wait_ge(sem["hstats"], b * GROUPS + g + 1)
                    dve.bn_aggr(hmv[:, g, :], hstats[:, g, :]).then_inc(sem["hmv"], 1)
                dve.wait_ge(sem["hmv"], (b + 1) * GROUPS)
                link(dve.tensor_tensor(sq, hmv[:, :, 0], hmv[:, :, 0], ALU.mult))
                link(dve.tensor_copy(sums[:, 0, :], hmv[:, :, 0]))
                dve.tensor_tensor(sums[:, 1, :], sq, hmv[:, :, 1], ALU.add).then_inc(sem["sums"], 1)

            def group_norm(b):
                dve.wait_ge(sem["head_psum"], b + 1)
                link(dve.tensor_copy(means, bank[HEAD_BANK][:, 0:2 * GROUPS].rearrange("p (a g) -> p a g", a=2)))
                link(dve.tensor_tensor(sq, means[:, 0, :], means[:, 0, :], ALU.mult))
                link(dve.tensor_tensor(tmp, means[:, 1, :], sq, ALU.subtract))
                dve.tensor_scalar(hvar, tmp, EPS, None, ALU.add).then_inc(sem["hvar"], 1)
                dve.wait_ge(sem["hstd"], b + 1)
                link(dve.reciprocal(hrstd, hstd))
                if b == 0:
                    dve.wait_ge(sem["gnw_in"], 16)
                    dve.wait_ge(sem["gnb_in"], 16)
                link(dve.tensor_tensor(gscale, gn_w, hrstd, ALU.mult))
                link(dve.tensor_tensor(tmp, means[:, 0, :], gscale, ALU.mult))
                link(dve.tensor_tensor(gshift, gn_b, tmp, ALU.subtract))

            def gated(b, groups):
                for g in groups:
                    n = b * GROUPS + g
                    dve.tensor_scalar(ret[:, n, :], ret[:, n, :], gscale[:, g:g + 1], gshift[:, g:g + 1],
                                      ALU.mult, ALU.add).then_inc(sem["gn"], 1)
                    dve.wait_ge(sem["gate"], n + 1)
                    dve.wait_ge(sem["gn"], n + 1)
                    dve.tensor_tensor(ret[:, n, :], ret[:, n, :], gate[:, n, :], ALU.mult)\
                       .then_inc(sem["gated"], 1)
                for g in groups:
                    n = b * GROUPS + g
                    dve.wait_ge(sem["g_hi"], n + 1)
                    dve.tensor_tensor(gated_lo[b][:, g, :], ret[:, n, :], gated_hi[b][:, g, :], ALU.subtract)\
                       .then_inc(sem["g_lo"], 1)

            def residual(i):
                dve.wait_ge(sem["wo"], i + 1)
                dve.wait_ge(sem["x_bo"], i + 1)
                dve.scalar_tensor_tensor(out=X[:, i, :], in0=bank[OUT_BANK[i]][:, :], scalar=1 / W_SCALE,
                                         in1=X[:, i, :], op0=ALU.mult, op1=ALU.add).then_inc(sem["x2"], 1)

            def project_qk(i):
                for h in HALVES:
                    biases(i, h)
                for h in HALVES:
                    cosine(i, h)

            def project_v(i):
                biases(i, "v")
                for h in HALVES:
                    turn(i, h)
                v_low(i)
            project_qk(0)
            project_v(0)
            kn_low(0)
            qk_low(0)
            for i in range(TILES):
                mask(i)
                if i + 1 < TILES:
                    project_qk(i + 1)
                if i % QT < LAST:
                    grow(i)
                if i + 1 < TILES:
                    project_v(i + 1)
                if i % QT < LAST:
                    state_low(i)
                if i + 1 < TILES:
                    kn_low(i + 1)
                    qk_low(i + 1)
                if i == QT:
                    head_sums(0)
                if i == QT + 1:
                    group_norm(0)
                for b, g in GATED_AT.get(i, ()):
                    gated(b, [g])
            head_sums(1)
            residual(0)
            group_norm(1)
            gated(1, range(GROUPS))
            for i in range(1, TILES):
                residual(i)

        @block.tensor
        def _(pe):
            def project(i, h):
                n = "qkv".index(h)
                pe.wait_ge(sem["xt_lo"], i + 1)
                wait(pe, sem[f"{h}_b"], i)
                if h == "q":
                    wait(pe, sem["gate"], i - 1)
                if h == "v" and i == QT + 3:
                    pe.wait_ge(sem["hvar"], 1)
                for k in range(KD):
                    last = three(pe, bank[QKV_BANK[h]][:, :], xt_hi[:, k, i * P:(i + 1) * P],
                                 xt_lo[:, k, i * P:(i + 1) * P], w_hi[:, n, k, :], w_lo[:, n, k, :],
                                 k == 0, k == KD - 1)
                last.then_inc(sem["qkv"], 1)

            def turn(i):
                for h in HALVES:
                    pe.wait_ge(sem[f"{h}_turn"], i + 1)
                    wait(pe, sem["masked"], GH * i)
                    for g in range(GROUPS):
                        last = pe.transpose(tp[TURN_BANK[h]][:, g, :], turned[h][:, g * P:(g + 1) * P],
                                            s["ident"][:, :])
                    last.then_inc(sem[f"{h}_tp"], 1)

            def gates(i):
                b, g = i // GROUPS, i % GROUPS
                pe.wait_ge(sem["q_b"], min(i + 2, TILES))
                for k in range(KD):
                    last = three(pe, bank[QKV_BANK["q"]][:, :], w_hi[:, 3, k, g * P:(g + 1) * P],
                                 w_lo[:, 3, k, g * P:(g + 1) * P], xt_hi[:, k, b * SEQ:(b + 1) * SEQ],
                                 xt_lo[:, k, b * SEQ:(b + 1) * SEQ], k == 0, k == KD - 1)
                last.then_inc(sem["gate_psum"], 1)

            def scores(i):
                if i == 0:
                    pe.wait_ge(sem["xt_lo"], TILES)
                pe.wait_ge(sem["q_lo"], i + 1)
                pe.wait_ge(sem["k_lo"], i + 1)
                wait(pe, sem["grown"], states(i))
                par = i % 2 * GROUPS
                for g in range(GROUPS):
                    for p in range(3):
                        for j in range(GH):
                            keys = (qk_lo if p == 2 else qk_hi)["k"]
                            queries = (qk_lo if p == 1 else qk_hi)["q"]
                            rows = slice(j * HEAD, (j + 1) * HEAD)
                            last = pe.matmul(bank[SCORE_BANK[j]][:, g * P:(g + 1) * P], keys[rows, par + g, :],
                                             queries[rows, par + g, :], start=(p == 0), stop=(p == 2))
                last.then_inc(sem["score"], 1)

            def values(i):
                if i % QT:
                    pe.wait_ge(sem["st_lo"], states(i))
                pe.wait_ge(sem["v_lo"], i + 1)
                pe.wait_ge(sem["s_lo_dve"], 2 * i + 2)
                pe.wait_ge(sem["s_lo_pool"], 2 * i + 2)
                wait(pe, sem["ret"], i)
                par = i % 2 * GROUPS
                for g in range(GROUPS):
                    cols = slice(g * P, (g + 1) * P)
                    if i % QT:
                        three(pe, bank[RET_BANK][:, cols], st_hi[:, g, :], st_lo[:, g, :],
                              qk_hi["q"][:, par + g, :], qk_lo["q"][:, par + g, :], True, False)
                    for p in range(3):
                        for j in range(GH):
                            v = (v_lo if p == 2 else v_hi)[:, i % 2, (GH * g + j) * HEAD:(GH * g + j + 1) * HEAD]
                            last = pe.matmul(bank[RET_BANK][j * HEAD:(j + 1) * HEAD, cols], v,
                                             (s_lo if p == 1 else s_hi)[:, j, cols],
                                             start=(i % QT == 0 and p == 0), stop=(p == 2))
                last.then_inc(sem["pv"], 1)

            def growth(i):
                pe.wait_ge(sem["kn_lo"], states(i) + 1)
                pe.wait_ge(sem["masked"], GH * (i + 1))
                for g in range(GROUPS):
                    cols = slice(g * P, (g + 1) * P)
                    last = three(pe, bank[STATE_BANK][:, cols], kn_hi[:, cols], kn_lo[:, cols],
                                 v_hi[:, i % 2, cols], v_lo[:, i % 2, cols], True, True)
                last.then_inc(sem["growth"], 1)

            def head_means(b):
                if b == 0:
                    pe.wait_ge(sem["same_in"], 16)
                pe.wait_ge(sem["v_b"], TILES if b else QT + 3)
                pe.wait_ge(sem["sums"], b + 1)
                pe.matmul(bank[HEAD_BANK][:, 0:2 * GROUPS], same_head, sums.rearrange("p a g -> p (a g)"),
                          start=True, stop=True).then_inc(sem["head_psum"], 1)

            def out(i):
                b, c = i // QT, i % QT
                pe.wait_ge(sem["g_lo"], (b + 1) * GROUPS)
                if i == 0:
                    pe.wait_ge(sem["gate"], TILES)
                if i == 1:
                    pe.wait_ge(sem["k_b"], TILES)
                if i >= 6:
                    pe.wait_ge(sem["x2"], i - 5)
                for g in range(GROUPS):
                    last = three(pe, bank[OUT_BANK[i]][:, :], gated_hi[b][:, g, c * P:(c + 1) * P],
                                 gated_lo[b][:, g, c * P:(c + 1) * P], w_hi[:, 4, g, :], w_lo[:, 4, g, :],
                                 g == 0, g == GROUPS - 1)
                last.then_inc(sem["wo"], 1)

            norm_tensor(pe, s, tp[6:8], sem, range(QT))
            for h in ("q", "k", "v"):
                project(0, h)
            norm_tensor(pe, s, tp[6:8], sem, range(QT, TILES))
            turn(0)
            for i in range(TILES):
                scores(i)
                if i + 1 < TILES:
                    project(i + 1, "q")
                    project(i + 1, "k")
                values(i)
                if i % QT < LAST:
                    growth(i)
                if i + 1 < TILES:
                    project(i + 1, "v")
                if i == QT + 1:
                    head_means(0)
                gates(i)
                if i + 1 < TILES:
                    turn(i + 1)
            out(0)
            head_means(1)
            for i in range(1, TILES):
                out(i)
    return sem


def experts(nc, t, s, arena):
    X, XN, xt_hi, xt_lo = s["X"], s["XN"], s["xt_hi"], s["xt_lo"]
    PICKS = TOPK * TILES
    raw_t = arena.take([2, KD, HCHUNK])
    raw_n = arena.take([2, HT, D])
    t_hi, t_lo, n_hi, n_lo = (arena.take([2 * KD, HCHUNK], F16) for _ in range(4))
    hidden = arena.take([2, HT * CAP])
    h_hi = arena.take([2 * HT, CAP], F16)
    h_lo = arena.take([2 * HT, CAP], F16)
    de = arena.take([CAP_TILES, D])
    de_hi = arena.take([KD, CAP], F16)
    de_lo = arena.take([KD, CAP], F16)
    eo = arena.take([CAP_TILES, D])
    b1 = arena.take([HID // P])
    b2 = arena.take([D])
    zeros = arena.take([D])
    gw = arena.take([KD, EXPERTS])
    gw_s = arena.take([KD, EXPERTS])
    gw_hi = arena.take([KD, EXPERTS], F16)
    gw_lo = arena.take([KD, EXPERTS], F16)
    number = arena.take([EXPERTS])
    before = arena.take([P], F16)
    ones = arena.take([P], F16)
    logits, shifted, raised, score = (arena.take([TILES, EXPERTS]) for _ in range(4))
    top8 = arena.take([TILES, 8])
    top8_at = arena.take([TILES, 8]).bitcast(U32)
    peak, mass, mass_r, pair, pair_r = (arena.take([TILES]) for _ in range(5))
    expert = arena.take([TOPK, TILES])
    chosen = arena.take([PICKS, EXPERTS])
    chosen_h = arena.take([PICKS, EXPERTS], F16)
    spread = arena.take([PICKS, EXPERTS])
    loc, valid, flat, kept, far = (arena.take([PICKS]) for _ in range(5))
    weight = arena.take([TOPK, TILES])
    to_slot = arena.take([PICKS]).bitcast(U32)
    from_slot = arena.take([PICKS]).bitcast(U32)
    over = Arena(arena.tensor, arena.words)
    got = over.take([PICKS, D])
    bank = s["banks"]
    tp = [bank[i][:, :].rearrange("p (k n) -> p k n", k=KD) for i in range(8)]
    CHUNKS_ALL = EXPERTS * HCHUNKS
    SLOTS = EXPERTS * CAP
    FAR_SLOT = 2 * SLOTS

    def within(e, place):
        return not isinstance(e, int) or 0 <= HCHUNKS * e + place < CHUNKS_ALL

    def steps(engine, slot):
        for c in range(-1, HCHUNKS):
            slot(0, c)
        with engine.Fori(1, EXPERTS - 1) as e:
            for c in range(HCHUNKS):
                slot(e, c)
        for c in range(HCHUNKS + 1):
            slot(EXPERTS - 1, c)

    with ExitStack() as ctx:
        names = NORM_SEMS + [
            "gw_in", "number_in", "before_in", "zero", "zeroed", "gw_s", "gw_hi", "gw_lo", "ones",
            "logit_psum", "small", "raised", "expd", "chosen", "loc_psum", "routed", "scattered",
            "t_in0", "t_in1", "n_in0", "n_in1", "b1_in", "b2_in", "de_in", "de_tp", "de_hi", "de_lo",
            "t_hi", "t_lo", "n_hi", "n_lo", "fc1", "relu", "h_hi", "h_lo", "fc2", "eo", "eo_out",
            "half", "sum", "out"]
        sem = semaphores(nc, "e_", names)
        got_in = [nc.alloc_semaphore(f"e_got_in{n}") for n in range(PICKS)]
        block = ctx.enter_context(nc.Block())

        @block.sync
        def _(sp):
            def at(a, i):
                if isinstance(i, int):
                    return a[i]
                a = a[bass.ds(i, 1)]
                return a.rearrange("a p n -> (a p) n") if len(a.shape) == 3 else \
                    a.rearrange("a p k n -> (a p) k n")

            def weights(e, c, part):
                u = HCHUNKS * e + c
                name, raw = (("t", raw_t), ("n", raw_n))[part]
                wait(sp, sem[name + "_hi"], (u - 1) * KD)
                wait(sp, sem[name + "_lo"], (u - 1) * KD)
                sp.dma_start(raw[:, c % 2], at(t[("fc1", "fc2")[part]], u)).then_inc(sem[f"{name}_in{c % 2}"], 16)

            def tokens(e):
                wait(sp, sem["de_tp"], CAP_TILES * e)
                src = s["disp"].rearrange("(e a p) d -> e p a d", p=P, a=CAP_TILES)
                sp.dma_start(de, at(src, e)).then_inc(sem["de_in"], 16)

            def bias1(e):
                wait(sp, sem["relu"], HT * HCHUNKS * e)
                sp.dma_start(b1, at(t["fc1_b"], e)).then_inc(sem["b1_in"], 16)

            def store(e):
                sp.wait_ge(sem["eo"], CAP_TILES * (e + 1))
                dst = s["eo_d"].rearrange("(e a p) d -> e p a d", p=P, a=CAP_TILES)
                sp.dma_start(at(dst, e), eo).then_inc(sem["eo_out"], 16)

            def bias2(e):
                wait(sp, sem["eo"], CAP_TILES * e)
                sp.dma_start(b2, at(t["fc2_b"], e)).then_inc(sem["b2_in"], 16)

            sp.dma_start(gw, t["gate_w"]).then_inc(sem["gw_in"], 16)
            sp.dma_start(number, t["expert_no"]).then_inc(sem["number_in"], 16)
            sp.dma_start(before, t["before"]).then_inc(sem["before_in"], 16)
            sp.wait_ge(sem["zero"], 1)
            for n in range(SLOTS // P):
                sp.dma_start(s["disp"][n * P:(n + 1) * P, :], zeros).then_inc(sem["zeroed"], 16)
            for c in range(2):
                weights(0, c, 0)
                weights(0, c, 1)
            bias1(0)
            bias2(0)
            sp.wait_ge(sem["scattered"], 16 * PICKS)
            tokens(0)
            for c in range(2, HCHUNKS):
                weights(0, c, 0)
                weights(0, c, 1)
            tokens(1)

            def step(e, last):
                for c in range(HCHUNKS):
                    weights(e, c, 0)
                    weights(e, c, 1)
                    if c == 1:
                        bias1(e)
                store(e - 1)
                bias2(e)
                if not last:
                    tokens(e + 1)
            with sp.Fori(1, EXPERTS - 1) as e:
                step(e, False)
            step(EXPERTS - 1, True)
            store(EXPERTS - 1)
            for i in range(TILES):
                sp.wait_ge(sem["sum"], i + 1)
                sp.dma_start(t["out"][:, i, :], X[:, i, :]).then_inc(sem["out"], 16)
            sp.wait_ge(sem["out"], 16 * TILES)

        @block.gpsimd
        def _(pool):
            pool.memset(zeros, 0.0).then_inc(sem["zero"], 1)
            pool.memset(ones, 1.0).then_inc(sem["ones"], 1)
            pool.wait_ge(sem["zeroed"], 16 * (SLOTS // P))
            pool.wait_ge(sem["xn"], TILES)
            pool.wait_ge(sem["routed"], 1)
            for n in range(PICKS):
                pool.indirect_dma_start(
                    out=s["disp"], out_offset=bass.IndirectOffsetOnAxis(ap=to_slot[:, n:n + 1], axis=0),
                    in_=XN[:, n % TILES, :], in_offset=None, bounds_check=SLOTS - 1, oob_is_err=False)\
                    .then_inc(sem["scattered"], 16)
            pool.wait_ge(sem["eo_out"], 16 * EXPERTS)
            for i in range(TILES):
                for k in range(TOPK):
                    n = k * TILES + i
                    pool.indirect_dma_start(
                        out=got[:, n, :], out_offset=None, in_=s["eo_d"],
                        in_offset=bass.IndirectOffsetOnAxis(ap=from_slot[:, n:n + 1], axis=0),
                        bounds_check=SLOTS - 1, oob_is_err=False).then_inc(got_in[n], 16)

        @block.scalar
        def _(act):
            act.wait_ge(sem["gw_in"], 16)
            act.activation(gw_s, gw, ACT.Copy, scale=W_SCALE).then_inc(sem["gw_s"], 1)
            act.wait_ge(sem["gw_s"], 1)
            act.activation(gw_hi, gw_s, ACT.Copy).then_inc(sem["gw_hi"], 1)
            norm_scalar(act, s, tp, sem)
            act.wait_ge(sem["raised"], 1)
            act.activation(raised, shifted, ACT.Exp).then_inc(sem["expd"], 1)

            def t_high(e, place):
                par = place % 2
                act.wait_ge(sem[f"t_in{par}"], 16 * (HCHUNKS // 2 * e + place // 2 + 1))
                wait(act, sem["fc1"], 2 * (HCHUNKS * e + place - 1))
                for k in range(KD):
                    act.activation(t_hi[:, par * KD + k, :], raw_t[:, par, k, :], ACT.Copy, scale=W_SCALE)\
                       .then_inc(sem["t_hi"], 1)

            def n_high(e, place):
                par = place % 2
                act.wait_ge(sem[f"n_in{par}"], 16 * (HCHUNKS // 2 * e + place // 2 + 1))
                wait(act, sem["fc2"], HCHUNKS * e + place - 1)
                for k in range(HT):
                    act.activation(n_hi[:, par * HT + k, :], raw_n[:, par, k, :], ACT.Copy, scale=W_SCALE)\
                       .then_inc(sem["n_hi"], 1)

            def de_high(e):
                for a in range(CAP_TILES):
                    act.wait_ge(sem["de_tp"], CAP_TILES * e + a + 1)
                    act.activation(de_hi[:, :, a * P:(a + 1) * P], tp[2 + a][:, :, :], ACT.Copy)\
                       .then_inc(sem["de_hi"], 1)

            def relus(e, place):
                u = HCHUNKS * e + place
                if place % HCHUNKS == 0:
                    act.wait_ge(sem["b1_in"], 16 * (e + place // HCHUNKS + 1))
                for h in range(HT):
                    if h % 2 == 0:
                        act.wait_ge(sem["fc1"], 2 * u + h // 2 + 1)
                        wait(act, sem["h_lo"], u - 1)
                    act.activation(hidden[:, place % 2, h * CAP:(h + 1) * CAP],
                                   bank[h // 2][:, h % 2 * CAP:(h % 2 + 1) * CAP], ACT.Relu,
                                   bias=b1[:, place % HCHUNKS * HT + h:place % HCHUNKS * HT + h + 1],
                                   scale=1 / W_SCALE).then_inc(sem["relu"], 1)

            def h_high(e, place):
                u = HCHUNKS * e + place
                par = place % 2
                act.wait_ge(sem["relu"], HT * (u + 1))
                wait(act, sem["fc2"], u - 1)
                act.activation(h_hi[:, par * HT:(par + 1) * HT, :].rearrange("p a c -> p (a c)"),
                               hidden[:, par, :], ACT.Copy).then_inc(sem["h_hi"], 1)

            def slot(e, c):
                if within(e, c + 2):
                    t_high(e, c + 2)
                if within(e, c + 1):
                    n_high(e, c + 1)
                    relus(e, c + 1)
                if c == 2 and (not isinstance(e, int) or e < EXPERTS - 1):
                    de_high(e + 1)
                if within(e, c + 1):
                    h_high(e, c + 1)
            t_high(0, 0)
            de_high(0)
            steps(act, slot)

        @block.vector
        def _(dve):
            norm_vector(dve, s, tp, sem)
            dve.wait_ge(sem["gw_hi"], 1)
            dve.tensor_tensor(gw_lo, gw_s, gw_hi, ALU.subtract).then_inc(sem["gw_lo"], 1)
            small = [0]

            def link(ins):
                small[0] += 1
                ins.then_inc(sem["small"], 1)
                dve.wait_ge(sem["small"], small[0])

            def along(a):
                return a.unsqueeze(2).to_broadcast([P, a.shape[1], EXPERTS])

            dve.wait_ge(sem["logit_psum"], 1)
            link(dve.tensor_scalar(logits, bank[2][:, 0:TILES * EXPERTS].rearrange("p (i e) -> p i e", e=EXPERTS),
                                   1 / W_SCALE, None, ALU.mult))
            link(dve.reduce_max(peak, logits, AX))
            dve.tensor_tensor(shifted, logits, along(peak), ALU.subtract).then_inc(sem["raised"], 1)
            dve.wait_ge(sem["expd"], 1)
            link(dve.reduce_sum(mass, raised, AX))
            link(dve.reciprocal(mass_r, mass))
            link(dve.tensor_tensor(score, raised, along(mass_r), ALU.mult))
            for i in range(TILES):
                link(dve.max(top8[:, i, :], score[:, i, :]))
                link(dve.max_index(top8_at[:, i, :], top8[:, i, :], score[:, i, :]))
            link(dve.tensor_tensor(pair, top8[:, :, 0], top8[:, :, 1], ALU.add))
            link(dve.reciprocal(pair_r, pair))
            for k in range(TOPK):
                link(dve.tensor_copy(expert[:, k, :], top8_at[:, :, k]))
            dve.wait_ge(sem["number_in"], 16)
            link(dve.tensor_tensor(chosen, along(expert.rearrange("p k i -> p (k i)")),
                                   number.unsqueeze(1).to_broadcast([P, PICKS, EXPERTS]), ALU.is_equal))
            dve.tensor_copy(chosen_h, chosen).then_inc(sem["chosen"], 1)
            dve.wait_ge(sem["loc_psum"], 1)
            link(dve.tensor_tensor(spread, bank[3][:, 0:PICKS * EXPERTS].rearrange("p (n e) -> p n e", e=EXPERTS),
                                   chosen, ALU.mult))
            link(dve.reduce_sum(loc, spread, AX))
            link(dve.tensor_scalar(valid, loc, float(CAP), None, ALU.is_lt))
            link(dve.scalar_tensor_tensor(out=flat, in0=expert.rearrange("p k i -> p (k i)"), scalar=float(CAP),
                                          in1=loc, op0=ALU.mult, op1=ALU.add))
            link(dve.tensor_tensor(kept, flat, valid, ALU.mult))
            link(dve.tensor_copy(from_slot, kept))
            link(dve.tensor_scalar(far, flat, -float(FAR_SLOT), None, ALU.add))
            link(dve.tensor_tensor(far, far, valid, ALU.mult))
            link(dve.tensor_scalar(far, far, float(FAR_SLOT), None, ALU.add))
            dve.tensor_copy(to_slot, far).then_inc(sem["routed"], 1)
            for k in range(TOPK):
                link(dve.tensor_tensor(weight[:, k, :], top8[:, :, k], pair_r, ALU.mult))
            link(dve.tensor_tensor(weight.rearrange("p k i -> p (k i)"), weight.rearrange("p k i -> p (k i)"),
                                   valid, ALU.mult))

            def lows(e, place, raw, hi, lo, name):
                par = place % 2
                for k in range(KD):
                    dve.wait_ge(sem[name + "_hi"], KD * (HCHUNKS * e + place) + k + 1)
                    dve.scalar_tensor_tensor(out=lo[:, par * KD + k, :], in0=raw[:, par, k, :], scalar=W_SCALE,
                                             in1=hi[:, par * KD + k, :], op0=ALU.mult, op1=ALU.subtract)\
                       .then_inc(sem[name + "_lo"], 1)

            def de_low(e):
                for a in range(CAP_TILES):
                    dve.wait_ge(sem["de_hi"], CAP_TILES * e + a + 1)
                    dve.tensor_tensor(de_lo[:, :, a * P:(a + 1) * P], tp[2 + a][:, :, :],
                                      de_hi[:, :, a * P:(a + 1) * P], ALU.subtract).then_inc(sem["de_lo"], 1)

            def result(e):
                dve.wait_ge(sem["fc2"], HCHUNKS * (e + 1))
                dve.wait_ge(sem["b2_in"], 16 * (e + 1))
                wait(dve, sem["eo_out"], 16 * e)
                for a in range(CAP_TILES):
                    dve.scalar_tensor_tensor(out=eo[:, a, :], in0=bank[4 + a][:, :], scalar=1 / W_SCALE,
                                             in1=b2, op0=ALU.mult, op1=ALU.add).then_inc(sem["eo"], 1)

            def slot(e, c):
                if c % HCHUNKS == 0 and (not isinstance(e, int) or e + c // HCHUNKS > 0):
                    result(e + c // HCHUNKS - 1)
                if within(e, c + 2):
                    lows(e, c + 2, raw_t, t_hi, t_lo, "t")
                if within(e, c + 1):
                    lows(e, c + 1, raw_n, n_hi, n_lo, "n")
                if c == 2 and (not isinstance(e, int) or e < EXPERTS - 1):
                    de_low(e + 1)
                if within(e, c + 1):
                    u = HCHUNKS * e + c + 1
                    par = (c + 1) % 2
                    dve.wait_ge(sem["h_hi"], u + 1)
                    dve.tensor_tensor(h_lo[:, par * HT:(par + 1) * HT, :].rearrange("p a c -> p (a c)"),
                                      hidden[:, par, :],
                                      h_hi[:, par * HT:(par + 1) * HT, :].rearrange("p a c -> p (a c)"),
                                      ALU.subtract).then_inc(sem["h_lo"], 1)
            lows(0, 0, raw_t, t_hi, t_lo, "t")
            de_low(0)
            steps(dve, slot)
            for i in range(TILES):
                for k in range(TOPK):
                    n = k * TILES + i
                    dve.wait_ge(got_in[n], 16)
                    if k:
                        dve.wait_ge(sem["half"], i + 1)
                    dve.scalar_tensor_tensor(out=X[:, i, :], in0=got[:, n, :], scalar=weight[:, k, i:i + 1],
                                             in1=X[:, i, :], op0=ALU.mult, op1=ALU.add)\
                       .then_inc(sem[("half", "sum")[k]], 1)

        @block.tensor
        def _(pe):
            norm_tensor(pe, s, tp, sem)
            pe.wait_ge(sem["gw_lo"], 1)
            for i in range(TILES):
                pe.wait_ge(sem["xt_lo"], i + 1)
                for k in range(KD):
                    last = three(pe, bank[2][:, i * EXPERTS:(i + 1) * EXPERTS], xt_hi[:, k, i * P:(i + 1) * P],
                                 xt_lo[:, k, i * P:(i + 1) * P], gw_hi[:, k, :], gw_lo[:, k, :],
                                 k == 0, k == KD - 1)
            last.then_inc(sem["logit_psum"], 1)
            pe.wait_ge(sem["chosen"], 1)
            pe.wait_ge(sem["before_in"], 16)
            pe.wait_ge(sem["ones"], 1)
            pe.matmul(bank[3][:, 0:PICKS * EXPERTS], before, chosen_h.rearrange("p n e -> p (n e)"),
                      start=True, stop=False)
            for n in range(PICKS - 1):
                last = pe.matmul(bank[3][:, (n + 1) * EXPERTS:PICKS * EXPERTS], ones,
                                 chosen_h[:, n:n + 1, :].to_broadcast([P, PICKS - 1 - n, EXPERTS]),
                                 start=False, stop=(n == PICKS - 2))
            last.then_inc(sem["loc_psum"], 1)

            def turn(e):
                pe.wait_ge(sem["de_in"], 16 * (e + 1))
                wait(pe, sem["de_lo"], CAP_TILES * e)
                for a in range(CAP_TILES):
                    for k in range(KD):
                        last = pe.transpose(tp[2 + a][:, k, :], de[:, a, k * P:(k + 1) * P], s["ident"][:, :])
                    last.then_inc(sem["de_tp"], 1)

            def fc1(e, place):
                u = HCHUNKS * e + place
                par = place % 2
                pe.wait_ge(sem["t_lo"], KD * (u + 1))
                if place % HCHUNKS == 0:
                    pe.wait_ge(sem["de_lo"], CAP_TILES * (e + place // HCHUNKS + 1))
                wait(pe, sem["relu"], HT * u)
                for h in range(HT):
                    for k in range(KD):
                        last = three(pe, bank[h // 2][:, h % 2 * CAP:(h % 2 + 1) * CAP],
                                     t_hi[:, par * KD + k, h * P:(h + 1) * P],
                                     t_lo[:, par * KD + k, h * P:(h + 1) * P], de_hi[:, k, :], de_lo[:, k, :],
                                     k == 0, k == KD - 1)
                    if h % 2:
                        last.then_inc(sem["fc1"], 1)

            def fc2(e, place):
                u = HCHUNKS * e + place
                par = place % 2
                pe.wait_ge(sem["n_lo"], HT * (u + 1))
                pe.wait_ge(sem["h_lo"], u + 1)
                if place % HCHUNKS == 0:
                    wait(pe, sem["eo"], CAP_TILES * (e + place // HCHUNKS))
                for a in range(CAP_TILES):
                    for h in range(HT):
                        last = three(pe, bank[4 + a][:, :], h_hi[:, par * HT + h, a * P:(a + 1) * P],
                                     h_lo[:, par * HT + h, a * P:(a + 1) * P], n_hi[:, par * HT + h, :],
                                     n_lo[:, par * HT + h, :], place % HCHUNKS == 0 and h == 0,
                                     place % HCHUNKS == HCHUNKS - 1 and h == HT - 1)
                last.then_inc(sem["fc2"], 1)

            def slot(e, c):
                if within(e, c + 1):
                    fc1(e, c + 1)
                if c == 2 and (not isinstance(e, int) or e < EXPERTS - 1):
                    turn(e + 1)
                if within(e, c):
                    fc2(e, c)
            turn(0)
            steps(pe, slot)


def _tables():
    f = np.float32
    inv = (1.0 / f(10000.0) ** (np.arange(0, HEAD, 2, dtype=f) / f(HEAD))).astype(f)
    pos = np.arange(SEQ, dtype=f)
    freqs = np.repeat(pos[:, None] * inv[None, :], 2, axis=-1).astype(f)
    base = ((np.arange(0, HEAD, 2, dtype=f) + f(0.4 * HEAD)) / f(1.4 * HEAD)).astype(f)
    power = (pos - SEQ // 2) / f(512.0)
    scale = np.repeat(base[None, :] ** power[:, None], 2, axis=-1).astype(f)
    cos, sin = np.cos(freqs), np.sin(freqs)
    sign = np.where(np.arange(HEAD) % 2 == 0, -1.0, 1.0).astype(f)
    gamma = (1.0 - 2.0 ** (-5.0 - np.arange(HEADS))).astype(np.float64)
    norm = 1 / np.sqrt(np.cumsum(gamma[None, :] ** np.arange(SEQ)[:, None], axis=0))
    grow = gamma[None, :] ** (np.arange(SEQ)[:, None] % P)
    q_head, k_head = (Q_SCALE * norm * grow)[:, :, None], (1 / grow)[:, :, None]
    tables = [((cos * scale)[:, None, :] * q_head), ((sin * scale * sign)[:, None, :] * q_head),
              ((cos / scale)[:, None, :] * k_head), ((sin / scale * sign)[:, None, :] * k_head)]
    tables = [np.ascontiguousarray(a.reshape(SEQ_TILES, P, -1).transpose(1, 0, 2), dtype=f) for a in tables]
    lane = np.arange(P)
    block = lane[:, None] // HEAD == lane[None, :] // HEAD
    by_lane = np.repeat(gamma.reshape(GROUPS, GH) ** P, HEAD, axis=1).T
    carry = (block[:, None, :] * by_lane[:, :, None]).astype(f)
    return tables + [carry]


def kernel(x, ctx_1024, L0_xattn_W, L0_xattn_b, L0_attn_Wq, L0_attn_bq, L0_attn_Wk, L0_attn_bk, L0_attn_Wv,
           L0_attn_bv, L0_attn_Wg, L0_attn_bg, L0_attn_Wo, L0_attn_bo, L0_attn_gn_w, L0_attn_gn_b,
           L0_ffn_gate_w, L0_ffn_fc1_w, L0_ffn_fc1_b, L0_ffn_fc2_w, L0_ffn_fc2_b):
    import concourse.bacc as bacc
    from concourse.bass_utils import run_bass_kernel_spmd

    def rows(a):
        a = np.asarray(a)
        return a.reshape(-1, P, a.shape[-1]).transpose(1, 0, 2)

    def cols(a):
        return np.asarray(a).reshape(-1, P).T

    ctx = np.asarray(ctx_1024).reshape(BATCH * CHUNKS, CHUNK, KD, P)
    fc1 = np.asarray(L0_ffn_fc1_w).reshape(EXPERTS * HCHUNKS, HCHUNK, KD, P)
    fc2 = np.asarray(L0_ffn_fc2_w).reshape(EXPERTS * HCHUNKS, HT, P, D)
    q_cos, q_sin, k_cos, k_sin, carry = _tables()
    lane = np.arange(P)
    heads = lambda a: np.repeat(np.asarray(a).reshape(GROUPS, GH), HEAD, axis=1).T
    arrays = {
        "x": rows(np.asarray(x).reshape(TOK, D)),
        "ident": np.eye(P, dtype=np.float32),
        "wxt": rows(np.asarray(L0_xattn_W).T),
        "wxn": rows(L0_xattn_W),
        "xb": cols(L0_xattn_b),
        "ctx_t": ctx.transpose(0, 3, 2, 1),
        "ctx_n": ctx.reshape(BATCH * CHUNKS, CHUNK // P, P, D).transpose(0, 2, 1, 3),
        "w5": np.stack([rows(w) for w in (L0_attn_Wq, L0_attn_Wk, L0_attn_Wv, L0_attn_Wg, L0_attn_Wo)]),
        "bias_rows": np.broadcast_to(np.stack([np.asarray(b) for b in (L0_attn_bq, L0_attn_bk, L0_attn_bv)]),
                                     (P, 3, D)),
        "bo": np.broadcast_to(np.asarray(L0_attn_bo), (P, D)),
        "bg": cols(L0_attn_bg),
        "gn_w": heads(L0_attn_gn_w),
        "gn_b": heads(L0_attn_gn_b),
        "same_head": (lane[:, None] // HEAD == lane[None, :] // HEAD).astype(np.float32) / HEAD,
        "q_cos": q_cos, "q_sin": q_sin, "k_cos": k_cos, "k_sin": k_sin,
        "carry": carry,
        "causal": (lane[:, None] <= lane[None, :]).astype(np.float32),
        "gate_w": rows(np.asarray(L0_ffn_gate_w).T),
        "fc1": fc1.transpose(0, 3, 2, 1),
        "fc2": fc2.transpose(0, 2, 1, 3),
        "fc1_b": np.asarray(L0_ffn_fc1_b).reshape(EXPERTS, HID // P, P).transpose(0, 2, 1),
        "fc2_b": np.broadcast_to(np.asarray(L0_ffn_fc2_b), (EXPERTS, P, D)),
        "expert_no": np.broadcast_to(np.arange(EXPERTS, dtype=np.float32), (P, EXPERTS)),
        "before": (lane[:, None] < lane[None, :]).astype(np.float16),
    }
    nc = bacc.Bacc("TRN2", target_bir_lowering=False, num_devices=1)
    arrays = {n: np.ascontiguousarray(a) for n, a in arrays.items()}
    t = {n: nc.dram_tensor(n, a.shape, mybir.dt.from_np(a.dtype), kind="ExternalInput").ap()
         for n, a in arrays.items()}
    t["out"] = nc.dram_tensor("out", (P, TILES, D), F32, kind="ExternalOutput").ap()
    perceiver_layer(nc, t)
    got = run_bass_kernel_spmd(nc, [arrays], core_ids=[0]).results[0]["out"]
    return np.ascontiguousarray(got.transpose(1, 0, 2)).reshape(BATCH, SEQ, D)
```

```python
from contextlib import ExitStack

import numpy as np

import concourse.bass as bass
from concourse import mybir

F32 = mybir.dt.float32
F16 = mybir.dt.float16
U32 = mybir.dt.uint32
I32 = mybir.dt.int32
ALU = mybir.AluOpType
ACT = mybir.ActivationFunctionType
AX = mybir.AxisListType.X

P = 128
BATCH, SEQ, D = 2, 512, 512
CTX = 8192
TOK = BATCH * SEQ
TILES = TOK // P
SEQ_TILES = SEQ // P
KD = D // P
CHUNK = 512
CHUNKS = CTX // CHUNK
HEADS, HEAD = 16, 32
GROUPS = HEADS * HEAD // P
GH = P // HEAD
EXPERTS, TOPK, HID = 8, 2, 2048
CAP = TOPK * (TOK // EXPERTS)
CAP_TILES = CAP // P
HCHUNK = 512
HCHUNKS = HID // HCHUNK
HT = HCHUNK // P
EPS = 1e-5
W_SCALE = 64.0
P_SCALE = 4096.0
Q_SCALE = 64.0
FAR = -1e30
N_W = 5


class Arena:

    def __init__(self, tensor, words):
        self.tensor, self.words, self.at = tensor, words, 0

    def take(self, shape, dtype=F32):
        n = int(np.prod(shape))
        words = n if dtype != F16 else n // 2
        view = self.tensor[:, self.at:self.at + words]
        self.at += words
        assert self.at <= self.words, (self.at, self.words)
        if dtype != F32:
            view = view.bitcast(dtype)
        if len(shape) == 2:
            return view.rearrange("p (a b) -> p a b", a=shape[0])
        if len(shape) == 3:
            return view.rearrange("p (a b c) -> p a b c", a=shape[0], b=shape[1])
        return view


def three(pe, out, left_hi, left_lo, right_hi, right_lo, first, last):
    pe.matmul(out, left_hi, right_hi, start=first, stop=False)
    pe.matmul(out, left_hi, right_lo, start=False, stop=False)
    return pe.matmul(out, left_lo, right_hi, start=False, stop=last)


def perceiver_layer(nc, t):
    ARENA = 29 * 1024
    with ExitStack() as top:
        def sb(name, shape, dtype=F32):
            return top.enter_context(nc.sbuf_tensor(name + "_sb", shape, dtype))

        X = sb("X", [P, TILES, D])
        XN = sb("XN", [P, TILES, D])
        xt_hi = sb("xt_hi", [P, KD, TOK], F16)
        xt_lo = sb("xt_lo", [P, KD, TOK], F16)
        w_hi = sb("w_hi", [P, N_W, KD, D], F16)
        w_lo = sb("w_lo", [P, N_W, KD, D], F16)
        ident = sb("ident", [P, P])
        stats = sb("stats", [P, TILES, 6])
        mv = sb("mv", [P, TILES, 2])
        var = sb("var", [P, TILES])
        std = sb("std", [P, TILES])
        rstd = sb("rstd", [P, TILES])
        gw = sb("gw", [P, KD, EXPERTS])
        gw_s = sb("gw_s", [P, KD, EXPERTS])
        gw_hi = sb("gw_hi", [P, KD, EXPERTS], F16)
        gw_lo = sb("gw_lo", [P, KD, EXPERTS], F16)
        arena_t = sb("arena", [P, ARENA])
        banks = [top.enter_context(nc.psum_tensor(f"bank{i}", [P, 512], F32)) for i in range(8)]
        disp = nc.dram_tensor("disp", (EXPERTS * CAP, D), F32, kind="Internal").ap()
        eo_d = nc.dram_tensor("expert_out", ((EXPERTS - 1) * CAP, D), F32, kind="Internal").ap()

        shared = dict(X=X, XN=XN, xt_hi=xt_hi, xt_lo=xt_lo, w_hi=w_hi, w_lo=w_lo, ident=ident,
                      gw=gw, gw_s=gw_s, gw_hi=gw_hi, gw_lo=gw_lo, stats=stats, mv=mv, var=var,
                      std=std, rstd=rstd, banks=banks, disp=disp, eo_d=eo_d)
        used = cross_attention(nc, t, shared, Arena(arena_t, ARENA))
        nc.clear_and_free_semaphores(list(used.values()))
        nc.all_engine_barrier()
        used = retention(nc, t, shared, Arena(arena_t, ARENA))
        nc.clear_and_free_semaphores(list(used.values()))
        nc.all_engine_barrier()
        experts(nc, t, shared, Arena(arena_t, ARENA))


def wait(engine, sem, value):
    if not isinstance(value, int) or value > 0:
        engine.wait_ge(sem, value)


def norm_stats(dve, s, sem, i):
    dve.bn_stats(s["stats"][:, i, :], s["X"][:, i, :]).then_inc(sem["ln_stats"], 1)


def norm_scale(dve, s, sem, tiles, done=0, group=0):
    cols = slice(tiles[0], tiles[-1] + 1)
    for n, i in enumerate(tiles):
        dve.wait_ge(sem["ln_stats"], done + n + 1)
        dve.bn_aggr(s["mv"][:, i, :], s["stats"][:, i, :]).then_inc(sem["ln_aggr"], 1)
    dve.wait_ge(sem["ln_aggr"], done + len(tiles))
    dve.tensor_scalar(s["var"][:, cols], s["mv"][:, cols, 1], EPS, None, ALU.add).then_inc(sem["ln_var"], 1)
    dve.wait_ge(sem["ln_std"], group + 1)
    dve.reciprocal(s["rstd"][:, cols], s["std"][:, cols]).then_inc(sem["ln_rstd"], 1)


def norm_root(act, s, sem, tiles, group=0):
    cols = slice(tiles[0], tiles[-1] + 1)
    act.wait_ge(sem["ln_var"], group + 1)
    act.activation(s["std"][:, cols], s["var"][:, cols], ACT.Sqrt).then_inc(sem["ln_std"], 1)


def norm_apply(engine, s, sem, i, group=0):
    engine.wait_ge(sem["ln_rstd"], group + 1)
    engine.tensor_scalar(s["XN"][:, i, :], s["X"][:, i, :], s["mv"][:, i, 0:1], s["rstd"][:, i:i + 1],
                         ALU.subtract, ALU.mult).then_inc(sem["xn"], 1)


def norm_turn(pe, s, m, sem, i, n):
    pe.wait_ge(sem["xn"], n + 1)
    wait(pe, sem["xt_lo"], n - len(m) + 1)
    for k in range(KD):
        last = pe.transpose(m[n % len(m)][:, k, :], s["XN"][:, i, k * P:(k + 1) * P], s["ident"][:, :])
    last.then_inc(sem["xt_psum"], 1)


def norm_high(act, s, m, sem, i, n):
    act.wait_ge(sem["xt_psum"], n + 1)
    act.activation(s["xt_hi"][:, :, i * P:(i + 1) * P], m[n % len(m)][:, :, :], ACT.Copy).then_inc(sem["xt_hi"], 1)


def norm_low(dve, s, m, sem, i, n):
    dve.wait_ge(sem["xt_hi"], n + 1)
    dve.tensor_tensor(s["xt_lo"][:, :, i * P:(i + 1) * P], m[n % len(m)][:, :, :],
                      s["xt_hi"][:, :, i * P:(i + 1) * P], ALU.subtract).then_inc(sem["xt_lo"], 1)


def norm_vector(dve, s, m, sem, tiles, done=0, group=0):
    norm_scale(dve, s, sem, tiles, done, group)
    for n, i in enumerate(tiles):
        norm_apply(dve, s, sem, i, group)
        if n >= 2:
            norm_low(dve, s, m, sem, i - 2, done + n - 2)
    for n in range(len(tiles) - 2, len(tiles)):
        norm_low(dve, s, m, sem, tiles[n], done + n)


def batch_tiles(b):
    return range(b * SEQ_TILES, (b + 1) * SEQ_TILES)


def semaphores(nc, prefix, names):
    return {n: nc.alloc_semaphore(prefix + n) for n in names}


NORM_SEMS = ["ln_stats", "ln_aggr", "ln_var", "ln_std", "ln_rstd", "xn", "xt_psum", "xt_hi", "xt_lo"]


def cross_attention(nc, t, s, arena):
    X, XN, xt_hi, xt_lo = s["X"], s["XN"], s["xt_hi"], s["xt_lo"]
    LT = SEQ_TILES
    raw_w = arena.take([2, KD, D])
    qt_hi = arena.take([KD, TOK], F16)
    qt_lo = arena.take([KD, TOK], F16)
    ctx_t = arena.take([2, KD, CHUNK])
    ctx_n = arena.take([2, KD, D])
    t_hi, t_lo, n_hi, n_lo = (arena.take([2 * KD, CHUNK], F16) for _ in range(4))
    at_pt = arena.at
    prob = arena.take([2, CHUNK])
    pt_hi = arena.take([2 * 4, P], F16)
    pt_lo = arena.take([2 * 4, P], F16)
    again = Arena(arena.tensor, arena.words)
    again.at = at_pt
    ext_hi = again.take([KD, SEQ], F16)
    ext_lo = again.take([KD, SEQ], F16)
    arena.at = max(arena.at, again.at)
    ext = arena.take([2, SEQ])
    xb = arena.take([KD])
    xb_cols = arena.take([KD])
    xb_hi = arena.take([KD], F16)
    xb_lo = arena.take([KD], F16)
    ex_b = arena.take([TILES])
    ms = [arena.take([TILES]) for _ in range(2)]
    cmax, nbias, drop, alpha, rows = (arena.take([4]) for _ in range(5))
    total = arena.take([TILES])
    recip, recip_s = arena.take([TILES]), arena.take([TILES])
    zeros = arena.take([D])
    acc = XN
    bank = s["banks"]
    tp = [bank[i][:, :].rearrange("p (k n) -> p k n", k=KD) for i in range(8)]

    LN_BANKS = (tp[0], tp[1], tp[6], tp[7])
    PAIR = 2 * LT
    PAIRS = BATCH * CHUNKS // 2
    UNITS = PAIR * PAIRS
    LAST = PAIRS - 1

    def within(i, place, count=UNITS, step=PAIR):
        return not isinstance(i, int) or 0 <= step * i + place < count

    def at_end(i):
        return isinstance(i, int) and i == LAST

    def cell(i, place):
        c = (i + place // PAIR) // (CHUNKS // 2) * LT + place % LT
        return slice(c, c + 1) if isinstance(c, int) else bass.ds(c, 1)

    def tile(i, place):
        c = (i + place // PAIR) // (CHUNKS // 2) * LT + place % LT
        return c if isinstance(c, int) else bass.ds(c, 1)

    def queries(i, place):
        c = (i + place // PAIR) // (CHUNKS // 2) * LT + place % LT
        return slice(c * P, c * P + P) if isinstance(c, int) else bass.ds(c * P, P)

    def steps(engine, slot):
        for j in range(-2, PAIR):
            slot(0, j)
        with engine.Fori(1, PAIRS - 1) as i:
            for j in range(PAIR):
                slot(i, j)
        for j in range(PAIR + 1):
            slot(PAIRS - 1, j)

    def split_piece(i, place):
        ahead = place // LT + 1
        return ahead % 2, place % LT, (2 * i + ahead) * KD + place % LT, i + ahead // 2

    with ExitStack() as ctx:
        names = NORM_SEMS + [
            "x_in0", "x_in1", "x_in2", "x_in3", "x_in4", "wxt_in", "wxn_in", "xb_in",
            "ident_in", "raw_in0", "raw_in1", "raw_late0", "raw_late1",
            "wx_hi", "wx_lo", "xb_s", "xb_h", "xb_l", "ex_psum", "ex", "ex_hi", "ex_lo",
            "q_psum", "q_hi", "q_lo", "exb_psum", "exb", "init", "acc_init", "w_s", "w_h", "w_l",
            "ct_in0", "ct_in1", "cn_in0", "cn_in1", "ct_hi", "ct_lo", "cn_hi", "cn_lo",
            "score", "cmax", "mnew", "nbias", "drop", "alpha", "prob", "pt_psum", "pt_hi", "pt_lo",
            "av", "acc", "total", "recip", "recip_s", "x1", "zero", "zeroed"]
        sem = semaphores(nc, "a_", names)
        block = ctx.enter_context(nc.Block())

        @block.sync
        def _(sp):
            for n in batch_tiles(0):
                sp.dma_start(X[:, n, :], t["x"][:, n, :]).then_inc(sem[f"x_in{n}"], 16)
            sp.dma_start(s["ident"][:, :], t["ident"]).then_inc(sem["ident_in"], 16)
            sp.dma_start(raw_w[:, 0, :, :], t["wxt"]).then_inc(sem["wxt_in"], 16)
            sp.dma_start(X[:, LT:TILES, :], t["x"][:, LT:TILES, :]).then_inc(sem[f"x_in{LT}"], 16)
            sp.dma_start(raw_w[:, 1, :, :], t["wxn"]).then_inc(sem["wxn_in"], 16)
            sp.dma_start(xb[:, :], t["xb"]).then_inc(sem["xb_in"], 16)

            def rows(name, i):
                if isinstance(i, int):
                    return t[name][i]
                return t[name][bass.ds(i, 1), :, :, :].rearrange("a p k m -> (a p) k m")

            def chunk(i, parity):
                sp.dma_start(ctx_t[:, parity, :, :], rows("ctx_t", i)).then_inc(sem[f"ct_in{parity}"], 16)
                sp.dma_start(ctx_n[:, parity, :, :], rows("ctx_n", i)).then_inc(sem[f"cn_in{parity}"], 16)
            chunk(0, 0)
            chunk(1, 1)
            for n in range(2):
                sp.wait_ge(sem["wx_lo"], KD * (n + 1))
                sp.dma_start(raw_w[:, n, :, :], t["w5"][n]).then_inc(sem[f"raw_in{n}"], 16)
            with sp.Fori(1, PAIRS) as i:
                for parity in range(2):
                    for part in ("ct_hi", "ct_lo", "cn_hi", "cn_lo"):
                        sp.wait_ge(sem[part], (2 * i + parity - 1) * KD)
                    chunk(2 * i + parity, parity)
            sp.wait_ge(sem["zero"], 1)
            for n in range(EXPERTS * CAP // P):
                sp.dma_start(s["disp"][n * P:(n + 1) * P, :], zeros).then_inc(sem["zeroed"], 16)
            sp.wait_ge(sem["zeroed"], 16 * (EXPERTS * CAP // P))

        @block.gpsimd
        def _(pool):
            pool.memset(zeros, 0.0).then_inc(sem["zero"], 1)
            pool.wait_ge(sem["xt_psum"], TILES)
            pool.memset(acc[:, :, :], 0.0).then_inc(sem["acc_init"], 1)
            for n in range(N_W):
                if n == 3:
                    pool.wait_ge(sem["exb_psum"], BATCH)
                raw = raw_w[:, n % 2, :, :]
                if n < 2:
                    pool.wait_ge(sem[f"raw_in{n}"], 16)
                else:
                    pool.wait_ge(sem[f"raw_late{n % 2}"], 16 * (n // 2))
                pool.tensor_scalar(raw, raw, W_SCALE, None, ALU.mult).then_inc(sem["w_s"], 1)
                pool.wait_ge(sem["w_s"], n + 1)
                pool.tensor_copy(s["w_hi"][:, n, :, :], raw).then_inc(sem["w_h"], 1)
                pool.wait_ge(sem["w_h"], n + 1)
                pool.tensor_tensor(s["w_lo"][:, n, :, :], raw, s["w_hi"][:, n, :, :], ALU.subtract)\
                    .then_inc(sem["w_l"], 1)
                if n + 2 < N_W:
                    pool.wait_ge(sem["w_l"], n + 1)
                    pool.dma_start(raw, t["w5"][n + 2]).then_inc(sem[f"raw_late{n % 2}"], 16)

        @block.scalar
        def _(act):
            def t_high(parity, k, count, pair):
                if k == 0:
                    act.wait_ge(sem[f"ct_in{parity}"], 16 * (pair + 1))
                if k == 0:
                    wait(act, sem["score"], count - KD)
                act.activation(t_hi[:, parity * KD + k, :], ctx_t[:, parity, k, :], ACT.Copy)\
                   .then_inc(sem["ct_hi"], 1)

            def n_high(parity, k, count, pair):
                if k == 0:
                    act.wait_ge(sem[f"cn_in{parity}"], 16 * (pair + 1))
                    wait(act, sem["av"], count - KD)
                act.activation(n_hi[:, parity * KD + k, :], ctx_n[:, parity, k, :], ACT.Copy)\
                   .then_inc(sem["cn_hi"], 1)

            def w_high(n, name):
                act.wait_ge(sem[name], 16)
                for k in range(KD):
                    act.activation(s["w_hi"][:, 3 + n, k, :], raw_w[:, n, k, :], ACT.Copy, scale=W_SCALE)\
                       .then_inc(sem["wx_hi"], 1)
            norm_root(act, s, sem, batch_tiles(0), 0)
            for i in (0, 1):
                norm_high(act, s, LN_BANKS, sem, i, i)
            w_high(0, "wxt_in")
            for i in (2, 3):
                norm_high(act, s, LN_BANKS, sem, i, i)
            norm_root(act, s, sem, batch_tiles(1), 1)
            w_high(1, "wxn_in")
            act.wait_ge(sem["xb_in"], 16)
            act.activation(xb_cols[:, :], xb[:, :], ACT.Copy, scale=W_SCALE).then_inc(sem["xb_s"], 1)
            act.wait_ge(sem["xb_s"], 1)
            act.activation(xb_hi[:, :], xb_cols[:, :], ACT.Copy).then_inc(sem["xb_h"], 1)
            for b in range(BATCH):
                for e in range(KD):
                    n = b * KD + e
                    act.wait_ge(sem["ex_psum"], n + 1)
                    wait(act, sem["ex_lo"], n - 1)
                    act.activation(ext[:, n % 2, :], bank[2 + n % 2][:, :], ACT.Identity,
                                   bias=xb[:, e:e + 1], scale=1 / W_SCALE).then_inc(sem["ex"], 1)
                    act.wait_ge(sem["ex"], n + 1)
                    if b and e == 0:
                        act.wait_ge(sem["exb_psum"], b)
                    act.activation(ext_hi[:, e, :], ext[:, n % 2, :], ACT.Copy).then_inc(sem["ex_hi"], 1)
                if b == 0:
                    for i in batch_tiles(1):
                        norm_high(act, s, LN_BANKS, sem, i, i)
                for d in range(KD):
                    n = b * KD + d
                    act.wait_ge(sem["q_psum"], n + 1)
                    act.activation(qt_hi[:, d, b * SEQ:(b + 1) * SEQ], bank[4 + n % 2][:, :], ACT.Copy,
                                   scale=1 / W_SCALE).then_inc(sem["q_hi"], 1)
                if b == 0:
                    for k in range(KD):
                        t_high(0, k, k, 0)
                    for k in range(KD):
                        n_high(0, k, k, 0)
            act.wait_ge(sem["init"], 2)

            def slot(i, j):
                if within(i, j + 2 + LT):
                    t_high(*split_piece(i, j + 2))
                if within(i, j) and within(i, j + LT):
                    n_high(*split_piece(i, j))
                v = PAIR * i + j + 1
                if within(i, j + 1):
                    m = (j + 1) % 2
                    act.wait_ge(sem["pt_psum"], v + 1)
                    wait(act, sem["av"], v - 1)
                    act.activation(pt_hi[:, 4 * m:4 * m + 4, :], tp[2 + m][:, :, :], ACT.Copy,
                                   scale=P_SCALE).then_inc(sem["pt_hi"], 1)
                v = PAIR * i + j + 2
                if within(i, j + 2):
                    m, q, new = (j + 2) % 2, (j + 2) % 4, (j + 2) // LT % 2
                    act.wait_ge(sem["drop"], v + 1)
                    wait(act, sem["acc"], v - 3)
                    wait(act, sem["total"], v - 3)
                    act.activation(alpha[:, q:q + 1], drop[:, q:q + 1], ACT.Exp).then_inc(sem["alpha"], 1)
                    act.wait_ge(sem["nbias"], v + 1)
                    wait(act, sem["pt_psum"], v - 1)
                    act.activation(prob[:, m, :], bank[m][:, :], ACT.Exp, bias=nbias[:, q:q + 1],
                                   accum_out=rows[:, q:q + 1]).then_inc(sem["prob"], 1)
                if at_end(i) and j == 3:
                    norm_root(act, s, sem, batch_tiles(0), BATCH)
                if at_end(i) and j in (6, 7):
                    for n in (2 * j - 12, 2 * j - 11):
                        norm_high(act, s, tp[6:8], sem, n, TILES + n)
            steps(act, slot)

        @block.vector
        def _(dve):
            def w_low(n):
                for k in range(KD):
                    dve.wait_ge(sem["wx_hi"], n * KD + k + 1)
                    dve.scalar_tensor_tensor(out=s["w_lo"][:, 3 + n, k, :], in0=raw_w[:, n, k, :],
                                             scalar=W_SCALE, in1=s["w_hi"][:, 3 + n, k, :],
                                             op0=ALU.mult, op1=ALU.subtract).then_inc(sem["wx_lo"], 1)

            def t_low(parity, k, count, pair):
                dve.wait_ge(sem["ct_hi"], count + 1)
                dve.tensor_tensor(t_lo[:, parity * KD + k, :], ctx_t[:, parity, k, :],
                                  t_hi[:, parity * KD + k, :], ALU.subtract).then_inc(sem["ct_lo"], 1)

            def n_low(parity, k, count, pair):
                dve.wait_ge(sem["cn_hi"], count + 1)
                dve.tensor_tensor(n_lo[:, parity * KD + k, :], ctx_n[:, parity, k, :],
                                  n_hi[:, parity * KD + k, :], ALU.subtract).then_inc(sem["cn_lo"], 1)

            for i in batch_tiles(0):
                dve.wait_ge(sem[f"x_in{i}"], 16)
                norm_stats(dve, s, sem, i)
            norm_vector(dve, s, LN_BANKS, sem, batch_tiles(0))
            w_low(0)
            dve.wait_ge(sem[f"x_in{LT}"], 16)
            for i in batch_tiles(1):
                norm_stats(dve, s, sem, i)
            norm_scale(dve, s, sem, batch_tiles(1), LT, 1)
            for i in batch_tiles(1):
                norm_apply(dve, s, sem, i, 1)
            w_low(1)
            dve.wait_ge(sem["xb_h"], 1)
            dve.tensor_tensor(xb_lo[:, :], xb_cols[:, :], xb_hi[:, :], ALU.subtract).then_inc(sem["xb_l"], 1)
            dve.memset(total[:, :], 0.0).then_inc(sem["init"], 1)
            dve.memset(ms[1][:, :], FAR).then_inc(sem["init"], 1)
            for b in range(BATCH):
                for e in range(KD):
                    n = b * KD + e
                    dve.wait_ge(sem["ex_hi"], n + 1)
                    dve.tensor_tensor(ext_lo[:, e, :], ext[:, n % 2, :], ext_hi[:, e, :], ALU.subtract)\
                       .then_inc(sem["ex_lo"], 1)
                if b == 0:
                    for i in batch_tiles(1):
                        norm_low(dve, s, LN_BANKS, sem, i, i)
                for d in range(KD):
                    n = b * KD + d
                    dve.wait_ge(sem["q_hi"], n + 1)
                    dve.scalar_tensor_tensor(out=qt_lo[:, d, b * SEQ:(b + 1) * SEQ], in0=bank[4 + n % 2][:, :],
                                             scalar=1 / W_SCALE, in1=qt_hi[:, d, b * SEQ:(b + 1) * SEQ],
                                             op0=ALU.mult, op1=ALU.subtract).then_inc(sem["q_lo"], 1)
                dve.wait_ge(sem["exb_psum"], b + 1)
                dve.tensor_scalar(ex_b[:, b * LT:(b + 1) * LT], bank[6][:, b * LT:(b + 1) * LT],
                                  1 / W_SCALE, None, ALU.mult).then_inc(sem["exb"], 1)
                if b == 0:
                    for k in range(KD):
                        t_low(0, k, k, 0)
                    for k in range(KD):
                        n_low(0, k, k, 0)
            dve.wait_ge(sem["init"], 2)
            dve.wait_ge(sem["acc_init"], 1)
            dve.wait_ge(sem["exb"], BATCH)

            scales = [0]

            def scale(b, first, end):
                scales[0] += 1
                dve.wait_ge(sem["total"], UNITS // BATCH if b == 0 else UNITS - TILES + end)
                dve.reciprocal(recip[:, first:end], total[:, first:end]).then_inc(sem["recip"], 1)
                dve.wait_ge(sem["recip"], scales[0])
                dve.tensor_scalar(recip_s[:, first:end], recip[:, first:end], 1 / P_SCALE, None, ALU.mult)\
                   .then_inc(sem["recip_s"], 1)
                dve.wait_ge(sem["recip_s"], scales[0])

            def x1(n):
                dve.wait_ge(sem["acc"], UNITS // BATCH if n < LT else UNITS - TILES + n + 1)
                dve.scalar_tensor_tensor(out=X[:, n, :], in0=acc[:, n, :], scalar=recip_s[:, n:n + 1],
                                         in1=X[:, n, :], op0=ALU.mult, op1=ALU.add)\
                   .then_inc(sem["x1"], 1)

            def finish(j):
                if j == 0:
                    scale(0, 0, LT)
                if j < 2:
                    x1(2 * j)
                    x1(2 * j + 1)
                if j == 2:
                    dve.wait_ge(sem["x1"], LT)
                    for n in batch_tiles(0):
                        norm_stats(dve, s, sem, n)
                if j == 3:
                    norm_scale(dve, s, sem, batch_tiles(0), TILES, BATCH)
                if j in (4, 5):
                    for n in (2 * j - 8, 2 * j - 7):
                        norm_apply(dve, s, sem, n, BATCH)
                if j in (6, 7):
                    scale(1, j - 2, j - 1)
                    x1(j - 2)
                if j in (6, 8):
                    for n in (j - 6, j - 5):
                        norm_low(dve, s, tp[6:8], sem, n, TILES + n)
                if j == 8:
                    scale(1, j - 2, j - 1)
                    x1(j - 2)

            def slot(i, j):
                v = PAIR * i + j - 1
                if within(i, j - 1):
                    m, q = (j - 1) % 2, (j - 1) % 4
                    dve.wait_ge(sem["av"], v + 1)
                    wait(dve, sem["acc"], v - 3)
                    here = tile(i, j - 1)
                    sums = acc[:, here, :] if isinstance(here, int) else \
                        acc[:, here, :].rearrange("p a d -> p (a d)")
                    dve.scalar_tensor_tensor(out=sums, in0=sums, scalar=alpha[:, q:q + 1],
                                             in1=bank[4 + m][:, :], op0=ALU.mult, op1=ALU.add)\
                       .then_inc(sem["acc"], 1)
                    wait(dve, sem["total"], v - 3)
                    c = cell(i, j - 1)
                    dve.scalar_tensor_tensor(out=total[:, c], in0=total[:, c], scalar=alpha[:, q:q + 1],
                                             in1=rows[:, q:q + 1], op0=ALU.mult, op1=ALU.add)\
                       .then_inc(sem["total"], 1)
                if within(i, j + 2 + LT):
                    t_low(*split_piece(i, j + 2))
                if within(i, j) and within(i, j + LT):
                    n_low(*split_piece(i, j))
                v = PAIR * i + j + 2
                if within(i, j + 2):
                    m, q, new = (j + 2) % 2, (j + 2) % 4, (j + 2) // LT % 2
                    c = cell(i, j + 2)
                    dve.wait_ge(sem["score"], v + 1)
                    dve.reduce_max(cmax[:, q:q + 1], bank[m][:, :], AX).then_inc(sem["cmax"], 1)
                    dve.wait_ge(sem["cmax"], v + 1)
                    dve.tensor_scalar(ms[new][:, c], cmax[:, q:q + 1], ex_b[:, c], ms[1 - new][:, c],
                                      ALU.add, ALU.max).then_inc(sem["mnew"], 1)
                    dve.wait_ge(sem["mnew"], v + 1)
                    dve.tensor_tensor(nbias[:, q:q + 1], ex_b[:, c], ms[new][:, c], ALU.subtract)\
                       .then_inc(sem["nbias"], 1)
                    wait(dve, sem["alpha"], v - 3)
                    dve.tensor_tensor(drop[:, q:q + 1], ms[1 - new][:, c], ms[new][:, c], ALU.subtract)\
                       .then_inc(sem["drop"], 1)
                v = PAIR * i + j + 1
                if within(i, j + 1):
                    m = (j + 1) % 2
                    dve.wait_ge(sem["pt_hi"], v + 1)
                    dve.scalar_tensor_tensor(out=pt_lo[:, 4 * m:4 * m + 4, :], in0=tp[2 + m][:, :, :],
                                             scalar=P_SCALE, in1=pt_hi[:, 4 * m:4 * m + 4, :],
                                             op0=ALU.mult, op1=ALU.subtract).then_inc(sem["pt_lo"], 1)
                if at_end(i):
                    finish(j)
            steps(dve, slot)
            scale(1, TILES - 1, TILES)
            x1(TILES - 1)

        @block.tensor
        def _(pe):
            pe.wait_ge(sem["ident_in"], 16)
            for i in batch_tiles(0):
                norm_turn(pe, s, LN_BANKS, sem, i, i)
            for b in range(BATCH):
                pe.wait_ge(sem["xt_lo"], SEQ_TILES * (b + 1))
                seq = slice(b * SEQ, (b + 1) * SEQ)
                for e in range(KD):
                    n = b * KD + e
                    wait(pe, sem["ex"], n - 1)
                    for k in range(KD):
                        if n == 0:
                            pe.wait_ge(sem["wx_lo"], k + 1)
                        last = three(pe, bank[2 + n % 2][:, :], s["w_hi"][:, 3, k, e * P:(e + 1) * P],
                                     s["w_lo"][:, 3, k, e * P:(e + 1) * P], xt_hi[:, k, seq],
                                     xt_lo[:, k, seq], k == 0, k == KD - 1)
                    last.then_inc(sem["ex_psum"], 1)
                if b == 0:
                    for i in batch_tiles(1):
                        norm_turn(pe, s, LN_BANKS, sem, i, i)
                pe.wait_ge(sem["wx_lo"], 2 * KD)
                pe.wait_ge(sem["ex_lo"], KD * (b + 1))
                for d in range(KD):
                    n = b * KD + d
                    wait(pe, sem["q_lo"], n - 1)
                    for e in range(KD):
                        last = three(pe, bank[4 + n % 2][:, :], s["w_hi"][:, 4, e, d * P:(d + 1) * P],
                                     s["w_lo"][:, 4, e, d * P:(d + 1) * P], ext_hi[:, e, :],
                                     ext_lo[:, e, :], e == 0, e == KD - 1)
                    last.then_inc(sem["q_psum"], 1)
                pe.wait_ge(sem["xb_l"], 1)
                wait(pe, sem["exb"], b)
                for n in range(LT):
                    for e in range(KD):
                        last = three(pe, bank[6][:, b * LT + n:b * LT + n + 1],
                                     ext_hi[:, e, n * P:(n + 1) * P], ext_lo[:, e, n * P:(n + 1) * P],
                                     xb_hi[:, e:e + 1], xb_lo[:, e:e + 1], e == 0, e == KD - 1)
                last.then_inc(sem["exb_psum"], 1)
            pe.wait_ge(sem["q_lo"], KD)

            def slot(i, j):
                v = PAIR * i + j + 2
                if within(i, j + 2):
                    m, par = (j + 2) % 2, (j + 2) // LT % 2
                    if j % LT == LT - 2:
                        pe.wait_ge(sem["ct_lo"], v + KD)
                    wait(pe, sem["prob"], v - 1)
                    if isinstance(i, int) and i == 0 and j == 0:
                        pe.wait_ge(sem["q_lo"], BATCH * KD)
                    q = queries(i, j + 2)
                    for k in range(KD):
                        last = three(pe, bank[m][:, :], qt_hi[:, k, q], qt_lo[:, k, q],
                                     t_hi[:, par * KD + k, :], t_lo[:, par * KD + k, :],
                                     k == 0, k == KD - 1)
                    last.then_inc(sem["score"], 1)
                v = PAIR * i + j + 1
                if within(i, j + 1):
                    m = (j + 1) % 2
                    pe.wait_ge(sem["prob"], v + 1)
                    wait(pe, sem["pt_lo"], v - 1)
                    for k in range(CHUNK // P):
                        last = pe.transpose(tp[2 + m][:, k, :], prob[:, m, k * P:(k + 1) * P],
                                            s["ident"][:, :])
                    last.then_inc(sem["pt_psum"], 1)
                v = PAIR * i + j
                if within(i, j):
                    m, par = j % 2, j // LT % 2
                    if j % LT == 0:
                        pe.wait_ge(sem["cn_lo"], v + KD)
                    pe.wait_ge(sem["pt_lo"], v + 1)
                    wait(pe, sem["acc"], v - 1)
                    for k in range(CHUNK // P):
                        last = three(pe, bank[4 + m][:, :], pt_hi[:, 4 * m + k, :], pt_lo[:, 4 * m + k, :],
                                     n_hi[:, par * KD + k, :], n_lo[:, par * KD + k, :],
                                     k == 0, k == CHUNK // P - 1)
                    last.then_inc(sem["av"], 1)
                if at_end(i) and j in (5, 7):
                    if j == 5:
                        pe.wait_ge(sem["exb"], BATCH)
                    for n in (j - 5, j - 4):
                        norm_turn(pe, s, tp[6:8], sem, n, TILES + n)
            steps(pe, slot)
    return sem


def retention(nc, t, s, arena):
    X, XN, xt_hi, xt_lo, w_hi, w_lo = (s[n] for n in ("X", "XN", "xt_hi", "xt_lo", "w_hi", "w_lo"))
    QT = SEQ_TILES
    HALVES = ("q", "k")
    cos = {h: arena.take([QT, D]) for h in HALVES}
    sin = {h: arena.take([QT, D]) for h in HALVES}
    bias = arena.take([3, D])
    gate = arena.take([BATCH * GROUPS, SEQ])
    bo = gate[:, BATCH * GROUPS - 1, :]
    qk_hi = {h: arena.take([2 * GROUPS, P], F16) for h in HALVES}
    qk_lo = {h: arena.take([2 * GROUPS, P], F16) for h in HALVES}
    v_hi, v_lo = arena.take([2, D], F16), arena.take([2, D], F16)
    kn_hi, kn_lo = arena.take([D], F16), arena.take([D], F16)
    masked = arena.take([GH, GROUPS * P])
    s_hi, s_lo = arena.take([GH, GROUPS * P], F16), arena.take([GH, GROUPS * P], F16)
    gated_hi = [arena.take([GROUPS, SEQ], F16), s_hi]
    gated_lo = [arena.take([GROUPS, SEQ], F16), s_lo]
    carry = arena.take([GROUPS, P])
    state = arena.take([GROUPS, P])
    grown = arena.take([GROUPS, P])
    st_hi, st_lo = arena.take([GROUPS, P], F16), arena.take([GROUPS, P], F16)
    causal = arena.take([P])
    bg, gn_w, gn_b = (arena.take([GROUPS]) for _ in range(3))
    same_head = arena.take([P])
    hstats = arena.take([GROUPS, QT * 6])
    hmv = arena.take([GROUPS, 2])
    sums = arena.take([2, GROUPS])
    means = arena.take([2, GROUPS])
    sq, hvar, hstd, hrstd, gscale, gshift, tmp = (arena.take([GROUPS]) for _ in range(7))
    biased = {h: arena.take([D]) for h in ("q", "k", "v")}
    swapped = {h: arena.take([D]) for h in HALVES}
    turned = {h: arena.take([D]) for h in HALVES}
    ret = XN
    bank = s["banks"]
    tp = [bank[i][:, :].rearrange("p (k n) -> p k n", k=KD) for i in range(8)]
    QKV_BANK = {"q": 0, "k": 1, "v": 2}
    TURN_BANK = {"q": 3, "k": 4}
    SCORE_BANK = (3, 4, 5, 6)
    RET_BANK, STATE_BANK = 7, 5
    HEAD_BANK = (0, 2)
    OUT_BANK = (0, 1, 3, 4, 5, 6, 0, 1)
    LN_BANKS = (tp[2], tp[7], tp[4], tp[5])
    FIRST_LN_BANK = (tp[2],)
    LOGIT_BANK = 3
    LAST = QT - 1

    def pairs(row):
        return row.rearrange("p (a two) -> p a two", two=2)

    def states(i):
        return i - i // QT

    with ExitStack() as ctx:
        names = NORM_SEMS + [
            f"{a}_{b}_in{n}" for a in ("q", "k") for b in ("cos", "sin") for n in range(2)] + [
            "bias_in", "bo_in", "bg_in", "gnw_in", "gnb_in", "same_in", "causal_in", "carry_in",
            "qkv", "q_b", "k_b", "v_b", "q_cos", "k_cos", "q_swap", "k_swap", "q_turn", "k_turn",
            "v_hi", "v_lo", "kn_hi", "kn_lo", "q_tp", "k_tp", "q_hi", "k_hi", "q_lo", "k_lo",
            "gate_psum", "gate", "score", "masked", "s_hi", "s_lo_dve", "s_lo_pool", "pv", "ret",
            "growth", "grown", "state", "st_hi", "st_lo", "hstats", "hmv", "gshift",
            "gw_in", "gw_s", "gw_hi", "gw_lo", "means",
            "sums", "head_psum", "small", "hvar", "hstd", "gn", "gated", "g_hi", "g_lo",
            "wo", "x_bo", "x2"]
        sem = semaphores(nc, "r_", names)
        block = ctx.enter_context(nc.Block())

        @block.sync
        def _(sp):
            sp.dma_start(bias, t["bias_rows"]).then_inc(sem["bias_in"], 16)
            def tables(first, end):
                for h in HALVES:
                    for table, name in ((cos, "cos"), (sin, "sin")):
                        sp.dma_start(table[h][:, first:end, :], t[f"{h}_{name}"][:, first:end, :])\
                            .then_inc(sem[f"{h}_{name}_in{first}"], 16)
            tables(0, 1)
            sp.dma_start(bg, t["bg"]).then_inc(sem["bg_in"], 16)
            sp.dma_start(causal, t["causal"]).then_inc(sem["causal_in"], 16)
            sp.dma_start(carry, t["carry"]).then_inc(sem["carry_in"], 16)
            tables(1, QT)
            sp.dma_start(bo, t["bo"]).then_inc(sem["bo_in"], 16)
            sp.dma_start(gn_w, t["gn_w"]).then_inc(sem["gnw_in"], 16)
            sp.dma_start(gn_b, t["gn_b"]).then_inc(sem["gnb_in"], 16)
            sp.dma_start(same_head, t["same_head"]).then_inc(sem["same_in"], 16)
            sp.dma_start(s["gw"][:, :, :], t["gate_w"]).then_inc(sem["gw_in"], 16)

        @block.gpsimd
        def _(pool):
            def swap(i):
                for h in HALVES:
                    if i < 2:
                        pool.wait_ge(sem[f"{h}_sin_in{i}"], 16)
                    pool.wait_ge(sem[f"{h}_b"], i + 1)
                    wait(pool, sem[f"{h}_turn"], i)
                    a, b, c = pairs(swapped[h]), pairs(biased[h]), pairs(sin[h][:, i % QT, :])
                    for o in range(2):
                        pool.tensor_tensor(a[:, :, o], b[:, :, 1 - o], c[:, :, o], ALU.mult)\
                            .then_inc(sem[f"{h}_swap"], 1)

            def low(i):
                wait(pool, sem["pv"], i)
                for j in range(2):
                    pool.wait_ge(sem["s_hi"], GH * i + j + 1)
                    pool.tensor_tensor(s_lo[:, j, :], masked[:, j, :], s_hi[:, j, :], ALU.subtract)\
                        .then_inc(sem["s_lo_pool"], 1)

            def decay(i):
                c = states(i)
                if i == 0:
                    pool.wait_ge(sem["carry_in"], 16)
                pool.wait_ge(sem["grown"], c + 1)
                wait(pool, sem["st_lo"], c)
                pool.tensor_tensor(state, grown, carry, ALU.mult).then_inc(sem["state"], 1)

            def out_bias(i):
                if i == 0:
                    pool.wait_ge(sem["bo_in"], 16)
                if i >= QT:
                    pool.wait_ge(sem["xn"], i - QT + 1)
                pool.tensor_tensor(X[:, i, :], X[:, i, :], bo, ALU.add).then_inc(sem["x_bo"], 1)

            swap(0)
            for i in range(TILES):
                low(i)
                if i + 1 < TILES:
                    swap(i + 1)
                if i % QT < LAST:
                    decay(i)
                if i < TILES // 2:
                    out_bias(2 * i)
                    out_bias(2 * i + 1)
        @block.scalar
        def _(act):

            def v_high(i):
                act.wait_ge(sem["v_b"], i + 1)
                wait(act, sem["pv"], i - 1)
                wait(act, sem["growth"], states(i - 1) if i else 0)
                act.activation(v_hi[:, i % 2, :], biased["v"], ACT.Copy).then_inc(sem["v_hi"], 1)

            def kn_high(i):
                if i % QT < LAST:
                    act.wait_ge(sem["k_turn"], i + 1)
                    wait(act, sem["growth"], states(i))
                    act.activation(kn_hi, turned["k"], ACT.Copy).then_inc(sem["kn_hi"], 1)

            def qk_high(i):
                par = i % 2 * GROUPS
                for h in HALVES:
                    act.wait_ge(sem[f"{h}_tp"], i + 1)
                    wait(act, sem["pv"], i - 1)
                    act.activation(qk_hi[h][:, par:par + GROUPS, :], tp[TURN_BANK[h]][:, :, :], ACT.Copy)\
                       .then_inc(sem[f"{h}_hi"], 1)

            def gates(i):
                if i == 0:
                    act.wait_ge(sem["bg_in"], 16)
                if i == TILES - 1:
                    act.wait_ge(sem["x_bo"], TILES)
                act.wait_ge(sem["gate_psum"], i + 1)
                act.activation(gate[:, i, :], bank[QKV_BANK["q"]][:, :], ACT.Silu,
                               bias=bg[:, i % GROUPS:i % GROUPS + 1], scale=1 / W_SCALE).then_inc(sem["gate"], 1)

            def result(i):
                act.wait_ge(sem["pv"], i + 1)
                if i == QT:
                    act.wait_ge(sem["xt_psum"], QT)
                b, k = i // QT, i % QT
                act.activation(ret[:, b * GROUPS:(b + 1) * GROUPS, k * P:(k + 1) * P], tp[RET_BANK][:, :, :],
                               ACT.Copy, scale=1 / Q_SCALE).then_inc(sem["ret"], 1)

            def state_high(i):
                act.wait_ge(sem["state"], states(i) + 1)
                act.activation(st_hi, state, ACT.Copy).then_inc(sem["st_hi"], 1)

            def head_root(b):
                act.wait_ge(sem["hvar"], b + 1)
                act.activation(hstd, hvar, ACT.Sqrt).then_inc(sem["hstd"], 1)
                act.wait_ge(sem["gshift"], b + 1)

            def gated_high(b, groups):
                for g in groups:
                    n = b * GROUPS + g
                    act.activation(ret[:, n, :], ret[:, n, :], ACT.Identity, bias=gshift[:, g:g + 1],
                                   scale=gscale[:, g:g + 1]).then_inc(sem["gn"], 1)
                for g in groups:
                    n = b * GROUPS + g
                    act.wait_ge(sem["gated"], n + 1)
                    act.activation(gated_hi[b][:, g, :], ret[:, n, :], ACT.Copy).then_inc(sem["g_hi"], 1)

            norm_root(act, s, sem, batch_tiles(1))
            gates(0)
            v_high(0)
            qk_high(0)
            kn_high(0)
            for i in range(TILES):
                for j in range(GH):
                    act.wait_ge(sem["masked"], GH * i + j + 1)
                    wait(act, sem["pv"], i)
                    act.activation(s_hi[:, j, :], masked[:, j, :], ACT.Copy).then_inc(sem["s_hi"], 1)
                if i == QT + 1:
                    head_root(0)
                    gated_high(0, (0, 1))
                if i == QT + 2:
                    gated_high(0, (2, 3))
                if i < 2:
                    norm_high(act, s, FIRST_LN_BANK, sem, QT + 2 * i, 2 * i)
                result(i)
                if i < 2:
                    norm_high(act, s, FIRST_LN_BANK, sem, QT + 2 * i + 1, 2 * i + 1)
                if i + 1 < TILES:
                    v_high(i + 1)
                if i % QT < LAST:
                    state_high(i)
                if i + 1 < TILES:
                    qk_high(i + 1)
                    kn_high(i + 1)
                    gates(i + 1)
            head_root(BATCH - 1)
            gated_high(BATCH - 1, range(GROUPS))
            act.wait_ge(sem["gw_in"], 16)
            act.activation(s["gw_s"][:, :, :], s["gw"][:, :, :], ACT.Copy, scale=W_SCALE).then_inc(sem["gw_s"], 1)
            act.wait_ge(sem["gw_s"], 1)
            act.activation(s["gw_hi"][:, :, :], s["gw_s"][:, :, :], ACT.Copy).then_inc(sem["gw_hi"], 1)

            def highs(*tiles):
                for i in tiles:
                    norm_high(act, s, LN_BANKS, sem, i, QT + i)
            norm_root(act, s, sem, batch_tiles(0), 1)
            norm_root(act, s, sem, (4, 5), 2)
            highs(0, 1)
            norm_root(act, s, sem, (6,), 3)
            highs(2, 3)
            norm_root(act, s, sem, (7,), 4)
            highs(4, 5, 6, 7)

        @block.vector
        def _(dve):
            for i in batch_tiles(1):
                norm_stats(dve, s, sem, i)
            small = [0]

            def link(ins):
                small[0] += 1
                ins.then_inc(sem["small"], 1)
                dve.wait_ge(sem["small"], small[0])

            def biases(i, h):
                if i == 0 and h == "q":
                    dve.wait_ge(sem["bias_in"], 16)
                dve.wait_ge(sem["qkv"], 3 * i + "qkv".index(h) + 1)
                if h == "v":
                    wait(dve, sem["v_lo"], i)
                else:
                    wait(dve, sem[f"{h}_swap"], 2 * i)
                    wait(dve, sem[f"{h}_cos"], i)
                dve.scalar_tensor_tensor(out=biased[h], in0=bank[QKV_BANK[h]][:, :], scalar=1 / W_SCALE,
                                         in1=bias[:, "qkv".index(h), :], op0=ALU.mult, op1=ALU.add)\
                   .then_inc(sem[f"{h}_b"], 1)

            def cosine(i, h):
                if i < 2:
                    dve.wait_ge(sem[f"{h}_cos_in{i}"], 16)
                dve.wait_ge(sem[f"{h}_b"], i + 1)
                wait(dve, sem[f"{h}_tp"], i)
                if h == "k":
                    wait(dve, sem["kn_lo"], states(i))
                dve.tensor_tensor(turned[h], biased[h], cos[h][:, i % QT, :], ALU.mult)\
                   .then_inc(sem[f"{h}_cos"], 1)

            def turn(i, h):
                dve.wait_ge(sem[f"{h}_swap"], 2 * i + 2)
                dve.wait_ge(sem[f"{h}_cos"], i + 1)
                dve.tensor_tensor(turned[h], turned[h], swapped[h], ALU.add).then_inc(sem[f"{h}_turn"], 1)

            def v_low(i):
                dve.wait_ge(sem["v_hi"], i + 1)
                dve.tensor_tensor(v_lo[:, i % 2, :], biased["v"], v_hi[:, i % 2, :], ALU.subtract)\
                   .then_inc(sem["v_lo"], 1)

            def kn_low(i):
                if i % QT < LAST:
                    dve.wait_ge(sem["kn_hi"], states(i) + 1)
                    dve.tensor_tensor(kn_lo, turned["k"], kn_hi, ALU.subtract).then_inc(sem["kn_lo"], 1)

            def qk_low(i):
                par = i % 2 * GROUPS
                for h in HALVES:
                    dve.wait_ge(sem[f"{h}_hi"], i + 1)
                    dve.tensor_tensor(qk_lo[h][:, par:par + GROUPS, :], tp[TURN_BANK[h]][:, :, :],
                                      qk_hi[h][:, par:par + GROUPS, :], ALU.subtract).then_inc(sem[f"{h}_lo"], 1)

            def mask(i):
                if i == 0:
                    dve.wait_ge(sem["causal_in"], 16)
                wait(dve, sem["s_lo_dve"], 2 * i)
                wait(dve, sem["s_lo_pool"], 2 * i)
                dve.wait_ge(sem["score"], i + 1)
                for j in range(GH):
                    dve.tensor_tensor(masked[:, j, :].rearrange("p (g n) -> p g n", g=GROUPS),
                                      tp[SCORE_BANK[j]][:, :, :],
                                      causal.unsqueeze(1).to_broadcast([P, GROUPS, P]), ALU.mult)\
                       .then_inc(sem["masked"], 1)
                wait(dve, sem["pv"], i)
                for j in range(2, GH):
                    dve.wait_ge(sem["s_hi"], GH * i + j + 1)
                    dve.tensor_tensor(s_lo[:, j, :], masked[:, j, :], s_hi[:, j, :], ALU.subtract)\
                       .then_inc(sem["s_lo_dve"], 1)

            def grow(i):
                c = states(i)
                dve.wait_ge(sem["growth"], c + 1)
                wait(dve, sem["state"], c)
                if i % QT == 0:
                    dve.tensor_copy(grown, tp[STATE_BANK][:, :, :]).then_inc(sem["grown"], 1)
                else:
                    dve.tensor_tensor(grown, tp[STATE_BANK][:, :, :], state, ALU.add).then_inc(sem["grown"], 1)

            def state_low(i):
                dve.wait_ge(sem["st_hi"], states(i) + 1)
                dve.tensor_tensor(st_lo, state, st_hi, ALU.subtract).then_inc(sem["st_lo"], 1)

            def tile_stats(i):
                dve.wait_ge(sem["ret"], i + 1)
                b, k = i // QT, i % QT
                wait(dve, sem["hmv"], b * GROUPS)
                for g in range(GROUPS):
                    dve.bn_stats(hstats[:, g, k * 6:(k + 1) * 6], ret[:, b * GROUPS + g, k * P:(k + 1) * P])\
                       .then_inc(sem["hstats"], 1)

            def head_sums(b):
                for g in range(GROUPS):
                    dve.wait_ge(sem["hstats"], ((b + 1) * QT - 1) * GROUPS + g + 1)
                    dve.bn_aggr(hmv[:, g, :], hstats[:, g, :]).then_inc(sem["hmv"], 1)
                dve.wait_ge(sem["hmv"], (b + 1) * GROUPS)
                link(dve.tensor_tensor(sq, hmv[:, :, 0], hmv[:, :, 0], ALU.mult))
                link(dve.tensor_copy(sums[:, 0, :], hmv[:, :, 0]))
                dve.tensor_tensor(sums[:, 1, :], sq, hmv[:, :, 1], ALU.add).then_inc(sem["sums"], 1)

            def head_averages(b):
                dve.wait_ge(sem["head_psum"], b + 1)
                dve.tensor_copy(means, bank[HEAD_BANK[b]][:, 0:2 * GROUPS].rearrange("p (a g) -> p a g", a=2))\
                   .then_inc(sem["means"], 1)

            def group_norm(b):
                dve.wait_ge(sem["means"], b + 1)
                link(dve.tensor_tensor(sq, means[:, 0, :], means[:, 0, :], ALU.mult))
                link(dve.tensor_tensor(tmp, means[:, 1, :], sq, ALU.subtract))
                dve.tensor_scalar(hvar, tmp, EPS, None, ALU.add).then_inc(sem["hvar"], 1)
                dve.wait_ge(sem["hstd"], b + 1)
                link(dve.reciprocal(hrstd, hstd))
                if b == 0:
                    dve.wait_ge(sem["gnw_in"], 16)
                    dve.wait_ge(sem["gnb_in"], 16)
                link(dve.tensor_tensor(gscale, gn_w, hrstd, ALU.mult))
                link(dve.tensor_tensor(tmp, means[:, 0, :], gscale, ALU.mult))
                dve.tensor_tensor(gshift, gn_b, tmp, ALU.subtract).then_inc(sem["gshift"], 1)

            def gated(b, groups):
                for g in groups:
                    n = b * GROUPS + g
                    dve.wait_ge(sem["gate"], n + 1)
                    dve.wait_ge(sem["gn"], n + 1)
                    dve.tensor_tensor(ret[:, n, :], ret[:, n, :], gate[:, n, :], ALU.mult)\
                       .then_inc(sem["gated"], 1)
                for g in groups:
                    n = b * GROUPS + g
                    dve.wait_ge(sem["g_hi"], n + 1)
                    dve.tensor_tensor(gated_lo[b][:, g, :], ret[:, n, :], gated_hi[b][:, g, :], ALU.subtract)\
                       .then_inc(sem["g_lo"], 1)

            def residual(i):
                dve.wait_ge(sem["wo"], i + 1)
                dve.wait_ge(sem["x_bo"], i + 1)
                dve.scalar_tensor_tensor(out=X[:, i, :], in0=bank[OUT_BANK[i]][:, :], scalar=1 / W_SCALE,
                                         in1=X[:, i, :], op0=ALU.mult, op1=ALU.add).then_inc(sem["x2"], 1)

            def project_qk(i):
                for h in HALVES:
                    biases(i, h)
                for h in HALVES:
                    cosine(i, h)

            def project_v(i):
                for h in HALVES:
                    turn(i, h)
                biases(i, "v")
                v_low(i)
            norm_scale(dve, s, sem, batch_tiles(1))
            project_qk(0)
            project_v(0)
            qk_low(0)
            for i in batch_tiles(1):
                norm_apply(dve, s, sem, i)
            kn_low(0)
            for i in range(TILES):
                mask(i)
                if i == QT + 1:
                    group_norm(0)
                if i + 1 < TILES:
                    project_qk(i + 1)
                if i == QT:
                    head_sums(0)
                if i == QT + 1:
                    gated(0, (0, 1))
                if i == QT + 2:
                    gated(0, (2, 3))
                if i < 2:
                    norm_low(dve, s, FIRST_LN_BANK, sem, QT + 2 * i, 2 * i)
                if i and i != QT:
                    tile_stats(i - 1)
                if i % QT < LAST:
                    grow(i)
                if i < 2:
                    norm_low(dve, s, FIRST_LN_BANK, sem, QT + 2 * i + 1, 2 * i + 1)
                if i + 1 < TILES:
                    project_v(i + 1)
                if i == QT:
                    head_averages(0)
                if i % QT < LAST:
                    state_low(i)
                if i + 1 < TILES:
                    qk_low(i + 1)
                    kn_low(i + 1)
                if i == LAST:
                    tile_stats(i)
            residual(0)
            tile_stats(TILES - 1)
            head_sums(1)
            residual(1)
            head_averages(1)
            group_norm(1)
            gated(1, range(GROUPS))
            for i in (2, 3):
                residual(i)

            def lows(*tiles):
                for i in tiles:
                    norm_low(dve, s, LN_BANKS, sem, i, QT + i)

            def stats(*tiles):
                for i in tiles:
                    dve.wait_ge(sem["x2"], i + 1)
                    norm_stats(dve, s, sem, i)
            def scaled(tiles, done, group):
                norm_scale(dve, s, sem, tiles, done, group)
                for i in tiles:
                    norm_apply(dve, s, sem, i, group)
            dve.wait_ge(sem["gw_hi"], 1)
            dve.tensor_tensor(s["gw_lo"][:, :, :], s["gw_s"][:, :, :], s["gw_hi"][:, :, :], ALU.subtract)\
               .then_inc(sem["gw_lo"], 1)
            stats(0, 1, 2, 3)
            scaled(batch_tiles(0), QT, 1)
            residual(4)
            stats(4)
            residual(5)
            stats(5)
            scaled((4, 5), 2 * QT, 2)
            residual(6)
            stats(6)
            lows(0)
            scaled((6,), 2 * QT + 2, 3)
            lows(1)
            residual(7)
            stats(7)
            lows(2)
            scaled((7,), 2 * QT + 3, 4)
            lows(3, 4, 5, 6, 7)

        @block.tensor
        def _(pe):
            def project(i, h):
                n = "qkv".index(h)
                wait(pe, sem["xt_lo"], i - QT + 1)
                if h == "v" and 1 <= i <= 2:
                    pe.wait_ge(sem["xt_lo"], 2 * i)
                wait(pe, sem[f"{h}_b"], i)
                if h == "q":
                    wait(pe, sem["gate"], i)
                for k in range(KD):
                    last = three(pe, bank[QKV_BANK[h]][:, :], xt_hi[:, k, i * P:(i + 1) * P],
                                 xt_lo[:, k, i * P:(i + 1) * P], w_hi[:, n, k, :], w_lo[:, n, k, :],
                                 k == 0, k == KD - 1)
                last.then_inc(sem["qkv"], 1)

            def turn(i):
                for h in HALVES:
                    pe.wait_ge(sem[f"{h}_turn"], i + 1)
                    wait(pe, sem["masked"], GH * i)
                    for g in range(GROUPS):
                        last = pe.transpose(tp[TURN_BANK[h]][:, g, :], turned[h][:, g * P:(g + 1) * P],
                                            s["ident"][:, :])
                    last.then_inc(sem[f"{h}_tp"], 1)

            def gates(i):
                b, g = i // GROUPS, i % GROUPS
                pe.wait_ge(sem["q_b"], i + 1)
                if i == QT + 1:
                    pe.wait_ge(sem["means"], 1)
                if i == QT:
                    pe.wait_ge(sem["xt_lo"], QT)
                for k in range(KD):
                    last = three(pe, bank[QKV_BANK["q"]][:, :], w_hi[:, 3, k, g * P:(g + 1) * P],
                                 w_lo[:, 3, k, g * P:(g + 1) * P], xt_hi[:, k, b * SEQ:(b + 1) * SEQ],
                                 xt_lo[:, k, b * SEQ:(b + 1) * SEQ], k == 0, k == KD - 1)
                last.then_inc(sem["gate_psum"], 1)

            def scores(i):
                pe.wait_ge(sem["q_lo"], i + 1)
                pe.wait_ge(sem["k_lo"], i + 1)
                wait(pe, sem["grown"], states(i))
                par = i % 2 * GROUPS
                for g in range(GROUPS):
                    for p in range(3):
                        for j in range(GH):
                            keys = (qk_lo if p == 2 else qk_hi)["k"]
                            queries = (qk_lo if p == 1 else qk_hi)["q"]
                            rows = slice(j * HEAD, (j + 1) * HEAD)
                            last = pe.matmul(bank[SCORE_BANK[j]][:, g * P:(g + 1) * P], keys[rows, par + g, :],
                                             queries[rows, par + g, :], start=(p == 0), stop=(p == 2))
                last.then_inc(sem["score"], 1)

            def values(i):
                if i % QT:
                    pe.wait_ge(sem["st_lo"], states(i))
                pe.wait_ge(sem["v_lo"], i + 1)
                pe.wait_ge(sem["s_lo_dve"], 2 * i + 2)
                pe.wait_ge(sem["s_lo_pool"], 2 * i + 2)
                wait(pe, sem["ret"], i)
                par = i % 2 * GROUPS
                for g in range(GROUPS):
                    cols = slice(g * P, (g + 1) * P)
                    if i % QT:
                        three(pe, bank[RET_BANK][:, cols], st_hi[:, g, :], st_lo[:, g, :],
                              qk_hi["q"][:, par + g, :], qk_lo["q"][:, par + g, :], True, False)
                    for p in range(3):
                        for j in range(GH):
                            v = (v_lo if p == 2 else v_hi)[:, i % 2, (GH * g + j) * HEAD:(GH * g + j + 1) * HEAD]
                            last = pe.matmul(bank[RET_BANK][j * HEAD:(j + 1) * HEAD, cols], v,
                                             (s_lo if p == 1 else s_hi)[:, j, cols],
                                             start=(i % QT == 0 and p == 0), stop=(p == 2))
                last.then_inc(sem["pv"], 1)

            def growth(i):
                pe.wait_ge(sem["kn_lo"], states(i) + 1)
                pe.wait_ge(sem["masked"], GH * (i + 1))
                for g in range(GROUPS):
                    cols = slice(g * P, (g + 1) * P)
                    last = three(pe, bank[STATE_BANK][:, cols], kn_hi[:, cols], kn_lo[:, cols],
                                 v_hi[:, i % 2, cols], v_lo[:, i % 2, cols], True, True)
                last.then_inc(sem["growth"], 1)

            def head_means(b):
                if b == 0:
                    pe.wait_ge(sem["same_in"], 16)
                if b:
                    pe.wait_ge(sem["v_b"], TILES)
                else:
                    pe.wait_ge(sem["q_b"], QT + 2)
                pe.wait_ge(sem["sums"], b + 1)
                pe.matmul(bank[HEAD_BANK[b]][:, 0:2 * GROUPS], same_head, sums.rearrange("p a g -> p (a g)"),
                          start=True, stop=True).then_inc(sem["head_psum"], 1)

            def out(i):
                b, c = i // QT, i % QT
                pe.wait_ge(sem["g_lo"], (b + 1) * GROUPS)
                if i == 0:
                    pe.wait_ge(sem["gate"], TILES)
                if i == 1:
                    pe.wait_ge(sem["k_b"], TILES)
                if i == 2:
                    pe.wait_ge(sem["masked"], GH * TILES)
                if i >= 6:
                    pe.wait_ge(sem["x2"], i - 5)
                for g in range(GROUPS):
                    last = three(pe, bank[OUT_BANK[i]][:, :], gated_hi[b][:, g, c * P:(c + 1) * P],
                                 gated_lo[b][:, g, c * P:(c + 1) * P], w_hi[:, 4, g, :], w_lo[:, 4, g, :],
                                 g == 0, g == GROUPS - 1)
                last.then_inc(sem["wo"], 1)

            for h in ("q", "k", "v"):
                project(0, h)
            gates(0)
            turn(0)
            for i in range(TILES):
                scores(i)
                if i + 1 < TILES:
                    project(i + 1, "q")
                    project(i + 1, "k")
                    if i < 2:
                        pe.wait_ge(sem["v_b"], i + 1)
                        norm_turn(pe, s, FIRST_LN_BANK, sem, QT + 2 * i, 2 * i)
                else:
                    out(0)
                values(i)
                if i < 2:
                    norm_turn(pe, s, FIRST_LN_BANK, sem, QT + 2 * i + 1, 2 * i + 1)
                if i % QT < LAST:
                    growth(i)
                if i + 1 < TILES:
                    project(i + 1, "v")
                if i == QT:
                    head_means(0)
                if i + 1 < TILES:
                    turn(i + 1)
                    gates(i + 1)
            out(1)
            head_means(1)
            out(2)
            out(3)
            out(4)
            out(5)

            def turns(*tiles):
                for i in tiles:
                    if i == 2:
                        pe.wait_ge(sem["x2"], 5)
                    norm_turn(pe, s, LN_BANKS, sem, i, QT + i)

            def logits(*tiles):
                for i in tiles:
                    if i == 0:
                        pe.wait_ge(sem["gw_lo"], 1)
                    pe.wait_ge(sem["xt_lo"], QT + i + 1)
                    for k in range(KD):
                        three(pe, bank[LOGIT_BANK][:, i * EXPERTS:(i + 1) * EXPERTS],
                              xt_hi[:, k, i * P:(i + 1) * P], xt_lo[:, k, i * P:(i + 1) * P],
                              s["gw_hi"][:, k, :], s["gw_lo"][:, k, :], k == 0, k == KD - 1)
            pe.wait_ge(sem["means"], BATCH)
            pe.wait_ge(sem["ret"], TILES)
            out(6)
            turns(0, 1)
            out(7)
            turns(2, 3, 4, 5)
            logits(0, 1)
            turns(6)
            logits(2)
            turns(7)
            logits(3, 4, 5, 6, 7)
    return sem


def experts(nc, t, s, arena):
    X, XN, xt_hi, xt_lo = s["X"], s["XN"], s["xt_hi"], s["xt_lo"]
    PICKS = TOPK * TILES
    raw_t = arena.take([2, KD, HCHUNK])
    raw_n = arena.take([2, HT, D])
    t_hi, t_lo, n_hi, n_lo = (arena.take([2 * KD, HCHUNK], F16) for _ in range(4))
    at_hidden = arena.at
    hidden = arena.take([2, HT * CAP])
    h_hi = arena.take([2 * HT, CAP], F16)
    h_lo = arena.take([2 * HT, CAP], F16)
    de = arena.take([CAP_TILES, D])
    de_hi = arena.take([KD, CAP], F16)
    de_lo = arena.take([KD, CAP], F16)
    at_eo = arena.at
    eo = arena.take([CAP_TILES, D])
    b1 = arena.take([HID // P])
    b2 = arena.take([D])
    number = arena.take([EXPERTS])
    before = arena.take([P], F16)
    ones = arena.take([P], F16)
    logits, shifted, raised, score = (arena.take([TILES, EXPERTS]) for _ in range(4))
    top8 = arena.take([TILES, 8])
    top8_at = arena.take([TILES, 8]).bitcast(U32)
    peak, mass, mass_r, pair, pair_r = (arena.take([TILES]) for _ in range(5))
    expert = arena.take([TOPK, TILES])
    chosen = arena.take([PICKS, EXPERTS])
    chosen_h = arena.take([PICKS, EXPERTS], F16)
    spread = arena.take([PICKS, EXPERTS])
    loc, valid, flat, far = (arena.take([PICKS]) for _ in range(4))
    weight = arena.take([TOPK, TILES])
    to_slot = arena.take([PICKS]).bitcast(U32)
    last_slot = arena.take([TILES])
    last_weight = arena.take([TILES])
    in_last = arena.take([PICKS])
    slot_no = arena.take([CAP])
    over = Arena(arena.tensor, arena.words)
    over.at = at_hidden
    xn_hi, xn_lo = over.take([TILES, D], F16), over.take([TILES, D], F16)
    over.at = at_eo
    picked = over.take([TILES, CAP], F16)

    def as_tiles(w):
        return w.rearrange("p n k d -> p (n k d)")[:, 0:2 * TILES * D].bitcast(F32)\
            .rearrange("p (i d) -> p i d", d=D)
    got = [as_tiles(s["w_hi"][:, :, :, :]), as_tiles(s["w_lo"][:, :, :, :])]
    taken = XN[:, 0:TILES * CAP // D, :].rearrange("p n d -> p (n d)").rearrange("p (i c) -> p i c", c=CAP)
    taken_t = XN[:, TILES * CAP // D:TILES * CAP // D + 2, :].rearrange("p n d -> p (n d)").bitcast(F16)\
        .rearrange("p (a n) -> p a n", a=CAP_TILES)
    eo_hi = XN[:, 6, :].bitcast(F16).rearrange("p (a d) -> p a d", a=CAP_TILES)
    eo_lo = XN[:, 7, :].bitcast(F16).rearrange("p (a d) -> p a d", a=CAP_TILES)
    bank = s["banks"]
    tp = [bank[i][:, :].rearrange("p (k n) -> p k n", k=KD) for i in range(8)]
    BACK_BANK = (0, 1, 2, 3, 6, 7, 4, 5)
    LOGIT_BANK = 3
    CHUNKS_ALL = EXPERTS * HCHUNKS
    SLOTS = EXPERTS * CAP
    FAR_SLOT = 2 * SLOTS

    def within(e, place):
        return not isinstance(e, int) or 0 <= HCHUNKS * e + place < CHUNKS_ALL

    def steps(engine, slot):
        for c in range(-1, HCHUNKS):
            slot(0, c)
        with engine.Fori(1, EXPERTS - 1) as e:
            for c in range(HCHUNKS):
                slot(e, c)
        for c in range(HCHUNKS + 1):
            slot(EXPERTS - 1, c)

    with ExitStack() as ctx:
        names = [
            "number_in", "before_in", "ones",
            "small", "raised", "expd", "top", "top_at", "valid", "chosen", "loc_psum", "routed", "scattered",
            "t_in0", "t_in1", "n_in0", "n_in1", "b1_in", "b2_in", "de_in", "de_tp", "de_hi", "de_lo",
            "t_hi", "t_lo", "n_hi", "n_lo", "fc1", "relu", "h_hi", "h_lo", "fc2", "eo", "eo_out",
            "slot_in", "xn_hi", "xn_lo", "picked", "first", "first_hi", "first_lo", "got_zero",
            "taken", "taken_psum", "taken_t", "got0", "got1", "half", "most", "last_hi", "last_lo", "back",
            "sum", "out", "fc2_half"]
        sem = semaphores(nc, "e_", names)
        block = ctx.enter_context(nc.Block())

        @block.sync
        def _(sp):
            def at(a, i):
                if isinstance(i, int):
                    return a[i]
                a = a[bass.ds(i, 1)]
                return a.rearrange("a p n -> (a p) n") if len(a.shape) == 3 else \
                    a.rearrange("a p k n -> (a p) k n")

            def weights(e, c, part):
                u = HCHUNKS * e + c
                name, raw = (("t", raw_t), ("n", raw_n))[part]
                wait(sp, sem[name + "_hi"], (u - 1) * KD)
                wait(sp, sem[name + "_lo"], (u - 1) * KD)
                sp.dma_start(raw[:, c % 2], at(t[("fc1", "fc2")[part]], u)).then_inc(sem[f"{name}_in{c % 2}"], 16)

            def next_tokens(e):
                wait(sp, sem["de_tp"], CAP_TILES * e)
                src = s["disp"].rearrange("(e a p) d -> e p a d", p=P, a=CAP_TILES)
                sp.dma_start(de, at(src, e + 1)).then_inc(sem["de_in"], 16)

            def bias1(e):
                wait(sp, sem["relu"], HT * HCHUNKS * e)
                sp.dma_start(b1, at(t["fc1_b"], e)).then_inc(sem["b1_in"], 16)

            def store(e):
                sp.wait_ge(sem["eo"], CAP_TILES * (e + 1))
                dst = s["eo_d"].rearrange("(e a p) d -> e p a d", p=P, a=CAP_TILES)
                sp.dma_start(at(dst, e), eo).then_inc(sem["eo_out"], 16)

            def bias2(e):
                wait(sp, sem["eo"], CAP_TILES * e)
                sp.dma_start(b2, at(t["fc2_b"], e)).then_inc(sem["b2_in"], 16)

            weights(0, 0, 0)
            sp.dma_start(number, t["expert_no"]).then_inc(sem["number_in"], 16)
            sp.dma_start(before, t["before"]).then_inc(sem["before_in"], 16)
            sp.dma_start(slot_no, t["slot_no"]).then_inc(sem["slot_in"], 16)
            weights(0, 1, 0)
            weights(0, 0, 1)
            bias1(0)
            weights(0, 1, 1)
            bias2(0)
            for c in range(2, HCHUNKS):
                weights(0, c, 0)
                weights(0, c, 1)
            sp.wait_ge(sem["scattered"], 16 * PICKS)
            next_tokens(0)

            def step(e, last):
                for c in range(HCHUNKS):
                    weights(e, c, 0)
                    weights(e, c, 1)
                    if c == 1:
                        bias1(e)
                    if c == 2:
                        store(e - 1)
                        bias2(e)
                if not last:
                    next_tokens(e)
            with sp.Fori(1, EXPERTS - 1) as e:
                step(e, False)
            step(EXPERTS - 1, True)
            for i in range(TILES):
                sp.wait_ge(sem["sum"], i + 1)
                sp.dma_start(t["out"][:, i, :], X[:, i, :]).then_inc(sem["out"], 16)
            sp.wait_ge(sem["out"], 16 * TILES)

        @block.gpsimd
        def _(pool):
            pool.memset(ones, 1.0).then_inc(sem["ones"], 1)
            for i in range(TILES):
                pool.wait_ge(sem["xn_hi"], i + 1)
                pool.tensor_tensor(xn_lo[:, i, :], XN[:, i, :], xn_hi[:, i, :], ALU.subtract)\
                    .then_inc(sem["xn_lo"], 1)
            pool.wait_ge(sem["routed"], 1)
            for n in range(PICKS):
                pool.indirect_dma_start(
                    out=s["disp"], out_offset=bass.IndirectOffsetOnAxis(ap=to_slot[:, n:n + 1], axis=0),
                    in_=XN[:, n % TILES, :], in_offset=None, bounds_check=SLOTS - 1, oob_is_err=False)\
                    .then_inc(sem["scattered"], 16)
            for k in range(TOPK):
                pool.memset(got[k], 0.0).then_inc(sem["got_zero"], 1)
            pool.wait_ge(sem["got_zero"], TOPK)
            pool.wait_ge(sem["eo_out"], 16 * (EXPERTS - 1))
            for k in range(TOPK):
                for i in range(TILES):
                    n = k * TILES + i
                    pool.indirect_dma_start(
                        out=got[k][:, i, :], out_offset=None, in_=s["eo_d"],
                        in_offset=bass.IndirectOffsetOnAxis(ap=to_slot[:, n:n + 1], axis=0),
                        bounds_check=SLOTS - CAP - 1, oob_is_err=False).then_inc(sem[f"got{k}"], 16)

        @block.scalar
        def _(act):
            act.wait_ge(sem["raised"], 1)
            act.activation(raised, shifted, ACT.Exp).then_inc(sem["expd"], 1)
            for i in range(TILES):
                act.activation(xn_hi[:, i, :], XN[:, i, :], ACT.Copy).then_inc(sem["xn_hi"], 1)

            def t_high(e, place):
                par = place % 2
                act.wait_ge(sem[f"t_in{par}"], 16 * (HCHUNKS // 2 * e + place // 2 + 1))
                wait(act, sem["fc1"], 2 * (HCHUNKS * e + place - 1))
                for k in range(KD):
                    act.activation(t_hi[:, par * KD + k, :], raw_t[:, par, k, :], ACT.Copy, scale=W_SCALE)\
                       .then_inc(sem["t_hi"], 1)

            def n_high(e, place):
                par = place % 2
                act.wait_ge(sem[f"n_in{par}"], 16 * (HCHUNKS // 2 * e + place // 2 + 1))
                wait(act, sem["fc2"], HCHUNKS * e + place - 1)
                for k in range(HT):
                    act.activation(n_hi[:, par * HT + k, :], raw_n[:, par, k, :], ACT.Copy, scale=W_SCALE)\
                       .then_inc(sem["n_hi"], 1)

            def next_de_high(e):
                for a in range(CAP_TILES):
                    act.wait_ge(sem["de_tp"], CAP_TILES * e + a + 1)
                    act.activation(de_hi[:, :, a * P:(a + 1) * P], tp[2 + a][:, :, :], ACT.Copy)\
                       .then_inc(sem["de_hi"], 1)

            def relus(e, place):
                u = HCHUNKS * e + place
                if place % HCHUNKS == 0:
                    act.wait_ge(sem["b1_in"], 16 * (e + place // HCHUNKS + 1))
                for h in range(HT):
                    if h % 2 == 0:
                        act.wait_ge(sem["fc1"], 2 * u + h // 2 + 1)
                        wait(act, sem["h_lo"], u - 1)
                    act.activation(hidden[:, place % 2, h * CAP:(h + 1) * CAP],
                                   bank[h // 2][:, h % 2 * CAP:(h % 2 + 1) * CAP], ACT.Relu,
                                   bias=b1[:, place % HCHUNKS * HT + h:place % HCHUNKS * HT + h + 1],
                                   scale=1 / W_SCALE).then_inc(sem["relu"], 1)

            def h_high(e, place):
                u = HCHUNKS * e + place
                par = place % 2
                act.wait_ge(sem["relu"], HT * (u + 1))
                wait(act, sem["fc2"], u - 1)
                act.activation(h_hi[:, par * HT:(par + 1) * HT, :].rearrange("p a c -> p (a c)"),
                               hidden[:, par, :], ACT.Copy).then_inc(sem["h_hi"], 1)

            def slot(e, c):
                if within(e, c + 2):
                    t_high(e, c + 2)
                if within(e, c + 1):
                    n_high(e, c + 1)
                    relus(e, c + 1)
                if c == 2 and (not isinstance(e, int) or e < EXPERTS - 1):
                    next_de_high(e)
                if within(e, c + 1):
                    h_high(e, c + 1)
                if isinstance(e, int) and e == 0 and c in (2, 3):
                    a = c - 2
                    act.wait_ge(sem["taken_psum"], a + 1)
                    for half in range(2):
                        act.activation(taken_t[:, a, half * 512:(half + 1) * 512], bank[6 + half][:, :],
                                       ACT.Copy).then_inc(sem["taken_t"], 1)
            t_high(0, 0)
            act.wait_ge(sem["first"], 1)
            for k in range(KD):
                act.activation(de_hi[:, k, :], bank[k][:, 0:CAP], ACT.Copy).then_inc(sem["first_hi"], 1)
            steps(act, slot)
            for a in range(CAP_TILES):
                act.wait_ge(sem["eo"], CAP_TILES * (EXPERTS - 1) + a + 1)
                act.activation(eo_hi[:, a, :], eo[:, a, :], ACT.Copy).then_inc(sem["last_hi"], 1)

        @block.vector
        def _(dve):
            small = [0]

            def link(ins):
                small[0] += 1
                ins.then_inc(sem["small"], 1)
                dve.wait_ge(sem["small"], small[0])

            def along(a):
                return a.unsqueeze(2).to_broadcast([P, a.shape[1], EXPERTS])

            link(dve.tensor_scalar(logits, bank[LOGIT_BANK][:, 0:TILES * EXPERTS].rearrange("p (i e) -> p i e", e=EXPERTS),
                                   1 / W_SCALE, None, ALU.mult))
            link(dve.reduce_max(peak, logits, AX))
            dve.tensor_tensor(shifted, logits, along(peak), ALU.subtract).then_inc(sem["raised"], 1)
            dve.wait_ge(sem["expd"], 1)
            link(dve.reduce_sum(mass, raised, AX))
            link(dve.reciprocal(mass_r, mass))
            link(dve.tensor_tensor(score, raised, along(mass_r), ALU.mult))
            for i in range(TILES):
                dve.max(top8[:, i, :], score[:, i, :]).then_inc(sem["top"], 1)
            for i in range(TILES):
                dve.wait_ge(sem["top"], i + 1)
                dve.max_index(top8_at[:, i, :], top8[:, i, :], score[:, i, :]).then_inc(sem["top_at"], 1)
            dve.wait_ge(sem["top_at"], TILES)
            link(dve.tensor_tensor(pair, top8[:, :, 0], top8[:, :, 1], ALU.add))
            link(dve.reciprocal(pair_r, pair))
            for k in range(TOPK):
                link(dve.tensor_copy(expert[:, k, :], top8_at[:, :, k]))
            dve.wait_ge(sem["number_in"], 16)
            link(dve.tensor_tensor(chosen, along(expert.rearrange("p k i -> p (k i)")),
                                   number.unsqueeze(1).to_broadcast([P, PICKS, EXPERTS]), ALU.is_equal))
            dve.tensor_copy(chosen_h, chosen).then_inc(sem["chosen"], 1)
            dve.wait_ge(sem["loc_psum"], 1)
            link(dve.tensor_tensor(spread, bank[2][:, 0:PICKS * EXPERTS].rearrange("p (n e) -> p n e", e=EXPERTS),
                                   chosen, ALU.mult))
            link(dve.reduce_sum(loc, spread, AX))
            dve.tensor_scalar(valid, loc, float(CAP), None, ALU.is_lt).then_inc(sem["valid"], 1)
            link(dve.scalar_tensor_tensor(out=flat, in0=expert.rearrange("p k i -> p (k i)"), scalar=float(CAP),
                                          in1=loc, op0=ALU.mult, op1=ALU.add))
            dve.wait_ge(sem["valid"], 1)
            link(dve.scalar_tensor_tensor(out=far, in0=flat, scalar=-float(FAR_SLOT), in1=valid,
                                          op0=ALU.add, op1=ALU.mult))
            link(dve.tensor_scalar(far, far, float(FAR_SLOT), None, ALU.add))
            dve.tensor_copy(to_slot, far).then_inc(sem["routed"], 1)
            dve.wait_ge(sem["slot_in"], 16)
            for i in range(TILES):
                link(dve.tensor_scalar(picked[:, i, :], slot_no, far[:, i:i + 1], None, ALU.is_equal))
                dve.scalar_tensor_tensor(out=picked[:, i, :], in0=slot_no, scalar=far[:, TILES + i:TILES + i + 1],
                                         in1=picked[:, i, :], op0=ALU.is_equal, op1=ALU.add)\
                   .then_inc(sem["picked"], 1)

            def choices():
                for k in range(TOPK):
                    link(dve.tensor_tensor(weight[:, k, :], top8[:, :, k], pair_r, ALU.mult))
                flat_weight = weight.rearrange("p k i -> p (k i)")
                link(dve.tensor_tensor(flat_weight, flat_weight, valid, ALU.mult))
                link(dve.tensor_scalar(in_last, expert.rearrange("p k i -> p (k i)"), float(EXPERTS - 1), None,
                                       ALU.is_equal))
                link(dve.tensor_scalar(far, far, -float(FAR_SLOT), None, ALU.add))
                link(dve.tensor_tensor(far, far, in_last, ALU.mult))
                link(dve.tensor_tensor(last_slot, far[:, 0:TILES], far[:, TILES:PICKS], ALU.add))
                link(dve.tensor_scalar(last_slot, last_slot, float(FAR_SLOT - SLOTS + CAP), None, ALU.add))
                link(dve.tensor_tensor(in_last, in_last, flat_weight, ALU.mult))
                link(dve.tensor_tensor(last_weight, in_last[:, 0:TILES], in_last[:, TILES:PICKS], ALU.add))

            def lows(e, place, raw, hi, lo, name):
                par = place % 2
                for k in range(KD):
                    dve.wait_ge(sem[name + "_hi"], KD * (HCHUNKS * e + place) + k + 1)
                    dve.scalar_tensor_tensor(out=lo[:, par * KD + k, :], in0=raw[:, par, k, :], scalar=W_SCALE,
                                             in1=hi[:, par * KD + k, :], op0=ALU.mult, op1=ALU.subtract)\
                       .then_inc(sem[name + "_lo"], 1)

            def next_de_low(e):
                for a in range(CAP_TILES):
                    dve.wait_ge(sem["de_hi"], CAP_TILES * e + a + 1)
                    dve.tensor_tensor(de_lo[:, :, a * P:(a + 1) * P], tp[2 + a][:, :, :],
                                      de_hi[:, :, a * P:(a + 1) * P], ALU.subtract).then_inc(sem["de_lo"], 1)

            def result(e):
                dve.wait_ge(sem["b2_in"], 16 * (e + 1))
                wait(dve, sem["eo_out"], 16 * e)
                for a in range(CAP_TILES):
                    if isinstance(e, int) and e == EXPERTS - 1 and a == 0:
                        dve.wait_ge(sem["fc2_half"], 1)
                    elif a < 2:
                        dve.wait_ge(sem["fc2"], HCHUNKS * (e + 1))
                    dve.scalar_tensor_tensor(out=eo[:, a, :], in0=bank[4 + a][:, :], scalar=1 / W_SCALE,
                                             in1=b2, op0=ALU.mult, op1=ALU.add).then_inc(sem["eo"], 1)

            def slot(e, c):
                if c % HCHUNKS == 0 and (not isinstance(e, int) or e + c // HCHUNKS > 0):
                    result(e + c // HCHUNKS - 1)
                if within(e, c + 2):
                    lows(e, c + 2, raw_t, t_hi, t_lo, "t")
                if within(e, c + 1):
                    lows(e, c + 1, raw_n, n_hi, n_lo, "n")
                if c == 2 and (not isinstance(e, int) or e < EXPERTS - 1):
                    next_de_low(e)
                if isinstance(e, int) and e == EXPERTS - 1 and c == 2:
                    combine(0)
                if within(e, c + 1):
                    u = HCHUNKS * e + c + 1
                    par = (c + 1) % 2
                    dve.wait_ge(sem["h_hi"], u + 1)
                    dve.tensor_tensor(h_lo[:, par * HT:(par + 1) * HT, :].rearrange("p a c -> p (a c)"),
                                      hidden[:, par, :],
                                      h_hi[:, par * HT:(par + 1) * HT, :].rearrange("p a c -> p (a c)"),
                                      ALU.subtract).then_inc(sem["h_lo"], 1)
                if isinstance(e, int) and e == 0 and c == 0:
                    choices()
                if isinstance(e, int) and e == 0 and c == 1:
                    take()
                if isinstance(e, int) and e == EXPERTS - 1 and c == 3:
                    combine(1)
            def take():
                dve.wait_ge(sem["scattered"], 16 * PICKS)
                dve.wait_ge(sem["xn_lo"], TILES)
                for i in range(TILES):
                    dve.tensor_scalar(taken[:, i, :], slot_no, last_slot[:, i:i + 1], None, ALU.is_equal)\
                       .then_inc(sem["taken"], 1)

            def combine(k):
                dve.wait_ge(sem[f"got{k}"], 16 * TILES)
                for i in range(TILES):
                    if k:
                        dve.wait_ge(sem["half"], i + 1)
                    dve.scalar_tensor_tensor(out=X[:, i, :], in0=got[k][:, i, :], scalar=weight[:, k, i:i + 1],
                                             in1=X[:, i, :], op0=ALU.mult, op1=ALU.add)\
                       .then_inc(sem[("half", "most")[k]], 1)
            lows(0, 0, raw_t, t_hi, t_lo, "t")
            dve.wait_ge(sem["first"], 2)
            for k in range(KD):
                dve.tensor_copy(de_lo[:, k, :], bank[4 + k][:, 0:CAP]).then_inc(sem["first_lo"], 1)
            steps(dve, slot)
            for a in range(CAP_TILES):
                dve.wait_ge(sem["last_hi"], a + 1)
                dve.tensor_tensor(eo_lo[:, a, :], eo[:, a, :], eo_hi[:, a, :], ALU.subtract)\
                   .then_inc(sem["last_lo"], 1)
            for i in range(TILES):
                dve.wait_ge(sem["back"], i + 1)
                dve.wait_ge(sem["most"], i + 1)
                dve.scalar_tensor_tensor(out=X[:, i, :], in0=bank[BACK_BANK[i]][:, :],
                                         scalar=last_weight[:, i:i + 1], in1=X[:, i, :],
                                         op0=ALU.mult, op1=ALU.add).then_inc(sem["sum"], 1)

        @block.tensor
        def _(pe):
            pe.wait_ge(sem["chosen"], 1)
            pe.wait_ge(sem["before_in"], 16)
            pe.wait_ge(sem["ones"], 1)
            pe.matmul(bank[2][:, 0:PICKS * EXPERTS], before, chosen_h.rearrange("p n e -> p (n e)"),
                      start=True, stop=False)
            for n in range(PICKS - 1):
                last = pe.matmul(bank[2][:, (n + 1) * EXPERTS:PICKS * EXPERTS], ones,
                                 chosen_h[:, n:n + 1, :].to_broadcast([P, PICKS - 1 - n, EXPERTS]),
                                 start=False, stop=(n == PICKS - 2))
            last.then_inc(sem["loc_psum"], 1)

            for i in range(TILES):
                pe.wait_ge(sem["picked"], i + 1)
                pe.wait_ge(sem["xn_lo"], i + 1)
                for part, first_bank in ((xn_hi, 0), (xn_lo, 4)):
                    for k in range(KD):
                        last = pe.matmul(bank[first_bank + k][:, 0:CAP], part[:, i, k * P:(k + 1) * P],
                                         picked[:, i, :], start=(i == 0), stop=(i == TILES - 1))
                    if i == TILES - 1:
                        last.then_inc(sem["first"], 1)

            def next_turn(e):
                pe.wait_ge(sem["de_in"], 16 * (e + 1))
                wait(pe, sem["de_lo"], CAP_TILES * e)
                for a in range(CAP_TILES):
                    for k in range(KD):
                        last = pe.transpose(tp[2 + a][:, k, :], de[:, a, k * P:(k + 1) * P], s["ident"][:, :])
                    last.then_inc(sem["de_tp"], 1)

            def fc1(e, place):
                u = HCHUNKS * e + place
                par = place % 2
                pe.wait_ge(sem["t_lo"], KD * (u + 1))
                if isinstance(u, int) and u == 0:
                    pe.wait_ge(sem["first_hi"], KD)
                    pe.wait_ge(sem["first_lo"], KD)
                elif place % HCHUNKS == 0:
                    pe.wait_ge(sem["de_lo"], CAP_TILES * (e + place // HCHUNKS))
                wait(pe, sem["relu"], HT * u)
                for h in range(HT):
                    for k in range(KD):
                        last = three(pe, bank[h // 2][:, h % 2 * CAP:(h % 2 + 1) * CAP],
                                     t_hi[:, par * KD + k, h * P:(h + 1) * P],
                                     t_lo[:, par * KD + k, h * P:(h + 1) * P], de_hi[:, k, :], de_lo[:, k, :],
                                     k == 0, k == KD - 1)
                    if h % 2:
                        last.then_inc(sem["fc1"], 1)

            def fc2(e, place):
                u = HCHUNKS * e + place
                par = place % 2
                pe.wait_ge(sem["n_lo"], HT * (u + 1))
                pe.wait_ge(sem["h_lo"], u + 1)
                if place % HCHUNKS == 0:
                    wait(pe, sem["eo"], CAP_TILES * (e + place // HCHUNKS))
                for a in range(CAP_TILES):
                    for h in range(HT):
                        last = three(pe, bank[4 + a][:, :], h_hi[:, par * HT + h, a * P:(a + 1) * P],
                                     h_lo[:, par * HT + h, a * P:(a + 1) * P], n_hi[:, par * HT + h, :],
                                     n_lo[:, par * HT + h, :], place % HCHUNKS == 0 and h == 0,
                                     place % HCHUNKS == HCHUNKS - 1 and h == HT - 1)
                    if isinstance(u, int) and u == CHUNKS_ALL - 1 and a == 0:
                        last.then_inc(sem["fc2_half"], 1)
                last.then_inc(sem["fc2"], 1)

            def slot(e, c):
                if within(e, c + 1):
                    fc1(e, c + 1)
                if c == 2 and (not isinstance(e, int) or e < EXPERTS - 1):
                    next_turn(e)
                if within(e, c):
                    fc2(e, c)
                if isinstance(e, int) and e == 0 and c in (2, 3):
                    a = c - 2
                    pe.wait_ge(sem["taken"], TILES)
                    wait(pe, sem["taken_t"], 2 * a)
                    for i in range(TILES):
                        last = pe.transpose(tp[6 + i // 4][:, i % 4, :], taken[:, i, a * P:(a + 1) * P],
                                            s["ident"][:, :])
                    last.then_inc(sem["taken_psum"], 1)
            steps(pe, slot)
            pe.wait_ge(sem["taken_t"], 2 * CAP_TILES)
            for i in range(TILES):
                for a in range(CAP_TILES):
                    if i == 0:
                        pe.wait_ge(sem["last_lo"], a + 1)
                    who = taken_t[:, a, i * P:(i + 1) * P]
                    pe.matmul(bank[BACK_BANK[i]][:, :], who, eo_hi[:, a, :], start=(a == 0), stop=False)
                    last = pe.matmul(bank[BACK_BANK[i]][:, :], who, eo_lo[:, a, :], start=False,
                                     stop=(a == CAP_TILES - 1))
                last.then_inc(sem["back"], 1)


def _tables():
    f = np.float32
    inv = (1.0 / f(10000.0) ** (np.arange(0, HEAD, 2, dtype=f) / f(HEAD))).astype(f)
    pos = np.arange(SEQ, dtype=f)
    freqs = np.repeat(pos[:, None] * inv[None, :], 2, axis=-1).astype(f)
    base = ((np.arange(0, HEAD, 2, dtype=f) + f(0.4 * HEAD)) / f(1.4 * HEAD)).astype(f)
    power = (pos - SEQ // 2) / f(512.0)
    scale = np.repeat(base[None, :] ** power[:, None], 2, axis=-1).astype(f)
    cos, sin = np.cos(freqs), np.sin(freqs)
    sign = np.where(np.arange(HEAD) % 2 == 0, -1.0, 1.0).astype(f)
    gamma = (1.0 - 2.0 ** (-5.0 - np.arange(HEADS))).astype(np.float64)
    norm = 1 / np.sqrt(np.cumsum(gamma[None, :] ** np.arange(SEQ)[:, None], axis=0))
    grow = gamma[None, :] ** (np.arange(SEQ)[:, None] % P)
    q_head, k_head = (Q_SCALE * norm * grow)[:, :, None], (1 / grow)[:, :, None]
    tables = [((cos * scale)[:, None, :] * q_head), ((sin * scale * sign)[:, None, :] * q_head),
              ((cos / scale)[:, None, :] * k_head), ((sin / scale * sign)[:, None, :] * k_head)]
    tables = [np.ascontiguousarray(a.reshape(SEQ_TILES, P, -1).transpose(1, 0, 2), dtype=f) for a in tables]
    lane = np.arange(P)
    block = lane[:, None] // HEAD == lane[None, :] // HEAD
    by_lane = np.repeat(gamma.reshape(GROUPS, GH) ** P, HEAD, axis=1).T
    carry = (block[:, None, :] * by_lane[:, :, None]).astype(f)
    return tables + [carry]


def kernel(x, ctx_1024, L0_xattn_W, L0_xattn_b, L0_attn_Wq, L0_attn_bq, L0_attn_Wk, L0_attn_bk, L0_attn_Wv,
           L0_attn_bv, L0_attn_Wg, L0_attn_bg, L0_attn_Wo, L0_attn_bo, L0_attn_gn_w, L0_attn_gn_b,
           L0_ffn_gate_w, L0_ffn_fc1_w, L0_ffn_fc1_b, L0_ffn_fc2_w, L0_ffn_fc2_b):
    import concourse.bacc as bacc
    from concourse.bass_utils import run_bass_kernel_spmd

    def rows(a):
        a = np.asarray(a)
        return a.reshape(-1, P, a.shape[-1]).transpose(1, 0, 2)

    def cols(a):
        return np.asarray(a).reshape(-1, P).T

    ctx = np.asarray(ctx_1024).reshape(BATCH * CHUNKS, CHUNK, KD, P)
    fc1 = np.asarray(L0_ffn_fc1_w).reshape(EXPERTS * HCHUNKS, HCHUNK, KD, P)
    fc2 = np.asarray(L0_ffn_fc2_w).reshape(EXPERTS * HCHUNKS, HT, P, D)
    q_cos, q_sin, k_cos, k_sin, carry = _tables()
    lane = np.arange(P)
    heads = lambda a: np.repeat(np.asarray(a).reshape(GROUPS, GH), HEAD, axis=1).T
    arrays = {
        "x": rows(np.asarray(x).reshape(TOK, D)),
        "ident": np.eye(P, dtype=np.float32),
        "wxt": rows(np.asarray(L0_xattn_W).T),
        "wxn": rows(L0_xattn_W),
        "xb": cols(L0_xattn_b),
        "ctx_t": ctx.transpose(0, 3, 2, 1),
        "ctx_n": ctx.reshape(BATCH * CHUNKS, CHUNK // P, P, D).transpose(0, 2, 1, 3),
        "w5": np.stack([rows(w) for w in (L0_attn_Wq, L0_attn_Wk, L0_attn_Wv, L0_attn_Wg, L0_attn_Wo)]),
        "bias_rows": np.broadcast_to(np.stack([np.asarray(b) for b in (L0_attn_bq, L0_attn_bk, L0_attn_bv)]),
                                     (P, 3, D)),
        "bo": np.broadcast_to(np.asarray(L0_attn_bo), (P, D)),
        "bg": cols(L0_attn_bg),
        "gn_w": heads(L0_attn_gn_w),
        "gn_b": heads(L0_attn_gn_b),
        "same_head": (lane[:, None] // HEAD == lane[None, :] // HEAD).astype(np.float32) / HEAD,
        "q_cos": q_cos, "q_sin": q_sin, "k_cos": k_cos, "k_sin": k_sin,
        "carry": carry,
        "causal": (lane[:, None] <= lane[None, :]).astype(np.float32),
        "gate_w": rows(np.asarray(L0_ffn_gate_w).T),
        "fc1": fc1.transpose(0, 3, 2, 1),
        "fc2": fc2.transpose(0, 2, 1, 3),
        "fc1_b": np.asarray(L0_ffn_fc1_b).reshape(EXPERTS, HID // P, P).transpose(0, 2, 1),
        "fc2_b": np.broadcast_to(np.asarray(L0_ffn_fc2_b), (EXPERTS, P, D)),
        "expert_no": np.broadcast_to(np.arange(EXPERTS, dtype=np.float32), (P, EXPERTS)),
        "slot_no": np.broadcast_to(np.arange(CAP, dtype=np.float32), (P, CAP)),
        "before": (lane[:, None] < lane[None, :]).astype(np.float16),
    }
    nc = bacc.Bacc("TRN2", target_bir_lowering=False, num_devices=1)
    arrays = {n: np.ascontiguousarray(a) for n, a in arrays.items()}
    t = {n: nc.dram_tensor(n, a.shape, mybir.dt.from_np(a.dtype), kind="ExternalInput").ap()
         for n, a in arrays.items()}
    t["out"] = nc.dram_tensor("out", (P, TILES, D), F32, kind="ExternalOutput").ap()
    perceiver_layer(nc, t)
    got = run_bass_kernel_spmd(nc, [arrays], core_ids=[0]).results[0]["out"]
    return np.ascontiguousarray(got.transpose(1, 0, 2)).reshape(BATCH, SEQ, D)
```
